# Optimizing a Trainium2 kernel written in Bass

```python
import numpy as np
import jax
import jax.numpy as jnp

def _softmax(x, axis=-1):
    return jax.nn.softmax(x, axis=axis)

def _gelu(x):
    return jax.nn.gelu(x, approximate=True)

def _silu(x):
    return jax.nn.silu(x)

def _sigmoid(x):
    return jax.nn.sigmoid(x)

def _layernorm(x, axis=-1, eps=1e-05):
    m = jnp.mean(x, axis=axis, keepdims=True)
    v = jnp.var(x, axis=axis, keepdims=True)
    return (x - m) / jnp.sqrt(v + eps)

def _scatter_add(tgt, idx, src, axis=0):
    return tgt.at[idx].add(src)

def _segment_sum(src, seg, n):
    return jax.ops.segment_sum(src, seg, n)
kernel_name = 'mk_decoder_preln_d1_seqx_r4_8e77e9'

def setup_inputs(seed: int=0):
    np.random.seed(seed)
    _w = jnp.asarray

    def _rec_inputs():
        import jax
        import jax.numpy as jnp
        _rk = jax.random.key(seed)
        x = 7.22e-05 + 1 * jax.random.normal(jax.random.fold_in(_rk, 1), (32, 128, 512), jnp.float32)
        _lenS = 128 - jax.random.randint(jax.random.fold_in(_rk, 7), (32,), 0, max(1, 128 // 4) + 1, jnp.int32)
        _lenS2 = 128 - jax.random.randint(jax.random.fold_in(_rk, 8), (32,), 0, max(1, 128 // 4) + 1, jnp.int32)
        _ctx_1024P = jax.random.normal(jax.random.fold_in(_rk, 11), (32, 16, 256), jnp.float32)
        _ctx_1024c = jax.random.dirichlet(jax.random.fold_in(_rk, 511), 0.3 * jnp.ones((16,), jnp.float32), (32, 128))
        _ctx_1024t = jnp.einsum('bsk,bkd->bsd', _ctx_1024c, _ctx_1024P)
        _ctx_1024t = _ctx_1024t * jax.lax.rsqrt(jnp.mean(jnp.square(_ctx_1024t)) + 1e-12) * 0.953939
        ctx_1024 = -1.39393e-06 + 0.999914 * (_ctx_1024t + 0.3 * jax.random.normal(jax.random.fold_in(_rk, 611), (32, 128, 256), jnp.float32))
        fside_BxSx2_0 = jax.random.uniform(jax.random.fold_in(_rk, 12), (32, 128, 2), jnp.float32, 0.0, 0.999707)
        return (x, ctx_1024, fside_BxSx2_0)
    x, ctx_1024, fside_BxSx2_0 = _rec_inputs()

    def _L0_attn_setup():
        import jax, jax.numpy as jnp
        import numpy as np
        import math
        D_MODEL = 512
        NUM_HEADS = 16
        D_K = D_MODEL // NUM_HEADS
        SEQ_LEN = 512
        THETA = 10000.0
        BATCH = 2

        def _rope(t):
            S = t.shape[-2]
            dk = t.shape[-1]
            inv_freq = jnp.exp(-math.log(THETA) * jnp.arange(0, dk, 2, dtype=jnp.float32) / dk)
            pos = jnp.arange(S, dtype=jnp.float32)
            freqs = pos[:, None] * inv_freq[None, :]
            cos = jnp.cos(freqs)
            sin = jnp.sin(freqs)
            t1 = t[..., ::2]
            t2 = t[..., 1::2]
            rot = jnp.stack([t1 * cos - t2 * sin, t1 * sin + t2 * cos], axis=-1)
            return rot.reshape(t.shape)
        key = jax.random.key(seed)
        ks = jax.random.split(key, 5)
        std = (2.0 / (D_MODEL + D_MODEL)) ** 0.5
        return {'x': jax.random.normal(ks[0], (BATCH, SEQ_LEN, D_MODEL), dtype=jnp.float32), 'Wq': jax.random.normal(ks[1], (D_MODEL, D_MODEL), dtype=jnp.float32) * std, 'Wk': jax.random.normal(ks[2], (D_MODEL, D_MODEL), dtype=jnp.float32) * std, 'Wv': jax.random.normal(ks[3], (D_MODEL, D_MODEL), dtype=jnp.float32) * std, 'Wo': jax.random.normal(ks[4], (D_MODEL, D_MODEL), dtype=jnp.float32) * std}
    _L0_attn_all = _L0_attn_setup()
    _L0_attn_in = {k: v for k, v in _L0_attn_all.items() if k in ('Wq', 'Wk', 'Wv', 'Wo')}
    del _L0_attn_all

    def _L0_xattn_setup():
        import jax, jax.numpy as jnp
        import numpy as np
        DIM = 512
        CTX_DIM = 256
        N_HEADS = 32
        HEAD_DIM = DIM // N_HEADS
        POS_DIM = 2
        B, N, CTXN = (2, 512, 512)
        ROPE_BASE = 10000.0

        def apply_axial_rope(x, pos):
            b, n, h, d = x.shape
            p = pos.shape[-1]
            dpa = d // p
            half = dpa // 2
            freqs = ROPE_BASE ** (-jnp.arange(half, dtype=x.dtype) / half)
            ang = pos[..., :, None] * freqs
            cos = jnp.cos(ang)[:, :, None, :, :]
            sin = jnp.sin(ang)[:, :, None, :, :]
            xr = x.reshape(b, n, h, p, half, 2)
            x1, x2 = (xr[..., 0], xr[..., 1])
            out = jnp.stack([x1 * cos - x2 * sin, x1 * sin + x2 * cos], axis=-1)
            return out.reshape(b, n, h, d)
        key = jax.random.key(seed)
        ks = jax.random.split(key, 8)
        x = jax.random.normal(ks[0], (B, N, DIM), jnp.float32)
        ctx = jax.random.normal(ks[1], (B, CTXN, CTX_DIM), jnp.float32)
        pos_map = jax.random.uniform(ks[2], (B, N, POS_DIM), jnp.float32)
        ctx_pos_map = jax.random.uniform(ks[3], (B, CTXN, POS_DIM), jnp.float32)
        Wq = jax.random.normal(ks[4], (DIM, DIM), jnp.float32) / np.sqrt(DIM)
        Wkv = jax.random.normal(ks[5], (CTX_DIM, 2 * DIM), jnp.float32) / np.sqrt(CTX_DIM)
        Wout = jax.random.normal(ks[6], (DIM, DIM), jnp.float32) / np.sqrt(DIM)
        bout = jnp.zeros((DIM,), jnp.float32)
        return {'x': x, 'ctx': ctx, 'pos_map': pos_map, 'ctx_pos_map': ctx_pos_map, 'Wq': Wq, 'Wkv': Wkv, 'Wout': Wout, 'bout': bout}
    _L0_xattn_all = _L0_xattn_setup()
    _L0_xattn_in = {k: v for k, v in _L0_xattn_all.items() if k in ('Wq', 'Wkv', 'Wout', 'bout')}
    del _L0_xattn_all

    def _L0_ffn_setup():
        import jax, jax.numpy as jnp
        import numpy as np
        DIM = 512
        HID = 1408
        ZERO_POINT = 128.0

        def _qlinear(x, wq, scale):
            W = (wq.astype(jnp.float32) - ZERO_POINT) * scale[:, None]
            return jnp.einsum('bsd,hd->bsh', x, W)
        key = jax.random.key(seed)
        ks = jax.random.split(key, 7)
        B, S = (4, 512)
        sg = jax.random.uniform(ks[1], (HID,)) * (0.02 / np.sqrt(DIM)) + 0.0001
        su = jax.random.uniform(ks[3], (HID,)) * (0.02 / np.sqrt(DIM)) + 0.0001
        sd = jax.random.uniform(ks[5], (DIM,)) * (0.02 / np.sqrt(HID)) + 0.0001
        return {'x': jax.random.normal(ks[0], (B, S, DIM), dtype=jnp.float32), 'wq_gate': jax.random.randint(ks[2], (HID, DIM), 0, 64, dtype=jnp.int32), 's_gate': sg, 'wq_up': jax.random.randint(ks[4], (HID, DIM), 0, 64, dtype=jnp.int32), 's_up': su, 'wq_down': jax.random.randint(ks[6], (DIM, HID), 0, 64, dtype=jnp.int32), 's_down': sd}
    _L0_ffn_all = _L0_ffn_setup()
    _L0_ffn_in = {k: v for k, v in _L0_ffn_all.items() if k in ('wq_gate', 's_gate', 'wq_up', 's_up', 'wq_down', 's_down')}
    del _L0_ffn_all
    return {'x': x, 'ctx_1024': ctx_1024, 'fside_BxSx2_0': fside_BxSx2_0, 'L0_attn_Wq': _L0_attn_in['Wq'], 'L0_attn_Wk': _L0_attn_in['Wk'], 'L0_attn_Wv': _L0_attn_in['Wv'], 'L0_attn_Wo': _L0_attn_in['Wo'], 'L0_xattn_Wq': _L0_xattn_in['Wq'], 'L0_xattn_Wkv': _L0_xattn_in['Wkv'], 'L0_xattn_Wout': _L0_xattn_in['Wout'], 'L0_xattn_bout': _L0_xattn_in['bout'], 'L0_ffn_wq_gate': _L0_ffn_in['wq_gate'], 'L0_ffn_s_gate': _L0_ffn_in['s_gate'], 'L0_ffn_wq_up': _L0_ffn_in['wq_up'], 'L0_ffn_s_up': _L0_ffn_in['s_up'], 'L0_ffn_wq_down': _L0_ffn_in['wq_down'], 'L0_ffn_s_down': _L0_ffn_in['s_down']}

def reference(x, ctx_1024, fside_BxSx2_0, L0_attn_Wq, L0_attn_Wk, L0_attn_Wv, L0_attn_Wo, L0_xattn_Wq, L0_xattn_Wkv, L0_xattn_Wout, L0_xattn_bout, L0_ffn_wq_gate, L0_ffn_s_gate, L0_ffn_wq_up, L0_ffn_s_up, L0_ffn_wq_down, L0_ffn_s_down):
    import jax
    import jax.numpy as jnp

    def _L0_attn_ref(x, Wq, Wk, Wv, Wo):
        import jax, jax.numpy as jnp
        import numpy as np
        import math
        D_MODEL = 512
        NUM_HEADS = 16
        D_K = D_MODEL // NUM_HEADS
        SEQ_LEN = 512
        THETA = 10000.0
        BATCH = 2

        def _rope(t):
            S = t.shape[-2]
            dk = t.shape[-1]
            inv_freq = jnp.exp(-math.log(THETA) * jnp.arange(0, dk, 2, dtype=jnp.float32) / dk)
            pos = jnp.arange(S, dtype=jnp.float32)
            freqs = pos[:, None] * inv_freq[None, :]
            cos = jnp.cos(freqs)
            sin = jnp.sin(freqs)
            t1 = t[..., ::2]
            t2 = t[..., 1::2]
            rot = jnp.stack([t1 * cos - t2 * sin, t1 * sin + t2 * cos], axis=-1)
            return rot.reshape(t.shape)
        B, S, D = x.shape
        H, dk = (NUM_HEADS, D // NUM_HEADS)

        def split_heads(t):
            return t.reshape(B, S, H, dk).transpose(0, 2, 1, 3)
        q = split_heads(x @ Wq.T)
        k = split_heads(x @ Wk.T)
        v = split_heads(x @ Wv.T)
        q = _rope(q)
        k = _rope(k)
        scores = jnp.einsum('bhqd,bhkd->bhqk', q, k) / math.sqrt(dk)
        causal = jnp.tril(jnp.ones((S, S), dtype=bool))
        scores = jnp.where(causal[None, None], scores, -jnp.inf)
        attn = jax.nn.softmax(scores, axis=-1)
        ctx = jnp.einsum('bhqk,bhkd->bhqd', attn, v)
        ctx = ctx.transpose(0, 2, 1, 3).reshape(B, S, D)
        return ctx @ Wo.T

    def _L0_xattn_ref(x, ctx, pos_map, ctx_pos_map, Wq, Wkv, Wout, bout):
        import jax, jax.numpy as jnp
        import numpy as np
        DIM = 512
        CTX_DIM = 256
        N_HEADS = 32
        HEAD_DIM = DIM // N_HEADS
        POS_DIM = 2
        B, N, CTXN = (2, 512, 512)
        ROPE_BASE = 10000.0

        def apply_axial_rope(x, pos):
            b, n, h, d = x.shape
            p = pos.shape[-1]
            dpa = d // p
            half = dpa // 2
            freqs = ROPE_BASE ** (-jnp.arange(half, dtype=x.dtype) / half)
            ang = pos[..., :, None] * freqs
            cos = jnp.cos(ang)[:, :, None, :, :]
            sin = jnp.sin(ang)[:, :, None, :, :]
            xr = x.reshape(b, n, h, p, half, 2)
            x1, x2 = (xr[..., 0], xr[..., 1])
            out = jnp.stack([x1 * cos - x2 * sin, x1 * sin + x2 * cos], axis=-1)
            return out.reshape(b, n, h, d)
        b, n, _ = x.shape
        ctx_n = ctx.shape[1]
        q = (x @ Wq).reshape(b, n, N_HEADS, HEAD_DIM)
        k, v = jnp.split(ctx @ Wkv, 2, axis=-1)
        k = k.reshape(b, ctx_n, N_HEADS, HEAD_DIM)
        v = v.reshape(b, ctx_n, N_HEADS, HEAD_DIM)
        q = apply_axial_rope(q, pos_map)
        k = apply_axial_rope(k, ctx_pos_map)
        scale = 1.0 / np.sqrt(HEAD_DIM).astype(np.float32)
        logits = jnp.einsum('bqhd,bkhd->bhqk', q, k) * scale
        w = jax.nn.softmax(logits, axis=-1)
        attn = jnp.einsum('bhqk,bkhd->bqhd', w, v)
        attn = attn.reshape(b, n, N_HEADS * HEAD_DIM)
        return attn @ Wout + bout

    def _L0_ffn_ref(x, wq_gate, s_gate, wq_up, s_up, wq_down, s_down):
        import jax, jax.numpy as jnp
        import numpy as np
        DIM = 512
        HID = 1408
        ZERO_POINT = 128.0

        def _qlinear(x, wq, scale):
            W = (wq.astype(jnp.float32) - ZERO_POINT) * scale[:, None]
            return jnp.einsum('bsd,hd->bsh', x, W)
        gate = _qlinear(x, wq_gate, s_gate)
        gate = jax.nn.silu(gate)
        up = _qlinear(x, wq_up, s_up)
        return _qlinear(gate * up, wq_down, s_down)
    x = x + _L0_attn_ref(_layernorm(x, axis=-1), L0_attn_Wq, L0_attn_Wk, L0_attn_Wv, L0_attn_Wo)
    x = x + _L0_xattn_ref(_layernorm(x, axis=-1), ctx_1024, fside_BxSx2_0, fside_BxSx2_0, L0_xattn_Wq, L0_xattn_Wkv, L0_xattn_Wout, L0_xattn_bout)
    x = x + _L0_ffn_ref(_layernorm(x, axis=-1), L0_ffn_wq_gate, L0_ffn_s_gate, L0_ffn_wq_up, L0_ffn_s_up, L0_ffn_wq_down, L0_ffn_s_down)
    return x

_drawn_inputs = setup_inputs


def setup_inputs(seed=0):
    import zlib

    import numpy as np

    out = dict(_drawn_inputs(seed))
    spreads = {'L0_xattn_bout': (0.0, 0.1)}
    factors = {'L0_ffn_s_gate': 2.998, 'L0_ffn_s_up': 3.397, 'L0_ffn_s_down': 3.616}
    for name, (base, spread) in spreads.items():
        noise = np.random.default_rng([zlib.crc32(name.encode()), seed]).standard_normal(out[name].shape)
        drawn = base * np.exp(spread * noise) if base else spread * noise
        out[name] = jnp.asarray(drawn.astype(out[name].dtype))
    for name, factor in factors.items():
        out[name] = (out[name] * factor).astype(out[name].dtype)
    return out
```

```python
import math
from contextlib import ExitStack, contextmanager

import numpy as np

import concourse.bass as bass
from concourse import mybir

P = 128
B = 32
D = 512
KT = D // P
CD = 256
CKT = CD // P
H1, DK1 = 16, 32
H2, DK2 = 32, 16
HID = 1408
HT = HID // P
G = 4
NS = H1 // G
NC = H2 // G
TPB = 4
NBLK = B // TPB
EPS = 1e-5
ZERO_POINT = 128.0
NEG = -1.0e30
THETA = 10000.0
HALF = 4
MAGIC = 12582912.0
TWO_PI = 2.0 * math.pi
PI_A = 6.28125
PI_B = float(np.float32(np.round((TWO_PI - PI_A) * 2.0 ** 20) / 2.0 ** 20))
PI_C = float(np.float32(TWO_PI - PI_A - PI_B))
NCONST = 2 * DK1 + 2


def shape_constants():
    inv = np.exp(np.float32(-math.log(THETA)) * np.arange(0, DK1, 2, dtype=np.float32) / np.float32(DK1))
    ang = np.arange(P, dtype=np.float32)[:, None] * inv.astype(np.float32)[None, :]
    cos, sin = np.cos(ang), np.sin(ang)
    c = np.zeros((P, NCONST), np.float32)
    c[:, 0:DK1:2] = cos
    c[:, 1:DK1:2] = cos
    c[:, DK1:2 * DK1:2] = -sin
    c[:, DK1 + 1:2 * DK1:2] = sin
    odd = (np.arange(P) // DK2) % 2
    c[:, 2 * DK1] = 1 - odd
    c[:, 2 * DK1 + 1] = odd
    return c


def build_decoder(nc, x, ctx_in, pos, consts, wq1, wk1, wv1, wo1, wq2, wkv2, wo2, bout,
                  wg, sg, wu, su, wd, sd, out, x2_dram):
    fp32, bf16, fp32r, i32 = mybir.dt.float32, mybir.dt.bfloat16, mybir.dt.float32r, mybir.dt.int32
    ALU = mybir.AluOpType
    ACT = mybir.ActivationFunctionType
    AX = mybir.AxisListType.X

    attention_phase(nc, fp32, bf16, fp32r, ALU, ACT, AX, x, ctx_in, pos, consts,
                    wq1, wk1, wv1, wo1, wq2, wkv2, wo2, bout, x2_dram)
    ffn_phase(nc, fp32, fp32r, i32, ALU, ACT, x2_dram, wg, sg, wu, su, wd, sd, out)


def attention_phase(nc, fp32, bf16, fp32r, ALU, ACT, AX, x, ctx_in, pos, consts,
                    wq1, wk1, wv1, wo1, wq2, wkv2, wo2, bout, x2_dram):
    es = ExitStack()
    with es:
        def sb(name, shape, dt=fp32):
            return es.enter_context(nc.sbuf_tensor(name, shape, dt))

        def sem(name):
            return es.enter_context(nc.semaphore(name))

        WSRC = [("q1", wq1, KT, D), ("k1", wk1, KT, D), ("v1", wv1, KT, D), ("o1", wo1, KT, D),
                ("kv2", wkv2, CKT, 2 * D), ("q2", wq2, KT, D), ("o2", wo2, KT, D)]
        WHI = {n: sb(f"w_{n}_hi", [P, k, m], fp32r) for n, _, k, m in WSRC}
        WLO = {n: sb(f"w_{n}_lo", [P, k, m], fp32r) for n, _, k, m in WSRC}

        cst = sb("cst", [P, NCONST])
        ident = sb("ident", [P, P])
        ident16 = sb("ident16", [P, P], bf16)
        causal = sb("causal", [P, G, P], bf16)
        bout_b = sb("bout_b", [P, D])
        cos2 = sb("cos2", [P, B, DK2])
        sin2 = sb("sin2", [P, B, DK2])
        eps_c, one_c = sb("eps_c", [P, 1]), sb("one_c", [P, 1])

        xA, xB = sb("xA", [P, D]), sb("xB", [P, D])
        x1A, x1B, x2 = sb("x1A", [P, D]), sb("x1B", [P, D]), sb("x2", [P, D])
        z1, z2 = sb("z1", [P, D]), sb("z2", [P, D])
        z1T_h, z1T_l = sb("z1T_h", [P, KT, P], fp32r), sb("z1T_l", [P, KT, P], fp32r)
        z2T_h, z2T_l = sb("z2T_h", [P, KT, P], fp32r), sb("z2T_l", [P, KT, P], fp32r)
        cx = sb("cx", [P, CD])
        cxT_h, cxT_l = sb("cxT_h", [P, CKT, P], fp32r), sb("cxT_l", [P, CKT, P], fp32r)
        rope_buf = sb("rope_buf", [P, 8, D])
        RA = {n: rope_buf[:, j, :] for j, n in enumerate(("q1", "k1", "q2", "k2"))}
        RB = {n: rope_buf[:, 4 + j, :] for j, n in enumerate(("q1", "k1", "q2", "k2"))}
        qT1, kT1 = sb("qT1", [P, KT, P]), sb("kT1", [P, KT, P])
        qT2, kT2e, kT2o = sb("qT2", [P, KT, P]), sb("kT2e", [P, KT, P]), sb("kT2o", [P, KT, P])
        v1 = sb("v1", [P, D])
        v2e, v2o = sb("v2e", [P, H2 // 2, 2, DK2]), sb("v2o", [P, H2 // 2, 2, DK2])
        NP = 3
        prob = sb("prob", [P, NP, G, P])
        probT = sb("probT", [P, NP, G, P])
        nmax = sb("nmax", [P, NP, G])
        rsum1, rsum2 = sb("rsum1", [P, H1]), sb("rsum2", [P, H2])
        rinv1, rinv2 = sb("rinv1", [P, H1]), sb("rinv2", [P, H2])
        rbc1, rbc2 = sb("rbc1", [P, H1, DK1]), sb("rbc2", [P, H2, DK2])
        rT1, rT2 = sb("rT1", [P, D]), sb("rT2", [P, D])
        cn, cn_h, cn_l = sb("cn", [P, KT, P]), sb("cn_h", [P, KT, P], fp32r), sb("cn_l", [P, KT, P], fp32r)
        st = {n: sb(f"st{n}", [P, 6]) for n in (1, 2)}
        mv = {n: sb(f"mv{n}", [P, 2]) for n in (1, 2)}
        lnv = {n: sb(f"lnv{n}", [P, 1]) for n in (1, 2)}
        r0 = {n: sb(f"r0{n}", [P, 1]) for n in (1, 2)}
        nt = {n: sb(f"nt{n}", [P, 4]) for n in (1, 2)}

        ang_s, ang_c = z2[:, 0:B * 2 * HALF], z2[:, B * 2 * HALF:2 * B * 2 * HALF]
        turns_sb, pos_sb = rT2[:, 0:B * 2 * HALF], rT2[:, B * 2 * HALF:B * 2 * HALF + 2 * B]
        def stage(n, k, m):
            return rope_buf[:, 4 * (n % 2):4 * (n % 2) + 4, :].rearrange("p a b -> p (a b)").rearrange("p (k n) -> p k n", k=k)

        bank = [es.enter_context(nc.psum_tensor(f"bank{n}", [P, 512], fp32)) for n in range(8)]
        PR0, PR1, PRV = bank[0], bank[1], bank[6]
        SC = [bank[2], bank[3]]
        TA, TB, TC = bank[4], bank[5], bank[7]
        TP = [TA, TB]

        wstage_in = [sem("wstage_in0"), sem("wstage_in1")]
        w_hi, w_lo = sem("w_hi_ready"), sem("w_lo_ready")
        c_in, c_zero, c_ready = sem("const_loaded"), sem("const_zeroed"), sem("const_ready")
        pos_in, tab, tab_act = sem("pos_loaded"), sem("rotary_table"), sem("rotary_sin")
        x_in, x_copied, cx_in = sem("x_loaded"), sem("x_copied"), sem("ctx_loaded")
        mv_r = {n: sem(f"mean_var{n}_ready") for n in (1, 2)}
        ln_r = {n: sem(f"log_var{n}_ready") for n in (1, 2)}
        rs_r = {n: sem(f"rough_rstd{n}_ready") for n in (1, 2)}
        z_r = {n: sem(f"z{n}_ready") for n in (1, 2)}
        zT_d = {n: sem(f"z{n}T_done") for n in (1, 2)}
        zT_hi = {n: sem(f"z{n}T_hi_ready") for n in (1, 2)}
        zT_lo = {n: sem(f"z{n}T_lo_ready") for n in (1, 2)}
        cxT_d, cxT_hi, cxT_lo = sem("ctxT_done"), sem("ctxT_hi_ready"), sem("ctxT_lo_ready")
        NAMES = ("q1", "k1", "q2", "k2")
        pj = {n: sem(f"proj_{n}_done") for n in NAMES + ("v1", "v2", "o1", "o2")}
        ab = {n: sem(f"rope_{n}_products") for n in NAMES}
        rot = {n: sem(f"rope_{n}_ready") for n in NAMES}
        rT_d = {n: sem(f"{n}_transposed") for n in NAMES}
        rT_r = {n: sem(f"{n}T_ready") for n in NAMES}
        v1_r, v2_r = sem("v1_ready"), sem("v2_ready")
        s_done, nmax_r, p_r = sem("scores_done"), sem("nmax_ready"), sem("prob_ready")
        pT_d, pTe_r, pTo_r = sem("probT_done"), sem("probT_even_ready"), sem("probT_odd_ready")
        av_d = sem("attn_out_done")
        ri_r = {n: sem(f"rinv{n}_ready") for n in (1, 2)}
        rb_r = {n: sem(f"rinv{n}_spread") for n in (1, 2)}
        ri_d = {n: sem(f"rinv{n}T_done") for n in (1, 2)}
        riT_r = {n: sem(f"rinv{n}T_ready") for n in (1, 2)}
        cn_r = {n: sem(f"ctxn{n}_ready") for n in (1, 2)}
        cn_hi = {n: sem(f"ctxn{n}_hi_ready") for n in (1, 2)}
        cn_lo = {n: sem(f"ctxn{n}_lo_ready") for n in (1, 2)}
        x1_r, x1b_r, x2_r, x2_out = sem("x1_ready"), sem("x1_bout_ready"), sem("x2_ready"), sem("x2_stored")
        dstep = sem("vector_small_step")
        aggr = sem("vector_aggregates")

        block = es.enter_context(nc.Block())

        def wait(eng, s, value):
            if not isinstance(value, int) or value > 0:
                eng.wait_ge(s, value)

        def chunks(sq, cq):
            return ([(1, c) for c in range(NS)] if sq is not None else []) + \
                   ([(2, c) for c in range(NC)] if cq is not None else [])

        def head(kind, c, j):
            return (P // DK1) * j + c if kind == 1 else (P // DK2) * j + c

        def first_chunk(sq, cq):
            return 0 if cq is None else NS + (NS + NC) * cq

        def slots(cq):
            return 0 if cq is None else NS

        LT, LA = 2, 3
        STEPS = NS + NC + LA

        def schedule(program, mid):
            program(0, None, 1)
            program(1, 0, 2)
            with mid(1, B - 2) as c:
                program(c + 1, c, c + 2)
            program(B - 1, B - 2, None)
            program(None, B - 1, None)

        @block.sync
        def _(sp):
            sp.dma_start(xA[:, :], x[0, :, :]).then_inc(x_in, 16)
            sp.dma_start(pos_sb[:, :], pos).then_inc(pos_in, 16)
            sp.dma_start(cst[:, :], consts).then_inc(c_in, 16)
            sp.dma_start(bout_b[:, :], bout.partition_broadcast(P)).then_inc(c_in, 16)
            for n, (name, src, k, m) in enumerate(WSRC):
                if n >= 2:
                    sp.wait_ge(w_lo, n - 1)
                sp.dma_start(stage(n, k, m), src.rearrange("(k p) n -> p k n", p=P)).then_inc(wstage_in[n % 2], 16)

            def program(sq, cq, nx):
                if sq is not None:
                    wait(sp, cxT_d, sq)
                    sp.dma_start(cx[:, :], ctx_in[sq, :, :]).then_inc(cx_in, 16)
                    sp.wait_ge(x_in, 16 * (sq + 1))
                    wait(sp, x1_r, sq)
                    sp.dma_start(xB[:, :], xA[:, :]).then_inc(x_copied, 16)
                if nx is not None:
                    sp.wait_ge(x_copied, 16 * nx)
                    sp.wait_ge(z_r[1], nx)
                    sp.dma_start(xA[:, :], x[nx, :, :]).then_inc(x_in, 16)
                if cq is not None:
                    sp.wait_ge(x2_r, cq + 1)
                    sp.dma_start(x2_dram[cq, :, :], x2[:, :]).then_inc(x2_out, 16)

            schedule(program, sp.Fori)
            sp.wait_ge(x2_out, 16 * B)

        @block.gpsimd
        def _(pool):
            pool.memset(ident[:, :], 0.0).then_inc(c_zero, 1)
            pool.memset(causal[:, :, :], 0.0).then_inc(c_zero, 1)
            pool.memset(v2e[:, :, :, :], 0.0).then_inc(c_zero, 1)
            pool.memset(v2o[:, :, :, :], 0.0).then_inc(c_zero, 1)
            pool.memset(eps_c[:, :], EPS).then_inc(c_zero, 1)
            pool.memset(one_c[:, :], 1.0).then_inc(c_zero, 1)
            pool.wait_ge(c_zero, 6)
            pool.affine_select(out=ident[:, :], in_=ident[:, :], compare_op=ALU.not_equal, fill=1.0,
                               base=0, pattern=[[-1, P]], channel_multiplier=1).then_inc(c_ready, 1)
            pool.affine_select(out=causal[:, :, :], in_=causal[:, :, :], compare_op=ALU.is_ge, fill=NEG,
                               base=0, pattern=[[0, G], [-1, P]], channel_multiplier=1).then_inc(c_ready, 1)
            pool.wait_ge(c_ready, 1)
            pool.tensor_copy(ident16[:, :], ident[:, :]).then_inc(c_ready, 1)

            def rope_sum(n, q):
                wait(pool, ab[n], q + 1)
                pool.tensor_tensor(RA[n][:, :], RA[n][:, :], RB[n][:, :], ALU.add).then_inc(rot[n], 1)

            def program(sq, cq, nx):
                if cq is not None:
                    wait(pool, x1_r, cq + 1)
                    wait(pool, x2_r, cq)
                    pool.tensor_tensor(x1B[:, :], x1A[:, :], bout_b[:, :], ALU.add).then_inc(x1b_r, 1)
                if sq is not None:
                    rope_sum("q1", sq)
                    rope_sum("k1", sq)
                if cq is not None:
                    rope_sum("q2", cq)
                for n, q, r, spread, h, w in ((1, sq, rinv1, rbc1, H1, DK1), (2, cq, rinv2, rbc2, H2, DK2)):
                    if q is not None:
                        wait(pool, ri_d[n], q)
                        pool.wait_ge(ri_r[n], q + 1)
                        pool.tensor_tensor(spread[:, :, :], r[:, :].unsqueeze(2).to_broadcast([P, h, w]),
                                           one_c[:, :].unsqueeze(2).to_broadcast([P, h, w]), ALU.mult).then_inc(rb_r[n], 1)
                if sq is not None:
                    rope_sum("k2", sq)

            pool.wait_ge(c_in, 32)
            schedule(program, pool.Fori)

        @block.tensor
        def _(pe):
            def transpose4(dst, src, k=KT):
                for j in range(k):
                    last = nc.tensor.transpose(dst[:, j * P:(j + 1) * P], src(j), ident[:, :])
                return last

            def project(dst, th, tl, name, k, cols=slice(0, D), lo_ready=None):
                hi, lo = WHI[name], WLO[name]
                n = 0
                for a, w in ((th, hi), (th, lo), (tl, hi)):
                    if a is tl and lo_ready is not None:
                        pe.wait_ge(*lo_ready)
                    for j in range(k):
                        last = nc.tensor.matmul(dst[:, :], a[:, j, :], w[:, j, cols],
                                                start=(n == 0), stop=(n == 3 * k - 1))
                        n += 1
                return last

            def scores(kind, c, slot, m):
                if kind == 1:
                    nc.tensor.matmul(SC[m][:, :], ident16[:, :], causal[:, :, :].rearrange("p g t -> p (g t)"),
                                     start=True, stop=False, skip_group_check=True)
                for j in range(G):
                    if kind == 1:
                        r, q, k = DK1 * c, qT1, kT1
                    else:
                        r, q, k = 2 * DK2 * (c // 2), qT2, (kT2e, kT2o)[c % 2]
                    last = nc.tensor.matmul(SC[m][:, j * P:(j + 1) * P], q[r:r + 32, j, :], k[r:r + 32, j, :],
                                            start=(kind == 2), stop=True, skip_group_check=True)
                last.then_inc(s_done, 1)

            def attend(kind, c, slot):
                for j in range(G):
                    if kind == 1:
                        r, dst, v = DK1 * c, PR1, v1[:, head(1, c, j) * DK1:(head(1, c, j) + 1) * DK1]
                        start, stop = True, True
                    else:
                        pair = head(2, c, j) // 2
                        r, dst, v = 2 * DK2 * (c // 2), PRV, (v2e, v2o)[c % 2][:, pair, :, :].rearrange("p a d -> p (a d)")
                        start, stop = c % 2 == 0 and j == 0, c % 2 == 1
                    last = nc.tensor.matmul(dst[r:r + 32, j * P:(j + 1) * P], v, probT[:, slot, j, :],
                                            start=start, stop=stop, skip_group_check=True)
                last.then_inc(av_d, 1)

            def program(sq, cq, nx):
                order = chunks(sq, cq)
                n0, s0 = first_chunk(sq, cq), slots(cq)
                e0 = NS // 2 if cq is not None else 0
                if cq is None:
                    par = 0
                else:
                    par = e0 + (NS + NC) // 2 * cq
                if sq is not None:
                    pe.wait_ge(z_r[1], sq + 1)
                    wait(pe, pTe_r, par)
                    transpose4(TA, lambda j: z1[:, j * P:(j + 1) * P]).then_inc(zT_d[1], 1)
                if cq is not None:
                    pe.wait_ge(z_r[2], cq + 1)
                    wait(pe, pTo_r, par)
                    transpose4(TB, lambda j: z2[:, j * P:(j + 1) * P]).then_inc(zT_d[2], 1)
                if sq is not None:
                    pe.wait_ge(zT_hi[1], sq + 1)
                    wait(pe, v2_r, sq)
                    project(PR0, z1T_h, z1T_l, "q1", KT, lo_ready=(zT_lo[1], sq + 1)).then_inc(pj["q1"], 1)
                    if cq is not None:
                        wait(pe, x2_r, cq)
                    project(PR1, z1T_h, z1T_l, "k1", KT).then_inc(pj["k1"], 1)
                    if cq is not None:
                        wait(pe, cn_r[2], cq)
                    project(PRV, z1T_h, z1T_l, "v1", KT).then_inc(pj["v1"], 1)
                if cq is not None:
                    pe.wait_ge(zT_hi[2], cq + 1)
                    if sq is not None:
                        pe.wait_ge(ab["q1"], sq + 1)
                    project(PR0, z2T_h, z2T_l, "q2", KT, lo_ready=(zT_lo[2], cq + 1)).then_inc(pj["q2"], 1)
                if sq is not None:
                    pe.wait_ge(rot["q1"], sq + 1)
                    if cq is not None:
                        pe.wait_ge(cxT_lo, cq + 1)
                    transpose4(TC, lambda j: RA["q1"][:, j * P:(j + 1) * P]).then_inc(rT_d["q1"], 1)
                    pe.wait_ge(rot["k1"], sq + 1)
                    transpose4(TA, lambda j: RA["k1"][:, j * P:(j + 1) * P]).then_inc(rT_d["k1"], 1)
                for t in range(STEPS):
                    if t == (2 if sq is not None else 0) and cq is not None:
                        pe.wait_ge(rot["q2"], cq + 1)
                        transpose4(TB, lambda j: RA["q2"][:, j * P:(j + 1) * P]).then_inc(rT_d["q2"], 1)
                        pe.wait_ge(rot["k2"], cq + 1)
                        if sq is not None:
                            pe.wait_ge(rT_r["q1"], sq + 1)
                        transpose4(TC, lambda j: RA["k2"][:, j * P:(j + 1) * P]).then_inc(rT_d["k2"], 1)
                    if t < len(order):
                        kind, c = order[t]
                        wait(pe, p_r, n0 + t - 1)
                        if kind == 1 and c == 0:
                            pe.wait_ge(rT_r["q1"], sq + 1)
                            pe.wait_ge(rT_r["k1"], sq + 1)
                        if kind == 2 and c == 0:
                            pe.wait_ge(rT_r["q2"], cq + 1)
                            pe.wait_ge(rT_r["k2"], cq + 1)
                        scores(kind, c, (s0 + t) % NP, t % 2)
                    if 0 <= t - LT < len(order):
                        u = t - LT
                        kind, c = order[u]
                        pe.wait_ge(p_r, n0 + u + 1)
                        if u == 0 and sq is None:
                            pe.wait_ge(rT_r["k2"], cq + 1)
                        if u >= 2:
                            pe.wait_ge((pTe_r, pTo_r)[u % 2], par + u // 2)
                        elif u == 0 and sq is not None:
                            pe.wait_ge(rT_r["k1"], sq + 1)
                        elif u == 1 and cq is not None:
                            pe.wait_ge(rT_r["q2"], cq + 1)
                        transpose4(TP[u % 2], lambda j, s=(s0 + u) % NP: prob[:, s, j, :]).then_inc(pT_d, 1)
                    if 0 <= t - LA < len(order):
                        u = t - LA
                        kind, c = order[u]
                        pe.wait_ge((pTe_r, pTo_r)[u % 2], par + u // 2 + 1)
                        if kind == 1 and c == 0:
                            pe.wait_ge(v1_r, sq + 1)
                            pe.wait_ge(ab["k1"], sq + 1)
                        if kind == 2 and c == 0:
                            pe.wait_ge(v2_r, cq + 1)
                            if sq is not None:
                                pe.wait_ge(v1_r, sq + 1)
                        attend(kind, c, (s0 + u) % NP)
                    if t == 6 and sq is not None:
                        pe.wait_ge(rb_r[1], sq + 1)
                        if cq is not None:
                            pe.wait_ge(rT_r["k2"], cq + 1)
                        transpose4(TC, lambda j: rbc1[:, G * j:G * (j + 1), :].rearrange("p h d -> p (h d)")).then_inc(ri_d[1], 1)
                    if t == 8 and sq is not None:
                        pe.wait_ge(cx_in, 16 * (sq + 1))
                        pe.wait_ge(riT_r[1], sq + 1)
                        transpose4(TC, lambda j: cx[:, j * P:(j + 1) * P], CKT).then_inc(cxT_d, 1)
                    if t == 9 and sq is not None:
                        pe.wait_ge(cn_hi[1], sq + 1)
                        if cq is not None:
                            pe.wait_ge(ab["q2"], cq + 1)
                        project(PR0, cn_h, cn_l, "o1", KT, lo_ready=(cn_lo[1], sq + 1)).then_inc(pj["o1"], 1)
                if cq is not None:
                    pe.wait_ge(rb_r[2], cq + 1)
                    if sq is not None:
                        pe.wait_ge(cxT_lo, sq + 1)
                    transpose4(TC, lambda j: rbc2[:, 8 * j:8 * (j + 1), :].rearrange("p h d -> p (h d)")).then_inc(ri_d[2], 1)
                if sq is not None:
                    pe.wait_ge(cxT_lo, sq + 1)
                    pe.wait_ge(cn_r[1], sq + 1)
                    project(PR1, cxT_h, cxT_l, "kv2", CKT, slice(0, D)).then_inc(pj["k2"], 1)
                    pe.wait_ge(x1_r, sq + 1)
                    project(PR0, cxT_h, cxT_l, "kv2", CKT, slice(D, 2 * D)).then_inc(pj["v2"], 1)
                if cq is not None:
                    pe.wait_ge(cn_hi[2], cq + 1)
                    if sq is not None:
                        pe.wait_ge(ab["k2"], sq + 1)
                    project(PR1, cn_h, cn_l, "o2", KT, lo_ready=(cn_lo[2], cq + 1)).then_inc(pj["o2"], 1)

            pe.wait_ge(c_ready, 3)
            pe.wait_ge(w_lo, len(WSRC))
            schedule(program, pe.Fori)

        @block.scalar
        def _(act):
            act.wait_ge(tab, 1)
            nc.scalar.activation(ang_s[:, :], ang_s[:, :], ACT.Sin).then_inc(tab_act, 1)
            nc.scalar.activation(ang_c[:, :], ang_c[:, :], ACT.Sin).then_inc(tab_act, 1)
            for n, (name, src, k, m) in enumerate(WSRC):
                act.wait_ge(wstage_in[n % 2], 16 * (n // 2 + 1))
                nc.scalar.activation(WHI[name][:, :, :], stage(n, k, m), ACT.Copy).then_inc(w_hi, 1)
            act.wait_ge(c_ready, 3)

            def rough_rstd(n, q):
                act.wait_ge(mv_r[n], q + 1)
                nc.scalar.activation(lnv[n][:, :], mv[n][:, 1:2], ACT.Ln, bias=eps_c[:, :]).then_inc(ln_r[n], 1)
                act.wait_ge(ln_r[n], q + 1)
                nc.scalar.activation(r0[n][:, :], lnv[n][:, :], ACT.Exp, scale=-0.5).then_inc(rs_r[n], 1)

            def flat(t):
                return t[:, :, :].rearrange("p k t -> p (k t)")

            def program(sq, cq, nx):
                order = chunks(sq, cq)
                n0, s0 = first_chunk(sq, cq), slots(cq)
                if sq is not None:
                    act.wait_ge(zT_d[1], sq + 1)
                    wait(act, pj["v1"], sq)
                    nc.scalar.activation(flat(z1T_h), TA[:, :], ACT.Copy).then_inc(zT_hi[1], 1)
                if cq is not None:
                    act.wait_ge(zT_d[2], cq + 1)
                    nc.scalar.activation(flat(z2T_h), TB[:, :], ACT.Copy).then_inc(zT_hi[2], 1)
                if sq is not None:
                    act.wait_ge(pj["v1"], sq + 1)
                    nc.scalar.activation(v1[:, :], PRV[:, :], ACT.Copy).then_inc(v1_r, 1)
                    act.wait_ge(rT_d["q1"], sq + 1)
                    nc.scalar.activation(flat(qT1), TC[:, :], ACT.Copy).then_inc(rT_r["q1"], 1)
                for t in range(STEPS):
                    if t == (2 if sq is not None else 0) and cq is not None:
                        act.wait_ge(rT_d["q2"], cq + 1)
                        nc.scalar.activation(flat(qT2), TB[:, :], ACT.Copy).then_inc(rT_r["q2"], 1)
                    if t < len(order):
                        s = (s0 + t) % NP
                        kind, c = order[t]
                        rs = (rsum1, rsum2)[kind - 1]
                        act.wait_ge(nmax_r, n0 + t + 1)
                        if kind == 1 and c == 0:
                            wait(act, ri_r[1], sq)
                        if kind == 2 and c == 0:
                            wait(act, ri_r[2], cq)
                        wait(act, pT_d, n0 + t - NP + 1)
                        for j in range(G):
                            last = nc.scalar.activation(prob[:, s, j, :], SC[t % 2][:, j * P:(j + 1) * P], ACT.Exp,
                                                        bias=nmax[:, s, j:j + 1],
                                                        accum_out=rs[:, head(kind, c, j):head(kind, c, j) + 1])
                        last.then_inc(p_r, 1)
                    u = t - LT
                    if 0 <= u < len(order) and u % 2 == 1:
                        act.wait_ge(pT_d, n0 + u + 1)
                        wait(act, av_d, n0 + u - NP + 1)
                        nc.scalar.activation(probT[:, (s0 + u) % NP, :, :].rearrange("p g t -> p (g t)"),
                                             TP[1][:, :], ACT.Copy).then_inc(pTo_r, 1)
                    if t == 4 and nx is not None:
                        rough_rstd(1, nx)
                    if t == 6 and sq is not None:
                        act.wait_ge(ri_d[1], sq + 1)
                        nc.scalar.activation(rT1[:, :], TC[:, :], ACT.Copy).then_inc(riT_r[1], 1)
                    if t == 7 and sq is not None:
                        act.wait_ge(cn_r[1], sq + 1)
                        if cq is not None:
                            wait(act, pj["o2"], cq)
                        nc.scalar.activation(flat(cn_h), flat(cn), ACT.Copy).then_inc(cn_hi[1], 1)
                    if t == 8 and sq is not None:
                        act.wait_ge(cxT_d, sq + 1)
                        nc.scalar.activation(flat(cxT_h), TC[:, 0:CD], ACT.Copy).then_inc(cxT_hi, 1)
                    if t == 10 and sq is not None:
                        rough_rstd(2, sq)
                if cq is not None:
                    act.wait_ge(ri_d[2], cq + 1)
                    nc.scalar.activation(rT2[:, :], TC[:, :], ACT.Copy).then_inc(riT_r[2], 1)
                    act.wait_ge(cn_r[2], cq + 1)
                    if sq is not None:
                        act.wait_ge(pj["o1"], sq + 1)
                    nc.scalar.activation(flat(cn_h), flat(cn), ACT.Copy).then_inc(cn_hi[2], 1)
                if sq is not None:
                    act.wait_ge(pj["v2"], sq + 1)
                    v2p = PR0[:, :].rearrange("p (g a d) -> p g a d", a=2, d=DK2)
                    nc.scalar.activation(v2e[:, :, 0, :], v2p[:, :, 0, :], ACT.Copy)
                    nc.scalar.activation(v2o[:, :, 1, :], v2p[:, :, 1, :], ACT.Copy).then_inc(v2_r, 1)

            act.wait_ge(mv_r[1], 1)
            rough_rstd(1, 0)
            schedule(program, act.Fori)

        @block.vector
        def _(dve):
            small = {"n": 0, "base": 0}

            def link(ins):
                small["n"] += 1
                ins.then_inc(dstep, 1)
                dve.wait_ge(dstep, small["base"] + small["n"])

            pos_t = pos_sb[:, :].rearrange("p (b c) -> p b c", c=2)
            full_s = ang_s[:, :].rearrange("p (b c i) -> p b c i", b=B, c=2)
            turns = turns_sb[:, :]
            dve.wait_ge(pos_in, 16)
            for i in range(HALF):
                last = nc.vector.tensor_scalar(full_s[:, :, :, i], pos_t, float(np.float32(10000.0 ** (-i / HALF))), None, ALU.mult)
            link(last)
            link(nc.vector.tensor_scalar(turns, ang_s[:, :], 1.0 / TWO_PI, MAGIC, ALU.mult, ALU.add))
            link(nc.vector.tensor_scalar(turns, turns, MAGIC, None, ALU.subtract))
            for part in (PI_A, PI_B, PI_C):
                link(nc.vector.scalar_tensor_tensor(out=ang_s[:, :], in0=turns, scalar=-part, in1=ang_s[:, :],
                                                    op0=ALU.mult, op1=ALU.add))
            link(nc.vector.tensor_scalar(ang_s[:, :], ang_s[:, :], math.pi - 1e-6, -(math.pi - 1e-6), ALU.min, ALU.max))
            link(nc.vector.scalar_tensor_tensor(out=ang_c[:, :], in0=ang_s[:, :], scalar=-1.0, in1=ang_s[:, :],
                                                op0=ALU.mult, op1=ALU.max))
            nc.vector.tensor_scalar(ang_c[:, :], ang_c[:, :], -1.0, math.pi / 2, ALU.mult, ALU.add).then_inc(tab, 1)
            dve.wait_ge(tab_act, 2)
            flat_s = ang_s[:, :].rearrange("p (b j) -> p b j", b=B)
            flat_c = ang_c[:, :].rearrange("p (b j) -> p b j", b=B)
            c2 = cos2[:, :, :].rearrange("p b (j e) -> p b j e", e=2)
            s2 = sin2[:, :, :].rearrange("p b (j e) -> p b j e", e=2)
            nc.vector.tensor_copy(c2[:, :, :, 0], flat_c)
            nc.vector.tensor_copy(c2[:, :, :, 1], flat_c)
            nc.vector.tensor_scalar(s2[:, :, :, 0], flat_s, -1.0, None, ALU.mult)
            link(nc.vector.tensor_copy(s2[:, :, :, 1], flat_s))
            for n, (name, src, k, m) in enumerate(WSRC):
                dve.wait_ge(w_hi, n + 1)
                nc.vector.tensor_tensor(WLO[name][:, :, :], stage(n, k, m), WHI[name][:, :, :], ALU.subtract).then_inc(w_lo, 1)
            dve.wait_ge(c_in, 32)

            def flat(t):
                return t[:, :, :].rearrange("p k t -> p (k t)")

            def statistics(n, tile, q):
                link(nc.vector.bn_stats(st[n][:, :], tile[:, :]))
                dve.sem_inc(aggr, 1)
                nc.vector.bn_aggr(mv[n][:, :], st[n][:, :]).then_inc(mv_r[n], 1)

            def normalise(n, tile, z, q):
                t = nt[n]
                dve.wait_ge(rs_r[n], q + 1)
                link(nc.vector.tensor_scalar(t[:, 0:1], mv[n][:, 1:2], EPS, None, ALU.add))
                link(nc.vector.scalar_tensor_tensor(out=t[:, 1:2], in0=r0[n][:, :], scalar=t[:, 0:1], in1=r0[n][:, :],
                                                    op0=ALU.mult, op1=ALU.mult))
                link(nc.vector.tensor_scalar(t[:, 2:3], t[:, 1:2], -0.5, 1.5, ALU.mult, ALU.add))
                link(nc.vector.tensor_tensor(t[:, 3:4], t[:, 2:3], r0[n][:, :], ALU.mult))
                wait(dve, zT_d[n], q)
                nc.vector.tensor_scalar(z[:, :], tile[:, :], mv[n][:, 0:1], t[:, 3:4], ALU.subtract, ALU.mult)\
                    .then_inc(z_r[n], 1)

            def rope(n, q, src, w, cos, sin, scale):
                h = D // w
                dve.wait_ge(pj[n], q + 1)
                wait(dve, rT_d[n], q)
                nc.vector.scalar_tensor_tensor(
                    out=RA[n][:, :].rearrange("p (h j) -> p h j", j=w), in0=src[:, :].rearrange("p (h j) -> p h j", j=w),
                    scalar=scale, in1=cos.to_broadcast([P, h, w]), op0=ALU.mult, op1=ALU.mult)
                for e in range(2):
                    last = nc.vector.scalar_tensor_tensor(
                        out=RB[n][:, :].rearrange("p (h j e) -> p h j e", j=w // 2, e=2)[:, :, :, e],
                        in0=src[:, :].rearrange("p (h j e) -> p h j e", j=w // 2, e=2)[:, :, :, 1 - e], scalar=scale,
                        in1=sin.rearrange("p o (j e) -> p o j e", e=2)[:, :, :, e].to_broadcast([P, h, w // 2]),
                        op0=ALU.mult, op1=ALU.mult)
                last.then_inc(ab[n], 1)

            cos1, sin1 = cst[:, 0:DK1].unsqueeze(1), cst[:, DK1:2 * DK1].unsqueeze(1)
            even, odd = cst[:, 2 * DK1:2 * DK1 + 1], cst[:, 2 * DK1 + 1:2 * DK1 + 2]

            def low(dst, src, hi, s):
                nc.vector.tensor_tensor(flat(dst), src, flat(hi), ALU.subtract).then_inc(s, 1)

            def program(sq, cq, nx):
                order = chunks(sq, cq)
                n0, s0 = first_chunk(sq, cq), slots(cq)
                if cq is not None and not isinstance(cq, int):
                    small["base"], small["n"] = small["n"] - LOOP_STEPS + LOOP_STEPS * cq, 0
                if sq is not None:
                    dve.wait_ge(zT_hi[1], sq + 1)
                    low(z1T_l, TA[:, :], z1T_h, zT_lo[1])
                if cq is not None:
                    dve.wait_ge(zT_hi[2], cq + 1)
                    low(z2T_l, TB[:, :], z2T_h, zT_lo[2])
                if sq is not None:
                    rope("q1", sq, PR0, DK1, cos1, sin1, DK1 ** -0.5)
                    rope("k1", sq, PR1, DK1, cos1, sin1, 1.0)
                if cq is not None:
                    rope("q2", cq, PR0, DK2, cos2[:, bass.ds(cq, 1), :], sin2[:, bass.ds(cq, 1), :], DK2 ** -0.5)
                if sq is not None:
                    dve.wait_ge(rT_d["k1"], sq + 1)
                    nc.vector.tensor_copy(flat(kT1), TA[:, :]).then_inc(rT_r["k1"], 1)
                for t in range(STEPS):
                    if t == (2 if sq is not None else 0) and cq is not None:
                        dve.wait_ge(rT_d["k2"], cq + 1)
                        nc.vector.tensor_scalar(flat(kT2e), TC[:, :], even, None, ALU.mult)
                        nc.vector.tensor_scalar(flat(kT2o), TC[:, :], odd, None, ALU.mult).then_inc(rT_r["k2"], 1)
                    if t < len(order):
                        s = (s0 + t) % NP
                        dve.wait_ge(s_done, n0 + t + 1)
                        wait(dve, p_r, n0 + t - NP + 1)
                        nc.vector.tensor_reduce(out=nmax[:, s, :], in_=SC[t % 2][:, :].rearrange("p (g k) -> p g k", g=G),
                                                op=ALU.max, axis=AX, negate=True).then_inc(nmax_r, 1)
                    u = t - LT
                    if 0 <= u < len(order) and u % 2 == 0:
                        dve.wait_ge(pT_d, n0 + u + 1)
                        wait(dve, av_d, n0 + u - NP + 1)
                        nc.vector.tensor_copy(probT[:, (s0 + u) % NP, :, :].rearrange("p g t -> p (g t)"),
                                              TP[0][:, :]).then_inc(pTe_r, 1)
                    if t == 3 and nx is not None:
                        dve.wait_ge(x_in, 16 * (nx + 1))
                        statistics(1, xA, nx)
                    if t == 5 and nx is not None:
                        normalise(1, xA, z1, nx)
                    if t == 4 and sq is not None:
                        dve.wait_ge(p_r, n0 + NS)
                        wait(dve, rb_r[1], sq)
                        nc.vector.reciprocal(rinv1[:, :], rsum1[:, :]).then_inc(ri_r[1], 1)
                    if t == 6 and sq is not None:
                        dve.wait_ge(riT_r[1], sq + 1)
                        dve.wait_ge(av_d, n0 + NS)
                        nc.vector.tensor_tensor(flat(cn), PR1[:, :], rT1[:, :], ALU.mult).then_inc(cn_r[1], 1)
                    if t == 7 and sq is not None:
                        dve.wait_ge(cn_hi[1], sq + 1)
                        low(cn_l, flat(cn), cn_h, cn_lo[1])
                    if t == 8 and sq is not None:
                        dve.wait_ge(cxT_hi, sq + 1)
                        low(cxT_l, TC[:, 0:CD], cxT_h, cxT_lo)
                    if t == 9 and sq is not None:
                        dve.wait_ge(pj["o1"], sq + 1)
                        dve.wait_ge(x_copied, 16 * (sq + 1))
                        wait(dve, x1b_r, sq)
                        nc.vector.tensor_tensor(x1A[:, :], PR0[:, :], xB[:, :], ALU.add).then_inc(x1_r, 1)
                        dve.wait_ge(x1_r, sq + 1)
                        statistics(2, x1A, sq)
                    if t == 11 and sq is not None:
                        normalise(2, x1A, z2, sq)
                if cq is not None:
                    dve.wait_ge(p_r, n0 + len(order))
                    wait(dve, rb_r[2], cq)
                    nc.vector.reciprocal(rinv2[:, :], rsum2[:, :]).then_inc(ri_r[2], 1)
                    dve.wait_ge(riT_r[2], cq + 1)
                    dve.wait_ge(av_d, n0 + len(order))
                    nc.vector.tensor_tensor(flat(cn), PRV[:, :], rT2[:, :], ALU.mult).then_inc(cn_r[2], 1)
                    dve.wait_ge(cn_hi[2], cq + 1)
                    low(cn_l, flat(cn), cn_h, cn_lo[2])
                if sq is not None:
                    rope("k2", sq, PR1, DK2, cos2[:, bass.ds(sq, 1), :], sin2[:, bass.ds(sq, 1), :], 1.0)
                if cq is not None:
                    dve.wait_ge(pj["o2"], cq + 1)
                    dve.wait_ge(x1b_r, cq + 1)
                    wait(dve, x2_out, 16 * cq)
                    nc.vector.tensor_tensor(x2[:, :], PR1[:, :], x1B[:, :], ALU.add).then_inc(x2_r, 1)
                if cq is not None and not isinstance(cq, int):
                    assert small["n"] == LOOP_STEPS
                    small["base"], small["n"] = 0, before["n"] + LOOP_STEPS * (B - 3)

            LOOP_STEPS = 10
            dve.wait_ge(x_in, 16)
            statistics(1, xA, 0)
            normalise(1, xA, z1, 0)
            before = {"n": 0}

            @contextmanager
            def turns_of(a, b):
                before["n"] = small["n"]
                with dve.Fori(a, b) as c:
                    yield c

            schedule(program, turns_of)


def ffn_phase(nc, fp32, fp32r, i32, ALU, ACT, x2_dram, wg, sg, wu, su, wd, sd, out):
    es = ExitStack()
    with es:
        def sb(name, shape, dt=fp32):
            return es.enter_context(nc.sbuf_tensor(name, shape, dt))

        def sem(name):
            return es.enter_context(nc.semaphore(name))

        T = TPB * P
        wg_h, wg_l = sb("wg_h", [P, KT, HID], fp32r), sb("wg_l", [P, KT, HID], fp32r)
        wu_h, wu_l = sb("wu_h", [P, KT, HID], fp32r), sb("wu_l", [P, KT, HID], fp32r)
        wd_h, wd_l = sb("wd_h", [P, HT, D], fp32r), sb("wd_l", [P, HT, D], fp32r)
        stages = [sb(f"wstage{n}", [P, 2 * D], i32) for n in range(2)]
        sg_c, su_c, sd_b = sb("sg_c", [P, HT]), sb("su_c", [P, HT]), sb("sd_b", [P, D])
        eps_f, ident = sb("eps_f", [P, 1]), sb("ident_f", [P, P])
        xn = sb("xn", [P, TPB, D])
        xr = sb("xr", [P, TPB, D])
        zT_h, zT_l = sb("zT_h", [P, KT, T], fp32r), sb("zT_l", [P, KT, T], fp32r)
        sil = [sb(f"sil{n}", [P, T]) for n in range(2)]
        h = [sb(f"h{n}", [P, T]) for n in range(2)]
        h_h = [sb(f"h_h{n}", [P, T], fp32r) for n in range(2)]
        h_l = [sb(f"h_l{n}", [P, T], fp32r) for n in range(2)]
        ys = [sb(f"ys{n}", [P, D]) for n in range(2)]
        st, mv = sb("st", [P, TPB, 6]), sb("mv", [P, TPB, 2])
        lnv, r0, nt = sb("lnv", [P, TPB]), sb("r0", [P, TPB]), sb("nt", [P, 4, TPB])

        bank = [es.enter_context(nc.psum_tensor(f"fbank{n}", [P, 512], fp32)) for n in range(8)]
        DN = bank[0:TPB]
        GT = [bank[4], bank[6]]
        UP = [bank[5], bank[7]]
        TZ = [bank[6], bank[7], bank[4], bank[5]]

        w_in = [sem("fw_loaded0"), sem("fw_loaded1")]
        w_hi, w_lo = sem("fw_hi_ready"), sem("fw_lo_ready")
        cin, czero, cready = sem("f_scales_loaded"), sem("f_const_zeroed"), sem("f_ident_ready")
        xn_in, xr_in, stored = sem("xn_loaded"), sem("xr_loaded"), sem("out_stored")
        mv_r, ln_r, rs_r, z_r = sem("f_mean_var_ready"), sem("f_log_var_ready"), sem("f_rough_rstd_ready"), sem("f_z_ready")
        zT_d, zT_hr, zT_lr = sem("f_zT_done"), sem("f_zT_hi_ready"), sem("f_zT_lo_ready")
        g_d, u_d, dn_d = sem("gate_done"), sem("up_done"), sem("down_done")
        sil_r, h_r, hh_r, hl_r = sem("silu_ready"), sem("h_ready"), sem("h_hi_ready"), sem("h_lo_ready")
        ys_r, y_r = sem("scaled_down_ready"), sem("out_ready")
        rstd_r = sem("f_rstd_ready")
        dstep, aggr = sem("f_vector_small_step"), sem("f_vector_aggregates")

        block = es.enter_context(nc.Block())

        def wait(eng, s, value):
            if not isinstance(value, int) or value > 0:
                eng.wait_ge(s, value)

        pieces = []
        for j in range(0, HT, 2):
            m = min(2, HT - j)
            pieces += [("g", j, m), ("u", j, m), ("d", j, m)]

        def parts(n):
            kind, j, m = pieces[n]
            if kind == "d":
                src = wd[j * P:(j + m) * P, :].rearrange("(k p) n -> p k n", p=P)
                s = stages[n % 2][:, 0:m * D].rearrange("p (k n) -> p k n", n=D)
                return src, s, wd_h[:, j:j + m, :], wd_l[:, j:j + m, :]
            w, hi, lo = (wg, wg_h, wg_l) if kind == "g" else (wu, wu_h, wu_l)
            cols = slice(j * P, (j + m) * P)
            s = stages[n % 2][:, 0:KT * m * P].rearrange("p (k n) -> p k n", k=KT)
            return w[:, cols].rearrange("(k p) n -> p k n", p=P), s, hi[:, :, cols], lo[:, :, cols]

        def pieces_at(j):
            return range(3 * (j // 2 + 1), min(3 * (j // 2 + 2), len(pieces))) if j % 2 == 0 else ()

        def seqs(ap, nb):
            first = nb * TPB
            return ap[bass.ds(first, TPB), :, :].rearrange("s p d -> p s d")

        def schedule(program, fori):
            program(0, 1, True)
            with fori(1, NBLK - 1) as nb:
                program(nb, nb + 1, False)
            program(NBLK - 1, None, False)

        @block.sync
        def _(sp):
            sp.dma_start(xn[:, :, :], seqs(x2_dram, 0)).then_inc(xn_in, 16)
            sp.dma_start(sg_c[:, :], sg).then_inc(cin, 16)
            sp.dma_start(su_c[:, :], su).then_inc(cin, 16)
            sp.dma_start(sd_b[:, :], sd.partition_broadcast(P)).then_inc(cin, 16)

            def load_pieces(a, b):
                for n in range(a, b):
                    src, s, _, _ = parts(n)
                    if n >= 2:
                        sp.wait_ge(w_lo, n - 1)
                    sp.dma_start(s, src).then_inc(w_in[n % 2], 16)

            load_pieces(0, 6)

            def program(nb, nx, first):
                wait(sp, stored, 16 * nb)
                sp.dma_start(xr[:, :, :], seqs(x2_dram, nb)).then_inc(xr_in, 16)
                if nx is not None:
                    sp.wait_ge(zT_d, KT * nx)
                    sp.dma_start(xn[:, :, :], seqs(x2_dram, nx)).then_inc(xn_in, 16)
                if first:
                    load_pieces(6, len(pieces))
                sp.wait_ge(y_r, TPB * (nb + 1))
                sp.dma_start(seqs(out, nb), xr[:, :, :]).then_inc(stored, 16)

            schedule(program, sp.Fori)
            sp.wait_ge(stored, 16 * NBLK)

        @block.gpsimd
        def _(pool):
            pool.memset(ident[:, :], 0.0).then_inc(czero, 1)
            pool.memset(eps_f[:, :], EPS).then_inc(czero, 1)
            pool.wait_ge(czero, 2)
            pool.affine_select(out=ident[:, :], in_=ident[:, :], compare_op=ALU.not_equal, fill=1.0,
                               base=0, pattern=[[-1, P]], channel_multiplier=1).then_inc(cready, 1)

            def program(nb, nx, first):
                pool.wait_ge(xr_in, 16 * (nb + 1))
                for s in range(TPB):
                    pool.wait_ge(ys_r, TPB * nb + s + 1)
                    pool.tensor_tensor(xr[:, s, :], xr[:, s, :], ys[s % 2][:, :], ALU.add).then_inc(y_r, 1)

            schedule(program, pool.Fori)

        @block.tensor
        def _(pe):
            def hidden(dst, wh, wl, j, nb):
                cols = slice(j * P, (j + 1) * P)
                n = 0
                for w, z in ((wh, zT_h), (wl, zT_h), (wh, zT_l)):
                    if z is zT_l and j == 0:
                        pe.wait_ge(zT_lr, KT * (nb + 1))
                    for k in range(KT):
                        last = nc.tensor.matmul(dst[:, :], w[:, k, cols], z[:, k, :], start=(n == 0), stop=(n == 3 * KT - 1))
                        n += 1
                return last

            def down(j, nb):
                pe.wait_ge(hh_r, HT * nb + j + 1)
                pe.wait_ge(hl_r, HT * nb + j + 1)
                if j == 0:
                    wait(pe, ys_r, TPB * nb)
                for s in range(TPB):
                    tok = slice(s * P, (s + 1) * P)
                    for n, (a, w) in enumerate(((h_h, wd_h), (h_h, wd_l), (h_l, wd_h))):
                        last = nc.tensor.matmul(DN[s][:, :], a[j % 2][:, tok], w[:, j, :],
                                                start=(j == 0 and n == 0), stop=(j == HT - 1 and n == 2))
                last.then_inc(dn_d, 1)

            def transpose_tile(k, nx):
                for s in range(TPB):
                    last = nc.tensor.transpose(TZ[k][:, s * P:(s + 1) * P], xn[:, s, k * P:(k + 1) * P], ident[:, :])
                last.then_inc(zT_d, 1)

            def program(nb, nx, first):
                pe.wait_ge(zT_hr, KT * (nb + 1))
                for j in range(HT):
                    if j == 0:
                        pe.wait_ge(zT_lr, KT * nb + 3)
                    elif j == 1:
                        pe.wait_ge(zT_lr, KT * nb + 2)
                    else:
                        pe.wait_ge(sil_r, HT * nb + j - 1)
                    if first:
                        pe.wait_ge(w_lo, min(3 * (j // 2) + 1, len(pieces)))
                    hidden(GT[j % 2], wg_h, wg_l, j, nb).then_inc(g_d, 1)
                    if j >= 2:
                        pe.wait_ge(h_r, HT * nb + j - 1)
                    elif j == 0:
                        pe.wait_ge(zT_lr, KT * nb + 4)
                    if first:
                        pe.wait_ge(w_lo, min(3 * (j // 2) + 2, len(pieces)))
                    hidden(UP[j % 2], wu_h, wu_l, j, nb).then_inc(u_d, 1)
                    if nx is not None and j == HT - 1:
                        pe.wait_ge(z_r, nx + 1)
                        pe.wait_ge(sil_r, HT * nb + HT - 1)
                        pe.wait_ge(h_r, HT * nb + HT - 1)
                        transpose_tile(0, nx)
                        transpose_tile(1, nx)
                    if j >= 1:
                        if first:
                            pe.wait_ge(w_lo, min(3 * ((j - 1) // 2) + 3, len(pieces)))
                        down(j - 1, nb)
                if nx is not None:
                    pe.wait_ge(sil_r, HT * (nb + 1))
                    pe.wait_ge(h_r, HT * (nb + 1))
                    transpose_tile(2, nx)
                    transpose_tile(3, nx)
                if first:
                    pe.wait_ge(w_lo, len(pieces))
                down(HT - 1, nb)

            pe.wait_ge(cready, 1)
            pe.wait_ge(z_r, 1)
            for k in range(KT):
                transpose_tile(k, 0)
            schedule(program, pe.Fori)

        @block.scalar
        def _(act):
            def split_hi(n):
                _, s, hi, _ = parts(n)
                act.wait_ge(w_in[n % 2], 16 * (n // 2 + 1))
                nc.scalar.activation(hi, s, ACT.Copy, bias=-ZERO_POINT).then_inc(w_hi, 1)

            def rough_rstd(q):
                act.wait_ge(mv_r, q + 1)
                nc.scalar.activation(lnv[:, :], mv[:, :, 1], ACT.Ln, bias=eps_f[:, :]).then_inc(ln_r, 1)
                act.wait_ge(ln_r, q + 1)
                nc.scalar.activation(r0[:, :], lnv[:, :], ACT.Exp, scale=-0.5).then_inc(rs_r, 1)

            def zT_high(k, q):
                act.wait_ge(zT_d, KT * q + k + 1)
                nc.scalar.activation(zT_h[:, k, :], TZ[k][:, :], ACT.Copy).then_inc(zT_hr, 1)

            def program(nb, nx, first):
                for j in range(HT):
                    if first:
                        for n in pieces_at(j):
                            split_hi(n)
                    act.wait_ge(g_d, HT * nb + j + 1)
                    if j >= 2:
                        act.wait_ge(h_r, HT * nb + j - 1)
                    nc.scalar.activation(sil[j % 2][:, :], GT[j % 2][:, :], ACT.Silu, scale=sg_c[:, j:j + 1]).then_inc(sil_r, 1)
                    if j == 5 and nx is not None:
                        rough_rstd(nx)
                    act.wait_ge(h_r, HT * nb + j + 1)
                    if j >= 2:
                        act.wait_ge(dn_d, HT * nb + j - 1)
                    else:
                        wait(act, dn_d, HT * nb)
                    nc.scalar.activation(h_h[j % 2][:, :], h[j % 2][:, :], ACT.Copy).then_inc(hh_r, 1)
                if nx is not None:
                    for k in range(KT):
                        zT_high(k, nx)

            act.wait_ge(czero, 2)
            rough_rstd(0)
            for n in range(3):
                split_hi(n)
            for k in range(KT):
                zT_high(k, 0)
            act.wait_ge(cin, 48)
            schedule(program, act.Fori)

        @block.vector
        def _(dve):
            def split_lo(n):
                _, s, hi, lo = parts(n)
                dve.wait_ge(w_hi, n + 1)
                nc.vector.scalar_tensor_tensor(out=lo, in0=s, scalar=ZERO_POINT, in1=hi,
                                               op0=ALU.subtract, op1=ALU.subtract).then_inc(w_lo, 1)

            NSTEP = 4

            def statistics(q):
                dve.wait_ge(xn_in, 16 * (q + 1))
                for s in range(TPB):
                    last = nc.vector.bn_stats(st[:, s, :], xn[:, s, :])
                last.then_inc(dstep, 1)
                dve.wait_ge(dstep, NSTEP * q + 1)
                dve.sem_inc(aggr, 1)
                for s in range(TPB):
                    last = nc.vector.bn_aggr(mv[:, s, :], st[:, s, :])
                last.then_inc(mv_r, 1)

            def normalise(q):
                dve.wait_ge(rs_r, q + 1)
                nc.vector.scalar_tensor_tensor(out=nt[:, 0, :], in0=mv[:, :, 1], scalar=EPS, in1=r0[:, :],
                                               op0=ALU.add, op1=ALU.mult).then_inc(dstep, 1)
                dve.wait_ge(dstep, NSTEP * q + 2)
                nc.vector.tensor_tensor(nt[:, 1, :], nt[:, 0, :], r0[:, :], ALU.mult).then_inc(dstep, 1)
                dve.wait_ge(dstep, NSTEP * q + 3)
                nc.vector.tensor_scalar(nt[:, 2, :], nt[:, 1, :], -0.5, 1.5, ALU.mult, ALU.add).then_inc(dstep, 1)
                dve.wait_ge(dstep, NSTEP * q + 4)
                nc.vector.tensor_tensor(nt[:, 3, :], nt[:, 2, :], r0[:, :], ALU.mult).then_inc(rstd_r, 1)
                dve.wait_ge(rstd_r, q + 1)
                for s in range(TPB):
                    last = nc.vector.tensor_scalar(xn[:, s, :], xn[:, s, :], mv[:, s, 0:1], nt[:, 3, s:s + 1],
                                                   ALU.subtract, ALU.mult)
                last.then_inc(z_r, 1)

            def zT_low(k, q):
                dve.wait_ge(zT_hr, KT * q + k + 1)
                nc.vector.tensor_tensor(zT_l[:, k, :], TZ[k][:, :], zT_h[:, k, :], ALU.subtract).then_inc(zT_lr, 1)

            def program(nb, nx, first):
                for j in range(HT):
                    if first:
                        for n in pieces_at(j):
                            split_lo(n)
                    dve.wait_ge(u_d, HT * nb + j + 1)
                    dve.wait_ge(sil_r, HT * nb + j + 1)
                    if j >= 2:
                        dve.wait_ge(hh_r, HT * nb + j - 1)
                    nc.vector.scalar_tensor_tensor(out=h[j % 2][:, :], in0=UP[j % 2][:, :], scalar=su_c[:, j:j + 1],
                                                   in1=sil[j % 2][:, :], op0=ALU.mult, op1=ALU.mult).then_inc(h_r, 1)
                    dve.wait_ge(hh_r, HT * nb + j + 1)
                    nc.vector.tensor_tensor(h_l[j % 2][:, :], h[j % 2][:, :], h_h[j % 2][:, :], ALU.subtract).then_inc(hl_r, 1)
                    if j == 4 and nx is not None:
                        statistics(nx)
                    if j == 6 and nx is not None:
                        normalise(nx)
                if nx is not None:
                    for k in range(KT):
                        zT_low(k, nx)
                dve.wait_ge(dn_d, HT * (nb + 1))
                for s in range(TPB):
                    if s >= 2:
                        dve.wait_ge(y_r, TPB * nb + s - 1)
                    else:
                        wait(dve, y_r, TPB * nb)
                    nc.vector.tensor_tensor(ys[s % 2][:, :], DN[s][:, :], sd_b[:, :], ALU.mult).then_inc(ys_r, 1)

            statistics(0)
            normalise(0)
            for n in range(3):
                split_lo(n)
            for k in range(KT):
                zT_low(k, 0)
            dve.wait_ge(cin, 48)
            schedule(program, dve.Fori)


def kernel(**inputs):
    import concourse.bacc as bacc
    from concourse.bass_utils import run_bass_kernel_spmd

    a = {k: np.asarray(v) for k, v in inputs.items()}

    def c(v):
        return np.ascontiguousarray(v)

    arrays = {
        "x": c(a["x"]), "ctx": c(a["ctx_1024"]), "pos": c(a["fside_BxSx2_0"].transpose(1, 0, 2).reshape(P, 2 * B)),
        "consts": shape_constants(),
        "wq1": c(a["L0_attn_Wq"].T), "wk1": c(a["L0_attn_Wk"].T), "wv1": c(a["L0_attn_Wv"].T), "wo1": c(a["L0_attn_Wo"].T),
        "wq2": c(a["L0_xattn_Wq"]), "wkv2": c(a["L0_xattn_Wkv"]), "wo2": c(a["L0_xattn_Wout"]), "bout": c(a["L0_xattn_bout"]),
        "wg": c(a["L0_ffn_wq_gate"].T), "sg": c(a["L0_ffn_s_gate"].reshape(HT, P).T),
        "wu": c(a["L0_ffn_wq_up"].T), "su": c(a["L0_ffn_s_up"].reshape(HT, P).T),
        "wd": c(a["L0_ffn_wq_down"].T), "sd": c(a["L0_ffn_s_down"]),
    }
    nc = bacc.Bacc("TRN2", target_bir_lowering=False, num_devices=1)
    t = {n: nc.dram_tensor(f"in_{n}", v.shape, mybir.dt.from_np(v.dtype), kind="ExternalInput").ap() for n, v in arrays.items()}
    out = nc.dram_tensor("out", (B, P, D), mybir.dt.float32, kind="ExternalOutput").ap()
    x2_dram = nc.dram_tensor("x2_scratch", (B, P, D), mybir.dt.float32, kind="Internal").ap()
    build_decoder(nc, t["x"], t["ctx"], t["pos"], t["consts"], t["wq1"], t["wk1"], t["wv1"], t["wo1"],
                  t["wq2"], t["wkv2"], t["wo2"], t["bout"], t["wg"], t["sg"], t["wu"], t["su"], t["wd"], t["sd"],
                  out, x2_dram)
    r = run_bass_kernel_spmd(nc, [{f"in_{n}": v for n, v in arrays.items()}], core_ids=[0])
    return r.results[0]["out"]
```

```python
import math
from contextlib import ExitStack, contextmanager

import numpy as np

import concourse.bass as bass
from concourse import mybir

P = 128
B = 32
D = 512
KT = D // P
CD = 256
CKT = CD // P
H1, DK1 = 16, 32
H2, DK2 = 32, 16
HID = 1408
HT = HID // P
G = 4
NS = H1 // G
NC = H2 // G
TPB = 4
NBLK = B // TPB
EPS = 1e-5
ZERO_POINT = 128.0
NEG = -1.0e30
THETA = 10000.0
HALF = 4
MAGIC = 12582912.0
TWO_PI = 2.0 * math.pi
PI_A = 6.28125
PI_B = float(np.float32(np.round((TWO_PI - PI_A) * 2.0 ** 20) / 2.0 ** 20))
PI_C = float(np.float32(TWO_PI - PI_A - PI_B))
NCONST = 2 * DK1 + 2


def shape_constants():
    inv = np.exp(np.float32(-math.log(THETA)) * np.arange(0, DK1, 2, dtype=np.float32) / np.float32(DK1))
    ang = np.arange(P, dtype=np.float32)[:, None] * inv.astype(np.float32)[None, :]
    cos, sin = np.cos(ang), np.sin(ang)
    c = np.zeros((P, NCONST), np.float32)
    c[:, 0:DK1:2] = cos
    c[:, 1:DK1:2] = cos
    c[:, DK1:2 * DK1:2] = -sin
    c[:, DK1 + 1:2 * DK1:2] = sin
    odd = (np.arange(P) // DK2) % 2
    c[:, 2 * DK1] = 1 - odd
    c[:, 2 * DK1 + 1] = odd
    return c


def build_decoder(nc, x, ctx_in, pos, consts, wq1, wk1, wv1, wo1, wq2, wkv2, wo2, bout,
                  wg, sg, wu, su, wd, sd, out, x2_dram):
    fp32, bf16, fp32r, i32 = mybir.dt.float32, mybir.dt.bfloat16, mybir.dt.float32r, mybir.dt.int32
    ALU = mybir.AluOpType
    ACT = mybir.ActivationFunctionType
    AX = mybir.AxisListType.X

    AXY = mybir.AxisListType.XY

    attention_phase(nc, fp32, bf16, fp32r, ALU, ACT, AX, x, ctx_in, pos, consts,
                    wq1, wk1, wv1, wo1, wq2, wkv2, wo2, bout, x2_dram)
    ffn_phase(nc, fp32, fp32r, i32, ALU, ACT, AX, AXY, x2_dram, wg, sg, wu, su, wd, sd, out)


def attention_phase(nc, fp32, bf16, fp32r, ALU, ACT, AX, x, ctx_in, pos, consts,
                    wq1, wk1, wv1, wo1, wq2, wkv2, wo2, bout, x2_dram):
    es = ExitStack()
    with es:
        def sb(name, shape, dt=fp32):
            return es.enter_context(nc.sbuf_tensor(name, shape, dt))

        def sem(name):
            return es.enter_context(nc.semaphore(name))

        WSRC = [("q1", wq1, KT, D), ("k1", wk1, KT, D), ("v1", wv1, KT, D), ("o1", wo1, KT, D),
                ("kv2", wkv2, CKT, 2 * D), ("q2", wq2, KT, D), ("o2", wo2, KT, D)]
        WHI = {n: sb(f"w_{n}_hi", [P, k, m], fp32r) for n, _, k, m in WSRC}
        WLO = {n: sb(f"w_{n}_lo", [P, k, m], fp32r) for n, _, k, m in WSRC}

        cst = sb("cst", [P, NCONST])
        ident = sb("ident", [P, P])
        ident16 = sb("ident16", [P, P], bf16)
        causal = sb("causal", [P, G, P], bf16)
        bout_b = sb("bout_b", [P, D])
        cos2 = sb("cos2", [P, B, DK2])
        sin2 = sb("sin2", [P, B, DK2])
        mhalf_c, one_c = sb("mhalf_c", [P, 1]), sb("one_c", [P, 1])

        xA, xB = sb("xA", [P, D]), sb("xB", [P, D])
        x1A, x1B, x2 = sb("x1A", [P, D]), sb("x1B", [P, D]), sb("x2", [P, D])
        z1, z2 = sb("z1", [P, D]), sb("z2", [P, D])
        z1T_h, z1T_l = sb("z1T_h", [P, KT, P], fp32r), sb("z1T_l", [P, KT, P], fp32r)
        z2T_h, z2T_l = sb("z2T_h", [P, KT, P], fp32r), sb("z2T_l", [P, KT, P], fp32r)
        cx = sb("cx", [P, CD])
        cxT_h, cxT_l = sb("cxT_h", [P, CKT, P], fp32r), sb("cxT_l", [P, CKT, P], fp32r)
        rope_buf = sb("rope_buf", [P, 8, D])
        RA = {n: rope_buf[:, j, :] for j, n in enumerate(("q1", "k1", "q2", "k2"))}
        RB = {n: rope_buf[:, 4 + j, :] for j, n in enumerate(("q1", "k1", "q2", "k2"))}
        qT1, kT1 = sb("qT1", [P, KT, P]), sb("kT1", [P, KT, P])
        qT2, kT2e, kT2o = sb("qT2", [P, KT, P]), sb("kT2e", [P, KT, P]), sb("kT2o", [P, KT, P])
        v1 = sb("v1", [P, D])
        v2e, v2o = sb("v2e", [P, H2 // 2, 2, DK2]), sb("v2o", [P, H2 // 2, 2, DK2])
        NP = 3
        prob = sb("prob", [P, NP, G, P])
        probT = sb("probT", [P, NP, G, P])
        nmax = sb("nmax", [P, NP, G])
        rsum1, rsum2 = sb("rsum1", [P, H1]), sb("rsum2", [P, H2])
        rinv1, rinv2 = sb("rinv1", [P, H1]), sb("rinv2", [P, H2])
        rbc1, rbc2 = sb("rbc1", [P, H1, DK1]), sb("rbc2", [P, H2, DK2])
        rT1, rT2 = sb("rT1", [P, D]), sb("rT2", [P, D])
        cn, cn_h, cn_l = sb("cn", [P, KT, P]), sb("cn_h", [P, KT, P], fp32r), sb("cn_l", [P, KT, P], fp32r)
        st = {n: sb(f"st{n}", [P, 6]) for n in (1, 2)}
        mv = {n: sb(f"mv{n}", [P, 2]) for n in (1, 2)}
        ve = {n: sb(f"ve{n}", [P, 1]) for n in (1, 2)}
        r0 = {n: sb(f"r0{n}", [P, 1]) for n in (1, 2)}
        nt = {n: sb(f"nt{n}", [P, 4]) for n in (1, 2)}

        ang_s, ang_c = z2[:, 0:B * 2 * HALF], z2[:, B * 2 * HALF:2 * B * 2 * HALF]
        turns_sb, pos_sb = rT2[:, 0:B * 2 * HALF], rT2[:, B * 2 * HALF:B * 2 * HALF + 2 * B]
        def stage(n, k, m):
            return rope_buf[:, 4 * (n % 2):4 * (n % 2) + 4, :].rearrange("p a b -> p (a b)").rearrange("p (k n) -> p k n", k=k)

        bank = [es.enter_context(nc.psum_tensor(f"bank{n}", [P, 512], fp32)) for n in range(8)]
        PA, PB, PC = bank[0], bank[1], bank[6]
        SC = [bank[2], bank[3]]
        TA, TB, TC = bank[4], bank[5], bank[7]
        TP = [TA, TB]

        wstage_in = [sem("wstage_in0"), sem("wstage_in1")]
        w_hi, w_lo = sem("w_hi_ready"), sem("w_lo_ready")
        c_in, c_zero, c_ready = sem("const_loaded"), sem("const_zeroed"), sem("const_ready")
        pos_in, tab, tab_act = sem("pos_loaded"), sem("rotary_table"), sem("rotary_sin")
        x_in, xb_in, cx_in = sem("x_loaded"), sem("x_residual_loaded"), sem("ctx_loaded")
        mv_r = {n: sem(f"mean_var{n}_ready") for n in (1, 2)}
        ve_r = {n: sem(f"var_eps{n}_ready") for n in (1, 2)}
        rs_r = {n: sem(f"rough_rstd{n}_ready") for n in (1, 2)}
        z_r = {n: sem(f"z{n}_ready") for n in (1, 2)}
        zT_d = {n: sem(f"z{n}T_done") for n in (1, 2)}
        zT_hi = {n: sem(f"z{n}T_hi_ready") for n in (1, 2)}
        zT_lo = {n: sem(f"z{n}T_lo_ready") for n in (1, 2)}
        cxT_d, cxT_hi, cxT_lo = sem("ctxT_done"), sem("ctxT_hi_ready"), sem("ctxT_lo_ready")
        NAMES = ("q1", "k1", "q2", "k2")
        pj = {n: sem(f"proj_{n}_done") for n in NAMES + ("v1", "v2", "o1", "o2")}
        ab = {n: sem(f"rope_{n}_products") for n in NAMES}
        rot = {n: sem(f"rope_{n}_ready") for n in NAMES}
        rT_d = {n: sem(f"{n}_transposed") for n in NAMES}
        rT_r = {n: sem(f"{n}T_ready") for n in NAMES}
        v1_r, v2_r = sem("v1_ready"), sem("v2_ready")
        s_done, nmax_r, p_r = sem("scores_done"), sem("nmax_ready"), sem("prob_ready")
        pT_d, pTe_r, pTo_r = sem("probT_done"), sem("probT_even_ready"), sem("probT_odd_ready")
        av_d = sem("attn_out_done")
        ri_r = {n: sem(f"rinv{n}_ready") for n in (1, 2)}
        rb_r = {n: sem(f"rinv{n}_spread") for n in (1, 2)}
        ri_d = {n: sem(f"rinv{n}T_done") for n in (1, 2)}
        riT_r = {n: sem(f"rinv{n}T_ready") for n in (1, 2)}
        cn_r = {n: sem(f"ctxn{n}_ready") for n in (1, 2)}
        cn_hi = {n: sem(f"ctxn{n}_hi_ready") for n in (1, 2)}
        cn_lo = {n: sem(f"ctxn{n}_lo_ready") for n in (1, 2)}
        x1_r, x1b_r, x2_r, x2_out = sem("x1_ready"), sem("x1_bout_ready"), sem("x2_ready"), sem("x2_stored")
        dstep = sem("vector_small_step")
        aggr = sem("vector_aggregates")

        block = es.enter_context(nc.Block())

        def wait(eng, s, value):
            if not isinstance(value, int) or value > 0:
                eng.wait_ge(s, value)

        def chunks(sq, cq):
            return ([(1, c) for c in range(NS)] if sq is not None else []) + \
                   ([(2, c) for c in range(NC)] if cq is not None else [])

        def head(kind, c, j):
            return (P // DK1) * j + c if kind == 1 else (P // DK2) * j + c

        def first_chunk(cq, oq):
            if cq is None:
                return 0 if oq is None else (NS + NC) * B
            return NS + (NS + NC) * cq

        def first_pair(cq, oq):
            if cq is None:
                return 0 if oq is None else (NS + NC) // 2 * B
            return NS // 2 + (NS + NC) // 2 * cq

        def slots(cq):
            return 0 if cq is None else NS

        LT, LA = 2, 3
        STEPS = NS + NC + LA
        K2T, V2T, Z2T, QA, V1A, NZ2, K2R, CXT, CXA, O2T = 10, 12, 14, 3, 7, 10, 13, 4, 4, 2

        def schedule(turn, fori):
            turn(None, None, 0, 1, None)
            turn(0, None, 1, 2, None)
            turn(1, 0, 2, 3, None)
            turn(2, 1, 3, 4, 0)
            with fori(2, B - 3) as c:
                turn(c + 1, c, c + 2, c + 3, c - 1)
            turn(B - 2, B - 3, B - 1, None, B - 4)
            turn(B - 1, B - 2, None, None, B - 3)
            turn(None, B - 1, None, None, B - 2)
            turn(None, None, None, None, B - 1)

        @block.sync
        def _(sp):
            sp.dma_start(xA[:, :], x[0, :, :]).then_inc(x_in, 16)
            sp.dma_start(pos_sb[:, :], pos).then_inc(pos_in, 16)
            sp.dma_start(cst[:, :], consts).then_inc(c_in, 16)
            sp.dma_start(bout_b[:, :], bout.partition_broadcast(P)).then_inc(c_in, 16)
            for n, (name, src, k, m) in enumerate(WSRC):
                if n >= 2:
                    sp.wait_ge(w_lo, n - 1)
                sp.dma_start(stage(n, k, m), src.rearrange("(k p) n -> p k n", p=P)).then_inc(wstage_in[n % 2], 16)

            def turn(sq, cq, nx, nz, oq):
                if sq is not None:
                    wait(sp, cxT_d, sq)
                    sp.dma_start(cx[:, :], ctx_in[sq, :, :]).then_inc(cx_in, 16)
                    wait(sp, x1_r, sq)
                    sp.dma_start(xB[:, :], x[sq, :, :]).then_inc(xb_in, 16)
                if nz is not None:
                    sp.wait_ge(z_r[1], nz)
                    sp.dma_start(xA[:, :], x[nz, :, :]).then_inc(x_in, 16)
                if oq is not None:
                    sp.wait_ge(x2_r, oq + 1)
                    sp.dma_start(x2_dram[oq, :, :], x2[:, :]).then_inc(x2_out, 16)

            schedule(turn, sp.Fori)
            sp.wait_ge(x2_out, 16 * B)

        @block.gpsimd
        def _(pool):
            pool.memset(ident[:, :], 0.0).then_inc(c_zero, 1)
            pool.memset(causal[:, :, :], 0.0).then_inc(c_zero, 1)
            pool.memset(v2e[:, :, :, :], 0.0).then_inc(c_zero, 1)
            pool.memset(v2o[:, :, :, :], 0.0).then_inc(c_zero, 1)
            pool.memset(mhalf_c[:, :], -0.5).then_inc(c_zero, 1)
            pool.memset(one_c[:, :], 1.0).then_inc(c_zero, 1)
            pool.wait_ge(c_zero, 6)
            pool.affine_select(out=ident[:, :], in_=ident[:, :], compare_op=ALU.not_equal, fill=1.0,
                               base=0, pattern=[[-1, P]], channel_multiplier=1).then_inc(c_ready, 1)
            pool.affine_select(out=causal[:, :, :], in_=causal[:, :, :], compare_op=ALU.is_ge, fill=NEG,
                               base=0, pattern=[[0, G], [-1, P]], channel_multiplier=1).then_inc(c_ready, 1)
            pool.wait_ge(c_ready, 1)
            pool.tensor_copy(ident16[:, :], ident[:, :]).then_inc(c_ready, 1)

            def rough_rstd(n, q):
                pool.wait_ge(ve_r[n], q + 1)
                pool.tensor_tensor(r0[n][:, :], ve[n][:, :], mhalf_c[:, :], ALU.pow).then_inc(rs_r[n], 1)

            def rope_sum(n, q):
                wait(pool, ab[n], q + 1)
                pool.tensor_tensor(RA[n][:, :], RA[n][:, :], RB[n][:, :], ALU.add).then_inc(rot[n], 1)

            def spread(n, q, r, tile, h, w):
                wait(pool, ri_d[n], q)
                pool.wait_ge(ri_r[n], q + 1)
                pool.tensor_tensor(tile[:, :, :], r[:, :].unsqueeze(2).to_broadcast([P, h, w]),
                                   one_c[:, :].unsqueeze(2).to_broadcast([P, h, w]), ALU.mult).then_inc(rb_r[n], 1)

            def ctx_low(n, q):
                pool.wait_ge(cn_r[n], q + 1)
                pool.tensor_tensor(cn_l[:, :, :], cn[:, :, :], cn_h[:, :, :], ALU.subtract).then_inc(cn_lo[n], 1)

            def turn(sq, cq, nx, nz, oq):
                if oq is not None:
                    ctx_low(2, oq)
                if cq is not None:
                    rope_sum("q2", cq)
                    pool.wait_ge(x1_r, cq + 1)
                    wait(pool, x2_r, cq)
                    pool.tensor_tensor(x1B[:, :], x1A[:, :], bout_b[:, :], ALU.add).then_inc(x1b_r, 1)
                if nx is not None:
                    rope_sum("q1", nx)
                if sq is not None:
                    spread(1, sq, rinv1, rbc1, H1, DK1)
                if nx is not None:
                    rope_sum("k1", nx)
                if nz is not None:
                    rough_rstd(1, nz)
                if sq is not None:
                    ctx_low(1, sq)
                    rough_rstd(2, sq)
                if cq is not None:
                    spread(2, cq, rinv2, rbc2, H2, DK2)
                if sq is not None:
                    rope_sum("k2", sq)

            pool.wait_ge(c_in, 32)
            rough_rstd(1, 0)
            schedule(turn, pool.Fori)

        @block.tensor
        def _(pe):
            def transpose4(dst, src, k=KT):
                for j in range(k):
                    last = nc.tensor.transpose(dst[:, j * P:(j + 1) * P], src(j), ident[:, :])
                return last

            def project(dst, th, tl, name, k, cols=slice(0, D), lo_ready=None):
                hi, lo = WHI[name], WLO[name]
                n = 0
                for a, w in ((th, hi), (th, lo), (tl, hi)):
                    if a is tl and lo_ready is not None:
                        pe.wait_ge(*lo_ready)
                    for j in range(k):
                        last = nc.tensor.matmul(dst[:, :], a[:, j, :], w[:, j, cols],
                                                start=(n == 0), stop=(n == 3 * k - 1))
                        n += 1
                return last

            def scores(kind, c, slot, m):
                if kind == 1:
                    nc.tensor.matmul(SC[m][:, :], ident16[:, :], causal[:, :, :].rearrange("p g t -> p (g t)"),
                                     start=True, stop=False, skip_group_check=True)
                for j in range(G):
                    if kind == 1:
                        r, q, k = DK1 * c, qT1, kT1
                    else:
                        r, q, k = 2 * DK2 * (c // 2), qT2, (kT2e, kT2o)[c % 2]
                    last = nc.tensor.matmul(SC[m][:, j * P:(j + 1) * P], q[r:r + 32, j, :], k[r:r + 32, j, :],
                                            start=(kind == 2), stop=True, skip_group_check=True)
                last.then_inc(s_done, 1)

            def attend(kind, c, slot):
                for j in range(G):
                    if kind == 1:
                        r, dst, v = DK1 * c, PC, v1[:, head(1, c, j) * DK1:(head(1, c, j) + 1) * DK1]
                        start, stop = True, True
                    else:
                        pair = head(2, c, j) // 2
                        r, dst, v = 2 * DK2 * (c // 2), PB, (v2e, v2o)[c % 2][:, pair, :, :].rearrange("p a d -> p (a d)")
                        start, stop = c % 2 == 0 and j == 0, c % 2 == 1
                    last = nc.tensor.matmul(dst[r:r + 32, j * P:(j + 1) * P], v, probT[:, slot, j, :],
                                            start=start, stop=stop, skip_group_check=True)
                last.then_inc(av_d, 1)

            def columns(t):
                return lambda j: t[:, j * P:(j + 1) * P]

            def turn(sq, cq, nx, nz, oq):
                order = chunks(sq, cq)
                n0, s0, par = first_chunk(cq, oq), slots(cq), first_pair(cq, oq)
                has_s, has_c, has_n, has_o = sq is not None, cq is not None, nx is not None, oq is not None
                if has_n:
                    pe.wait_ge(z_r[1], nx + 1)
                    wait(pe, pTe_r, par)
                    transpose4(TA, columns(z1)).then_inc(zT_d[1], 1)
                if has_o and not has_s:
                    transpose_rinv2(oq, par)
                if has_c and not has_s:
                    project_q2(cq)
                for t in range(STEPS):
                    if t < len(order):
                        kind, c = order[t]
                        wait(pe, p_r, n0 + t - 1)
                        if kind == 1 and c == 0:
                            pe.wait_ge(rT_r["q1"], sq + 1)
                            pe.wait_ge(rT_r["k1"], sq + 1)
                        if kind == 2 and c == 0:
                            if not has_s:
                                transpose_q2_k2(cq, par, has_o)
                            pe.wait_ge(rT_r["q2"], cq + 1)
                            pe.wait_ge(rT_r["k2"], cq + 1)
                        scores(kind, c, (s0 + t) % NP, t % 2)
                    if t == 0 and has_o and has_s:
                        transpose_rinv2(oq, par)
                    if t == 0 and has_c and has_s:
                        project_q2(cq)
                    if t == O2T and has_o:
                        pe.wait_ge(cn_r[2], oq + 1)
                        project(PB, cn_h, cn_l, "o2", KT, lo_ready=(cn_lo[2], oq + 1)).then_inc(pj["o2"], 1)
                    if t == 2 and has_c and has_s:
                        transpose_q2_k2(cq, par, has_o)
                    if t == 3 and has_n:
                        pe.wait_ge(zT_hi[1], nx + 1)
                        if has_c:
                            pe.wait_ge(ab["q2"], cq + 1)
                        else:
                            wait(pe, v1_r, nx)
                        project(PA, z1T_h, z1T_l, "q1", KT, lo_ready=(zT_lo[1], nx + 1)).then_inc(pj["q1"], 1)
                    if t == 4 and has_n:
                        if has_o:
                            pe.wait_ge(x2_r, oq + 1)
                        else:
                            wait(pe, ab["k1"], nx)
                        project(PB, z1T_h, z1T_l, "k1", KT).then_inc(pj["k1"], 1)
                    if t == CXT and has_s:
                        pe.wait_ge(cx_in, 16 * (sq + 1))
                        if has_c:
                            pe.wait_ge(rT_r["k2"], cq + 1)
                        transpose4(TC, columns(cx), CKT).then_inc(cxT_d, 1)
                    if t == 6 and has_n:
                        pe.wait_ge(ab["q1"], nx + 1)
                        project(PA, z1T_h, z1T_l, "v1", KT).then_inc(pj["v1"], 1)
                    if t == 6 and has_s:
                        pe.wait_ge(rb_r[1], sq + 1)
                        pe.wait_ge(cxT_lo, sq + 1)
                        transpose4(TC, columns(rbc1[:, :, :].rearrange("p h d -> p (h d)"))).then_inc(ri_d[1], 1)
                    if t == 8 and has_s:
                        pe.wait_ge(cn_r[1], sq + 1)
                        project(PC, cn_h, cn_l, "o1", KT, lo_ready=(cn_lo[1], sq + 1)).then_inc(pj["o1"], 1)
                    if t == 9 and has_n:
                        pe.wait_ge(rot["q1"], nx + 1)
                        if has_s:
                            pe.wait_ge(riT_r[1], sq + 1)
                        transpose4(TC, columns(RA["q1"])).then_inc(rT_d["q1"], 1)
                    if t == 11 and has_n:
                        pe.wait_ge(rot["k1"], nx + 1)
                        pe.wait_ge(rT_r["q1"], nx + 1)
                        transpose4(TC, columns(RA["k1"])).then_inc(rT_d["k1"], 1)
                    if t == K2T and has_s:
                        if has_n:
                            pe.wait_ge(v1_r, nx + 1)
                        elif has_c:
                            pe.wait_ge(ab["q2"], cq + 1)
                        project(PA, cxT_h, cxT_l, "kv2", CKT, slice(0, D)).then_inc(pj["k2"], 1)
                    if t == V2T and has_s:
                        pe.wait_ge(x1_r, sq + 1)
                        project(PC, cxT_h, cxT_l, "kv2", CKT, slice(D, 2 * D)).then_inc(pj["v2"], 1)
                    if t == Z2T and has_s:
                        pe.wait_ge(z_r[2], sq + 1)
                        if has_n:
                            pe.wait_ge(rT_r["k1"], nx + 1)
                        transpose4(TC, columns(z2)).then_inc(zT_d[2], 1)
                    if 0 <= t - LT < len(order):
                        u = t - LT
                        pe.wait_ge(p_r, n0 + u + 1)
                        if u >= 2:
                            pe.wait_ge((pTe_r, pTo_r)[u % 2], par + u // 2)
                        elif u == 0 and has_n:
                            pe.wait_ge(zT_lo[1], nx + 1)
                        elif has_c:
                            pe.wait_ge(rT_r["q2"], cq + 1)
                        transpose4(TP[u % 2], lambda j, s=(s0 + u) % NP: prob[:, s, j, :]).then_inc(pT_d, 1)
                    if 0 <= t - LA < len(order):
                        u = t - LA
                        kind, c = order[u]
                        pe.wait_ge((pTe_r, pTo_r)[u % 2], par + u // 2 + 1)
                        if kind == 1 and c == 0:
                            pe.wait_ge(v1_r, sq + 1)
                            wait(pe, v2_r, sq)
                        if kind == 2 and c == 0:
                            pe.wait_ge(v2_r, cq + 1)
                            if has_n:
                                pe.wait_ge(ab["k1"], nx + 1)
                            elif has_o:
                                pe.wait_ge(x2_r, oq + 1)
                        attend(kind, c, (s0 + u) % NP)

            def transpose_rinv2(oq, par):
                pe.wait_ge(rb_r[2], oq + 1)
                pe.wait_ge(pTo_r, par)
                transpose4(TB, columns(rbc2[:, :, :].rearrange("p h d -> p (h d)"))).then_inc(ri_d[2], 1)

            def project_q2(cq):
                pe.wait_ge(zT_hi[2], cq + 1)
                pe.wait_ge(ab["k2"], cq + 1)
                project(PA, z2T_h, z2T_l, "q2", KT, lo_ready=(zT_lo[2], cq + 1)).then_inc(pj["q2"], 1)

            def transpose_q2_k2(cq, par, has_o):
                pe.wait_ge(rot["q2"], cq + 1)
                if has_o:
                    pe.wait_ge(riT_r[2], cq)
                else:
                    wait(pe, pTo_r, par)
                transpose4(TB, columns(RA["q2"])).then_inc(rT_d["q2"], 1)
                pe.wait_ge(rot["k2"], cq + 1)
                pe.wait_ge(zT_lo[2], cq + 1)
                transpose4(TC, columns(RA["k2"])).then_inc(rT_d["k2"], 1)

            pe.wait_ge(c_ready, 3)
            pe.wait_ge(w_lo, len(WSRC))
            schedule(turn, pe.Fori)

        @block.scalar
        def _(act):
            act.wait_ge(tab, 1)
            nc.scalar.activation(ang_s[:, :], ang_s[:, :], ACT.Sin).then_inc(tab_act, 1)
            nc.scalar.activation(ang_c[:, :], ang_c[:, :], ACT.Sin).then_inc(tab_act, 1)
            for n, (name, src, k, m) in enumerate(WSRC):
                act.wait_ge(wstage_in[n % 2], 16 * (n // 2 + 1))
                nc.scalar.activation(WHI[name][:, :, :], stage(n, k, m), ACT.Copy).then_inc(w_hi, 1)
            act.wait_ge(c_ready, 3)

            def flat(t):
                return t[:, :, :].rearrange("p k t -> p (k t)")

            def copy_rinv2(oq):
                act.wait_ge(ri_d[2], oq + 1)
                nc.scalar.activation(rT2[:, :], TB[:, :], ACT.Copy).then_inc(riT_r[2], 1)

            def turn(sq, cq, nx, nz, oq):
                order = chunks(sq, cq)
                n0, s0 = first_chunk(cq, oq), slots(cq)
                has_s, has_c, has_n, has_o = sq is not None, cq is not None, nx is not None, oq is not None
                if has_o and not has_s:
                    copy_rinv2(oq)
                if has_n:
                    act.wait_ge(zT_d[1], nx + 1)
                    wait(act, pj["v1"], nx)
                    nc.scalar.activation(flat(z1T_h), TA[:, :], ACT.Copy).then_inc(zT_hi[1], 1)
                for t in range(STEPS):
                    if t == (QA if has_s else 0) and has_c:
                        act.wait_ge(rT_d["q2"], cq + 1)
                        nc.scalar.activation(flat(qT2), TB[:, :], ACT.Copy).then_inc(rT_r["q2"], 1)
                    if t < len(order):
                        s = (s0 + t) % NP
                        kind, c = order[t]
                        rs = (rsum1, rsum2)[kind - 1]
                        act.wait_ge(nmax_r, n0 + t + 1)
                        if c == 0:
                            wait(act, ri_r[kind], (sq, cq)[kind - 1])
                        wait(act, pT_d, n0 + t - NP + 1)
                        for j in range(G):
                            last = nc.scalar.activation(prob[:, s, j, :], SC[t % 2][:, j * P:(j + 1) * P], ACT.Exp,
                                                        bias=nmax[:, s, j:j + 1],
                                                        accum_out=rs[:, head(kind, c, j):head(kind, c, j) + 1])
                        last.then_inc(p_r, 1)
                    if t == 0 and has_o and has_s:
                        copy_rinv2(oq)
                    u = t - LT
                    if 0 <= u < len(order) and u % 2 == 1:
                        act.wait_ge(pT_d, n0 + u + 1)
                        wait(act, av_d, n0 + u - NP + 1)
                        nc.scalar.activation(probT[:, (s0 + u) % NP, :, :].rearrange("p g t -> p (g t)"),
                                             TP[1][:, :], ACT.Copy).then_inc(pTo_r, 1)
                    if t == CXA and has_s:
                        act.wait_ge(cxT_d, sq + 1)
                        nc.scalar.activation(flat(cxT_h), TC[:, 0:CD], ACT.Copy).then_inc(cxT_hi, 1)
                    if t == 6 and has_s:
                        act.wait_ge(ri_d[1], sq + 1)
                        nc.scalar.activation(rT1[:, :], TC[:, :], ACT.Copy).then_inc(riT_r[1], 1)
                    if t == 9 and has_n:
                        act.wait_ge(rT_d["q1"], nx + 1)
                        nc.scalar.activation(flat(qT1), TC[:, :], ACT.Copy).then_inc(rT_r["q1"], 1)
                    if t == V1A and has_n:
                        act.wait_ge(pj["v1"], nx + 1)
                        if has_s:
                            act.wait_ge(av_d, n0 + NS)
                        nc.scalar.activation(v1[:, :], PA[:, :], ACT.Copy).then_inc(v1_r, 1)
                    if t == Z2T and has_s:
                        act.wait_ge(zT_d[2], sq + 1)
                        nc.scalar.activation(flat(z2T_h), TC[:, :], ACT.Copy).then_inc(zT_hi[2], 1)
                if has_s:
                    act.wait_ge(pj["v2"], sq + 1)
                    act.wait_ge(av_d, n0 + len(order))
                    v2p = PC[:, :].rearrange("p (g a d) -> p g a d", a=2, d=DK2)
                    nc.scalar.activation(v2e[:, :, 0, :], v2p[:, :, 0, :], ACT.Copy)
                    nc.scalar.activation(v2o[:, :, 1, :], v2p[:, :, 1, :], ACT.Copy).then_inc(v2_r, 1)

            schedule(turn, act.Fori)

        @block.vector
        def _(dve):
            small = {"n": 0, "base": 0}

            def link(ins):
                small["n"] += 1
                ins.then_inc(dstep, 1)
                dve.wait_ge(dstep, small["base"] + small["n"])

            pos_t = pos_sb[:, :].rearrange("p (b c) -> p b c", c=2)
            full_s = ang_s[:, :].rearrange("p (b c i) -> p b c i", b=B, c=2)
            turns = turns_sb[:, :]
            dve.wait_ge(pos_in, 16)
            for i in range(HALF):
                last = nc.vector.tensor_scalar(full_s[:, :, :, i], pos_t, float(np.float32(10000.0 ** (-i / HALF))), None, ALU.mult)
            link(last)
            link(nc.vector.tensor_scalar(turns, ang_s[:, :], 1.0 / TWO_PI, MAGIC, ALU.mult, ALU.add))
            link(nc.vector.tensor_scalar(turns, turns, MAGIC, None, ALU.subtract))
            for part in (PI_A, PI_B, PI_C):
                link(nc.vector.scalar_tensor_tensor(out=ang_s[:, :], in0=turns, scalar=-part, in1=ang_s[:, :],
                                                    op0=ALU.mult, op1=ALU.add))
            link(nc.vector.tensor_scalar(ang_s[:, :], ang_s[:, :], math.pi - 1e-6, -(math.pi - 1e-6), ALU.min, ALU.max))
            link(nc.vector.scalar_tensor_tensor(out=ang_c[:, :], in0=ang_s[:, :], scalar=-1.0, in1=ang_s[:, :],
                                                op0=ALU.mult, op1=ALU.max))
            nc.vector.tensor_scalar(ang_c[:, :], ang_c[:, :], -1.0, math.pi / 2, ALU.mult, ALU.add).then_inc(tab, 1)
            dve.wait_ge(tab_act, 2)
            flat_s = ang_s[:, :].rearrange("p (b j) -> p b j", b=B)
            flat_c = ang_c[:, :].rearrange("p (b j) -> p b j", b=B)
            c2 = cos2[:, :, :].rearrange("p b (j e) -> p b j e", e=2)
            s2 = sin2[:, :, :].rearrange("p b (j e) -> p b j e", e=2)
            nc.vector.tensor_copy(c2[:, :, :, 0], flat_c)
            nc.vector.tensor_copy(c2[:, :, :, 1], flat_c)
            nc.vector.tensor_scalar(s2[:, :, :, 0], flat_s, -1.0, None, ALU.mult)
            link(nc.vector.tensor_copy(s2[:, :, :, 1], flat_s))
            for n, (name, src, k, m) in enumerate(WSRC):
                dve.wait_ge(w_hi, n + 1)
                nc.vector.tensor_tensor(WLO[name][:, :, :], stage(n, k, m), WHI[name][:, :, :], ALU.subtract).then_inc(w_lo, 1)
            dve.wait_ge(c_in, 32)

            def flat(t):
                return t[:, :, :].rearrange("p k t -> p (k t)")

            def statistics(n, tile, q):
                link(nc.vector.bn_stats(st[n][:, :], tile[:, :]))
                dve.sem_inc(aggr, 1)
                nc.vector.bn_aggr(mv[n][:, :], st[n][:, :]).then_inc(mv_r[n], 1)
                dve.wait_ge(mv_r[n], q + 1)
                nc.vector.tensor_scalar(ve[n][:, :], mv[n][:, 1:2], EPS, None, ALU.add).then_inc(ve_r[n], 1)

            def normalise(n, tile, z, q):
                t = nt[n]
                dve.wait_ge(rs_r[n], q + 1)
                link(nc.vector.scalar_tensor_tensor(out=t[:, 1:2], in0=r0[n][:, :], scalar=ve[n][:, :], in1=r0[n][:, :],
                                                    op0=ALU.mult, op1=ALU.mult))
                link(nc.vector.tensor_scalar(t[:, 2:3], t[:, 1:2], -0.5, 1.5, ALU.mult, ALU.add))
                link(nc.vector.tensor_tensor(t[:, 3:4], t[:, 2:3], r0[n][:, :], ALU.mult))
                wait(dve, zT_d[n], q)
                nc.vector.tensor_scalar(z[:, :], tile[:, :], mv[n][:, 0:1], t[:, 3:4], ALU.subtract, ALU.mult)\
                    .then_inc(z_r[n], 1)

            def rope(n, q, src, w, cos, sin, scale):
                h = D // w
                dve.wait_ge(pj[n], q + 1)
                wait(dve, rT_d[n], q)
                nc.vector.scalar_tensor_tensor(
                    out=RA[n][:, :].rearrange("p (h j) -> p h j", j=w), in0=src[:, :].rearrange("p (h j) -> p h j", j=w),
                    scalar=scale, in1=cos.to_broadcast([P, h, w]), op0=ALU.mult, op1=ALU.mult)
                for e in range(2):
                    last = nc.vector.scalar_tensor_tensor(
                        out=RB[n][:, :].rearrange("p (h j e) -> p h j e", j=w // 2, e=2)[:, :, :, e],
                        in0=src[:, :].rearrange("p (h j e) -> p h j e", j=w // 2, e=2)[:, :, :, 1 - e], scalar=scale,
                        in1=sin.rearrange("p o (j e) -> p o j e", e=2)[:, :, :, e].to_broadcast([P, h, w // 2]),
                        op0=ALU.mult, op1=ALU.mult)
                last.then_inc(ab[n], 1)

            cos1, sin1 = cst[:, 0:DK1].unsqueeze(1), cst[:, DK1:2 * DK1].unsqueeze(1)
            even, odd = cst[:, 2 * DK1:2 * DK1 + 1], cst[:, 2 * DK1 + 1:2 * DK1 + 2]

            def normalise_ctx(n, src, r):
                nc.vector.tensor_tensor(flat(cn_h), src[:, :], r[:, :], ALU.mult).then_inc(cn_hi[n], 1)
                nc.vector.tensor_tensor(flat(cn), src[:, :], r[:, :], ALU.mult).then_inc(cn_r[n], 1)

            def cross_out(oq, n0):
                dve.wait_ge(riT_r[2], oq + 1)
                dve.wait_ge(av_d, n0)
                normalise_ctx(2, PB, rT2)

            def low(dst, src, hi, s):
                nc.vector.tensor_tensor(flat(dst), src, flat(hi), ALU.subtract).then_inc(s, 1)

            def turn(sq, cq, nx, nz, oq):
                order = chunks(sq, cq)
                n0, s0 = first_chunk(cq, oq), slots(cq)
                has_s, has_c, has_n, has_o = sq is not None, cq is not None, nx is not None, oq is not None
                in_loop = has_c and not isinstance(cq, int)
                if in_loop:
                    small["base"], small["n"] = small["n"] - 2 * LOOP_STEPS + LOOP_STEPS * cq, 0
                if has_n:
                    dve.wait_ge(zT_hi[1], nx + 1)
                    low(z1T_l, TA[:, :], z1T_h, zT_lo[1])
                if has_o and not has_s:
                    cross_out(oq, n0)
                if has_c and not has_s:
                    rope("q2", cq, PA, DK2, cos2[:, bass.ds(cq, 1), :], sin2[:, bass.ds(cq, 1), :], DK2 ** -0.5)
                for t in range(STEPS):
                    if t == (3 if has_s else 0) and has_c:
                        dve.wait_ge(rT_d["k2"], cq + 1)
                        nc.vector.tensor_scalar(flat(kT2e), TC[:, :], even, None, ALU.mult)
                        nc.vector.tensor_scalar(flat(kT2o), TC[:, :], odd, None, ALU.mult).then_inc(rT_r["k2"], 1)
                    if t < len(order):
                        s = (s0 + t) % NP
                        dve.wait_ge(s_done, n0 + t + 1)
                        wait(dve, p_r, n0 + t - NP + 1)
                        nc.vector.tensor_reduce(out=nmax[:, s, :], in_=SC[t % 2][:, :].rearrange("p (g k) -> p g k", g=G),
                                                op=ALU.max, axis=AX, negate=True).then_inc(nmax_r, 1)
                    u = t - LT
                    if 0 <= u < len(order) and u % 2 == 0:
                        dve.wait_ge(pT_d, n0 + u + 1)
                        wait(dve, av_d, n0 + u - NP + 1)
                        nc.vector.tensor_copy(probT[:, (s0 + u) % NP, :, :].rearrange("p g t -> p (g t)"),
                                              TP[0][:, :]).then_inc(pTe_r, 1)
                    if t == 0 and has_o and has_s:
                        cross_out(oq, n0)
                    if t == 0 and has_c and has_s:
                        rope("q2", cq, PA, DK2, cos2[:, bass.ds(cq, 1), :], sin2[:, bass.ds(cq, 1), :], DK2 ** -0.5)
                    if t == O2T and has_o:
                        dve.wait_ge(pj["o2"], oq + 1)
                        dve.wait_ge(x1b_r, oq + 1)
                        wait(dve, x2_out, 16 * oq)
                        nc.vector.tensor_tensor(x2[:, :], PB[:, :], x1B[:, :], ALU.add).then_inc(x2_r, 1)
                    if t == 3 and has_n:
                        rope("q1", nx, PA, DK1, cos1, sin1, DK1 ** -0.5)
                    if t == 4 and has_s:
                        dve.wait_ge(p_r, n0 + NS)
                        wait(dve, rb_r[1], sq)
                        nc.vector.reciprocal(rinv1[:, :], rsum1[:, :]).then_inc(ri_r[1], 1)
                    if t == 4 and has_n:
                        rope("k1", nx, PB, DK1, cos1, sin1, 1.0)
                    if t == CXA and has_s:
                        dve.wait_ge(cxT_hi, sq + 1)
                        low(cxT_l, TC[:, 0:CD], cxT_h, cxT_lo)
                    if t == 5 and nz is not None:
                        dve.wait_ge(x_in, 16 * (nz + 1))
                        statistics(1, xA, nz)
                    if t == 6 and has_s:
                        dve.wait_ge(riT_r[1], sq + 1)
                        dve.wait_ge(av_d, n0 + NS)
                        normalise_ctx(1, PC, rT1)
                    if t == 7 and nz is not None:
                        normalise(1, xA, z1, nz)
                    if t == 8 and has_s:
                        dve.wait_ge(pj["o1"], sq + 1)
                        dve.wait_ge(xb_in, 16 * (sq + 1))
                        wait(dve, x1b_r, sq)
                        nc.vector.tensor_tensor(x1A[:, :], PC[:, :], xB[:, :], ALU.add).then_inc(x1_r, 1)
                        dve.wait_ge(x1_r, sq + 1)
                        statistics(2, x1A, sq)
                    if t == NZ2 and has_s:
                        normalise(2, x1A, z2, sq)
                    if t == K2R and has_s:
                        rope("k2", sq, PA, DK2, cos2[:, bass.ds(sq, 1), :], sin2[:, bass.ds(sq, 1), :], 1.0)
                    if t == 11 and has_n:
                        dve.wait_ge(rT_d["k1"], nx + 1)
                        nc.vector.tensor_copy(flat(kT1), TC[:, :]).then_inc(rT_r["k1"], 1)
                    if t == Z2T and has_s:
                        dve.wait_ge(zT_hi[2], sq + 1)
                        low(z2T_l, TC[:, :], z2T_h, zT_lo[2])
                    if t == STEPS - LA and has_c:
                        dve.wait_ge(p_r, n0 + len(order))
                        wait(dve, rb_r[2], cq)
                        nc.vector.reciprocal(rinv2[:, :], rsum2[:, :]).then_inc(ri_r[2], 1)
                if in_loop:
                    assert small["n"] == LOOP_STEPS
                    small["base"], small["n"] = 0, before["n"] + LOOP_STEPS * (B - 5)

            LOOP_STEPS = 8
            dve.wait_ge(x_in, 16)
            statistics(1, xA, 0)
            normalise(1, xA, z1, 0)
            before = {"n": 0}

            @contextmanager
            def turns_of(a, b):
                before["n"] = small["n"]
                with dve.Fori(a, b) as c:
                    yield c

            schedule(turn, turns_of)


def ffn_phase(nc, fp32, fp32r, i32, ALU, ACT, AX, AXY, x2_dram, wg, sg, wu, su, wd, sd, out):
    es = ExitStack()
    with es:
        def sb(name, shape, dt=fp32):
            return es.enter_context(nc.sbuf_tensor(name, shape, dt))

        def sem(name):
            return es.enter_context(nc.semaphore(name))

        T = TPB * P
        wg_h, wg_l = sb("wg_h", [P, KT, HID], fp32r), sb("wg_l", [P, KT, HID], fp32r)
        wu_h, wu_l = sb("wu_h", [P, KT, HID], fp32r), sb("wu_l", [P, KT, HID], fp32r)
        wd_h, wd_l = sb("wd_h", [P, HT, D], fp32r), sb("wd_l", [P, HT, D], fp32r)
        stages = [sb(f"wstage{n}", [P, 2 * D], i32) for n in range(2)]
        sg_c, su_c, sd_b = sb("sg_c", [P, HT]), sb("su_c", [P, HT]), sb("sd_b", [P, D])
        mhalf, ident = sb("mhalf", [P, TPB]), sb("ident_f", [P, P])
        xn = sb("xn", [P, TPB, D])
        xr = sb("xr", [P, TPB, D])
        zT_h, zT_l = sb("zT_h", [P, KT, T], fp32r), sb("zT_l", [P, KT, T], fp32r)
        sil = [sb(f"sil{n}", [P, T]) for n in range(2)]
        h = [sb(f"h{n}", [P, T]) for n in range(2)]
        h_h = [sb(f"h_h{n}", [P, T], fp32r) for n in range(2)]
        h_l = [sb(f"h_l{n}", [P, T], fp32r) for n in range(2)]
        ys = [sb(f"ys{n}", [P, D]) for n in range(2)]
        st, mv = sb("st", [P, TPB, 6]), sb("mv", [P, TPB, 2])
        ve, r0, nt = sb("ve", [P, TPB]), sb("r0", [P, TPB]), sb("nt", [P, 4, TPB])
        low_piece, low_part = sb("low_piece", [P, 3 * ((HT + 1) // 2)]), sb("low_part", [P, 1])
        low_row, low_max, low_flag = sb("low_row", [1, P]), sb("low_max", [1, 1]), sb("low_flag", [1, 1], i32)

        bank = [es.enter_context(nc.psum_tensor(f"fbank{n}", [P, 512], fp32)) for n in range(8)]
        DN = bank[0:TPB]
        GT = [bank[4], bank[6]]
        UP = [bank[5], bank[7]]
        TZ = [bank[6], bank[7], bank[4], bank[5]]

        w_in = [sem("fw_loaded0"), sem("fw_loaded1")]
        w_hi, w_lo = sem("fw_hi_ready"), sem("fw_lo_ready")
        cin, czero, cready = sem("f_scales_loaded"), sem("f_const_zeroed"), sem("f_ident_ready")
        xn_in, xr_in, stored = sem("xn_loaded"), sem("xr_loaded"), sem("out_stored")
        mv_r, ve_r, rs_r, z_r = sem("f_mean_var_ready"), sem("f_var_eps_ready"), sem("f_rough_rstd_ready"), sem("f_z_ready")
        zT_d, zT_hr, zT_lr = sem("f_zT_done"), sem("f_zT_hi_ready"), sem("f_zT_lo_ready")
        g_d, u_d, dn_d = sem("gate_done"), sem("up_done"), sem("down_done")
        sil_r, h_r, hh_r, hl_r = sem("silu_ready"), sem("h_ready"), sem("h_hi_ready"), sem("h_lo_ready")
        ys_r, y_r = sem("scaled_down_ready"), sem("out_ready")
        rstd_r = sem("f_rstd_ready")
        dstep, aggr = sem("f_vector_small_step"), sem("f_vector_aggregates")
        low_p, low_c, low_in = sem("low_pieces_reduced"), sem("low_partitions_reduced"), sem("low_row_loaded")
        low_m, flag_r = sem("low_max_ready"), sem("low_flag_ready")

        block = es.enter_context(nc.Block())

        def wait(eng, s, value):
            if not isinstance(value, int) or value > 0:
                eng.wait_ge(s, value)

        pieces = []
        for j in range(0, HT, 2):
            m = min(2, HT - j)
            pieces += [("g", j, m), ("u", j, m), ("d", j, m)]

        def parts(n):
            kind, j, m = pieces[n]
            if kind == "d":
                src = wd[j * P:(j + m) * P, :].rearrange("(k p) n -> p k n", p=P)
                s = stages[n % 2][:, 0:m * D].rearrange("p (k n) -> p k n", n=D)
                return src, s, wd_h[:, j:j + m, :], wd_l[:, j:j + m, :]
            w, hi, lo = (wg, wg_h, wg_l) if kind == "g" else (wu, wu_h, wu_l)
            cols = slice(j * P, (j + m) * P)
            s = stages[n % 2][:, 0:KT * m * P].rearrange("p (k n) -> p k n", k=KT)
            return w[:, cols].rearrange("(k p) n -> p k n", p=P), s, hi[:, :, cols], lo[:, :, cols]

        def pieces_at(j):
            return range(3 * (j // 2 + 1), min(3 * (j // 2 + 2), len(pieces))) if j % 2 == 0 else ()

        def seqs(ap, nb):
            first = nb * TPB
            return ap[bass.ds(first, TPB), :, :].rearrange("s p d -> p s d")

        def schedule(program, fori):
            program(0, 1, True)
            with fori(1, NBLK - 1) as nb:
                program(nb, nb + 1, False)
            program(NBLK - 1, None, False)

        @block.sync
        def _(sp):
            sp.dma_start(xn[:, :, :], seqs(x2_dram, 0)).then_inc(xn_in, 16)
            sp.dma_start(sg_c[:, :], sg).then_inc(cin, 16)
            sp.dma_start(su_c[:, :], su).then_inc(cin, 16)
            sp.dma_start(sd_b[:, :], sd.partition_broadcast(P)).then_inc(cin, 16)

            def load_pieces(a, b):
                for n in range(a, b):
                    src, s, _, _ = parts(n)
                    if n >= 2:
                        sp.wait_ge(w_lo, n - 1)
                    sp.dma_start(s, src).then_inc(w_in[n % 2], 16)

            load_pieces(0, 6)

            def program(nb, nx, first):
                wait(sp, stored, 16 * nb)
                sp.dma_start(xr[:, :, :], seqs(x2_dram, nb)).then_inc(xr_in, 16)
                if nx is not None:
                    sp.wait_ge(zT_d, KT * nx)
                    sp.dma_start(xn[:, :, :], seqs(x2_dram, nx)).then_inc(xn_in, 16)
                if first:
                    load_pieces(6, len(pieces))
                    sp.wait_ge(low_c, 1)
                    sp.dma_start(low_row[:, :], low_part[:, :]).then_inc(low_in, 16)
                sp.wait_ge(y_r, TPB * (nb + 1))
                sp.dma_start(seqs(out, nb), xr[:, :, :]).then_inc(stored, 16)

            schedule(program, sp.Fori)
            sp.wait_ge(stored, 16 * NBLK)

        @block.gpsimd
        def _(pool):
            pool.memset(ident[:, :], 0.0).then_inc(czero, 1)
            pool.memset(mhalf[:, :], -0.5).then_inc(czero, 1)
            pool.wait_ge(czero, 2)
            pool.affine_select(out=ident[:, :], in_=ident[:, :], compare_op=ALU.not_equal, fill=1.0,
                               base=0, pattern=[[-1, P]], channel_multiplier=1).then_inc(cready, 1)

            def rough_rstd(q):
                pool.wait_ge(ve_r, q + 1)
                pool.tensor_tensor(r0[:, :], ve[:, :], mhalf[:, :], ALU.pow).then_inc(rs_r, 1)

            rough_rstd(0)

            def program(nb, nx, first):
                if nx is not None:
                    rough_rstd(nx)
                pool.wait_ge(xr_in, 16 * (nb + 1))
                for s in range(TPB):
                    pool.wait_ge(ys_r, TPB * nb + s + 1)
                    pool.tensor_tensor(xr[:, s, :], xr[:, s, :], ys[s % 2][:, :], ALU.add).then_inc(y_r, 1)

            schedule(program, pool.Fori)

        @block.tensor
        def _(pe):
            def hidden(dst, wh, wl, j, nb, low):
                cols = slice(j * P, (j + 1) * P)
                passes = ((wh, zT_h), (wl, zT_h), (wh, zT_l)) if low else ((wh, zT_h), (wh, zT_l))
                n = 0
                for w, z in passes:
                    if z is zT_l and j == 0:
                        pe.wait_ge(zT_lr, KT * (nb + 1))
                    for k in range(KT):
                        last = nc.tensor.matmul(dst[:, :], w[:, k, cols], z[:, k, :], start=(n == 0),
                                                stop=(n == len(passes) * KT - 1))
                        n += 1
                return last

            def down(j, nb, low):
                passes = ((h_h, wd_h), (h_h, wd_l), (h_l, wd_h)) if low else ((h_h, wd_h), (h_l, wd_h))
                pe.wait_ge(hh_r, HT * nb + j + 1)
                pe.wait_ge(hl_r, HT * nb + j + 1)
                if j == 0:
                    wait(pe, ys_r, TPB * nb)
                for s in range(TPB):
                    tok = slice(s * P, (s + 1) * P)
                    for n, (a, w) in enumerate(passes):
                        last = nc.tensor.matmul(DN[s][:, :], a[j % 2][:, tok], w[:, j, :], start=(j == 0 and n == 0),
                                                stop=(j == HT - 1 and n == len(passes) - 1))
                last.then_inc(dn_d, 1)

            def transpose_tile(k, nx):
                for s in range(TPB):
                    last = nc.tensor.transpose(TZ[k][:, s * P:(s + 1) * P], xn[:, s, k * P:(k + 1) * P], ident[:, :])
                last.then_inc(zT_d, 1)

            def program(nb, nx, first, low):
                pe.wait_ge(zT_hr, KT * (nb + 1))
                for j in range(HT):
                    if j == 0:
                        pe.wait_ge(zT_lr, KT * nb + 3)
                    elif j == 1:
                        pe.wait_ge(zT_lr, KT * nb + 2)
                    else:
                        pe.wait_ge(sil_r, HT * nb + j - 1)
                    if first:
                        pe.wait_ge(w_lo, min(3 * (j // 2) + 1, len(pieces)))
                    hidden(GT[j % 2], wg_h, wg_l, j, nb, low).then_inc(g_d, 1)
                    if j >= 2:
                        pe.wait_ge(h_r, HT * nb + j - 1)
                    elif j == 0:
                        pe.wait_ge(zT_lr, KT * nb + 4)
                    if first:
                        pe.wait_ge(w_lo, min(3 * (j // 2) + 2, len(pieces)))
                    hidden(UP[j % 2], wu_h, wu_l, j, nb, low).then_inc(u_d, 1)
                    if nx is not None and j == HT - 1:
                        pe.wait_ge(z_r, nx + 1)
                        pe.wait_ge(sil_r, HT * nb + HT - 1)
                        pe.wait_ge(h_r, HT * nb + HT - 1)
                        transpose_tile(0, nx)
                        transpose_tile(1, nx)
                    if j >= 1:
                        if first:
                            pe.wait_ge(w_lo, min(3 * ((j - 1) // 2) + 3, len(pieces)))
                        down(j - 1, nb, low)
                if nx is not None:
                    pe.wait_ge(sil_r, HT * (nb + 1))
                    pe.wait_ge(h_r, HT * (nb + 1))
                    transpose_tile(2, nx)
                    transpose_tile(3, nx)
                if first:
                    pe.wait_ge(w_lo, len(pieces))
                down(HT - 1, nb, low)

            pe.wait_ge(cready, 1)
            pe.wait_ge(z_r, 1)
            for k in range(KT):
                transpose_tile(k, 0)
            program(0, 1, True, True)
            pe.wait_ge(flag_r, 1)
            some_low = pe.value_load(low_flag[0:1, 0:1], min_val=0, max_val=1)
            for low in (True, False):
                with pe.If(some_low == 1 if low else some_low == 0):
                    with pe.Fori(1, NBLK - 1) as nb:
                        program(nb, nb + 1, False, low)
                    program(NBLK - 1, None, False, low)

        @block.scalar
        def _(act):
            def split_hi(n):
                _, s, hi, _ = parts(n)
                act.wait_ge(w_in[n % 2], 16 * (n // 2 + 1))
                nc.scalar.activation(hi, s, ACT.Copy, bias=-ZERO_POINT).then_inc(w_hi, 1)

            def zT_high(k, q):
                act.wait_ge(zT_d, KT * q + k + 1)
                nc.scalar.activation(zT_h[:, k, :], TZ[k][:, :], ACT.Copy).then_inc(zT_hr, 1)

            def program(nb, nx, first):
                for j in range(HT):
                    if first:
                        for n in pieces_at(j):
                            split_hi(n)
                    act.wait_ge(g_d, HT * nb + j + 1)
                    if j >= 2:
                        act.wait_ge(h_r, HT * nb + j - 1)
                    nc.scalar.activation(sil[j % 2][:, :], GT[j % 2][:, :], ACT.Silu, scale=sg_c[:, j:j + 1]).then_inc(sil_r, 1)
                    act.wait_ge(h_r, HT * nb + j + 1)
                    if j >= 2:
                        act.wait_ge(dn_d, HT * nb + j - 1)
                    else:
                        wait(act, dn_d, HT * nb)
                    nc.scalar.activation(h_h[j % 2][:, :], h[j % 2][:, :], ACT.Copy).then_inc(hh_r, 1)
                if nx is not None:
                    for k in range(KT):
                        zT_high(k, nx)

            for n in range(3):
                split_hi(n)
            for k in range(KT):
                zT_high(k, 0)
            act.wait_ge(cin, 48)
            schedule(program, act.Fori)

        @block.vector
        def _(dve):
            def split_lo(n):
                _, s, hi, lo = parts(n)
                dve.wait_ge(w_hi, n + 1)
                nc.vector.scalar_tensor_tensor(out=lo, in0=s, scalar=ZERO_POINT, in1=hi,
                                               op0=ALU.subtract, op1=ALU.subtract).then_inc(w_lo, 1)

            def largest_low():
                dve.wait_ge(low_p, len(pieces))
                nc.vector.tensor_reduce(low_part[:, :], low_piece[:, :], axis=AX, op=ALU.max).then_inc(low_c, 1)

            def low_to_flag():
                dve.wait_ge(low_in, 16)
                nc.vector.tensor_reduce(low_max[:, :], low_row[:, :], axis=AX, op=ALU.max).then_inc(low_m, 1)
                dve.wait_ge(low_m, 1)
                nc.vector.tensor_scalar(low_flag[:, :], low_max[:, :], 0.0, None, ALU.is_gt).then_inc(flag_r, 1)

            def low_size(n):
                _, _, _, lo = parts(n)
                dve.wait_ge(w_lo, n + 1)
                nc.vector.tensor_reduce(low_piece[:, n:n + 1], lo, axis=AXY, op=ALU.max,
                                        apply_absolute_value=True).then_inc(low_p, 1)

            NSTEP = 4

            def statistics(q):
                dve.wait_ge(xn_in, 16 * (q + 1))
                for s in range(TPB):
                    last = nc.vector.bn_stats(st[:, s, :], xn[:, s, :])
                last.then_inc(dstep, 1)
                dve.wait_ge(dstep, NSTEP * q + 1)
                dve.sem_inc(aggr, 1)
                for s in range(TPB):
                    last = nc.vector.bn_aggr(mv[:, s, :], st[:, s, :])
                last.then_inc(mv_r, 1)
                dve.wait_ge(mv_r, q + 1)
                nc.vector.tensor_scalar(ve[:, :], mv[:, :, 1], EPS, None, ALU.add).then_inc(ve_r, 1)

            def normalise(q):
                dve.wait_ge(rs_r, q + 1)
                nc.vector.tensor_tensor(nt[:, 0, :], ve[:, :], r0[:, :], ALU.mult).then_inc(dstep, 1)
                dve.wait_ge(dstep, NSTEP * q + 2)
                nc.vector.tensor_tensor(nt[:, 1, :], nt[:, 0, :], r0[:, :], ALU.mult).then_inc(dstep, 1)
                dve.wait_ge(dstep, NSTEP * q + 3)
                nc.vector.tensor_scalar(nt[:, 2, :], nt[:, 1, :], -0.5, 1.5, ALU.mult, ALU.add).then_inc(dstep, 1)
                dve.wait_ge(dstep, NSTEP * q + 4)
                nc.vector.tensor_tensor(nt[:, 3, :], nt[:, 2, :], r0[:, :], ALU.mult).then_inc(rstd_r, 1)
                dve.wait_ge(rstd_r, q + 1)
                for s in range(TPB):
                    last = nc.vector.tensor_scalar(xn[:, s, :], xn[:, s, :], mv[:, s, 0:1], nt[:, 3, s:s + 1],
                                                   ALU.subtract, ALU.mult)
                last.then_inc(z_r, 1)

            def zT_low(k, q):
                dve.wait_ge(zT_hr, KT * q + k + 1)
                nc.vector.tensor_tensor(zT_l[:, k, :], TZ[k][:, :], zT_h[:, k, :], ALU.subtract).then_inc(zT_lr, 1)

            def program(nb, nx, first):
                for j in range(HT):
                    if first:
                        for n in pieces_at(j):
                            split_lo(n)
                    dve.wait_ge(u_d, HT * nb + j + 1)
                    dve.wait_ge(sil_r, HT * nb + j + 1)
                    if j >= 2:
                        dve.wait_ge(hh_r, HT * nb + j - 1)
                    nc.vector.scalar_tensor_tensor(out=h[j % 2][:, :], in0=UP[j % 2][:, :], scalar=su_c[:, j:j + 1],
                                                   in1=sil[j % 2][:, :], op0=ALU.mult, op1=ALU.mult).then_inc(h_r, 1)
                    dve.wait_ge(hh_r, HT * nb + j + 1)
                    nc.vector.tensor_tensor(h_l[j % 2][:, :], h[j % 2][:, :], h_h[j % 2][:, :], ALU.subtract).then_inc(hl_r, 1)
                    if first:
                        for n in [*(range(3) if j == 0 else ()), *pieces_at(j)]:
                            low_size(n)
                        if j == HT - 2:
                            largest_low()
                        if j == HT - 1:
                            low_to_flag()
                    if j == 4 and nx is not None:
                        statistics(nx)
                    if j == 6 and nx is not None:
                        normalise(nx)
                if nx is not None:
                    for k in range(KT):
                        zT_low(k, nx)
                dve.wait_ge(dn_d, HT * (nb + 1))
                for s in range(TPB):
                    if s >= 2:
                        dve.wait_ge(y_r, TPB * nb + s - 1)
                    else:
                        wait(dve, y_r, TPB * nb)
                    nc.vector.tensor_tensor(ys[s % 2][:, :], DN[s][:, :], sd_b[:, :], ALU.mult).then_inc(ys_r, 1)

            statistics(0)
            normalise(0)
            for n in range(3):
                split_lo(n)
            for k in range(KT):
                zT_low(k, 0)
            dve.wait_ge(cin, 48)
            schedule(program, dve.Fori)


def kernel(**inputs):
    import concourse.bacc as bacc
    from concourse.bass_utils import run_bass_kernel_spmd

    a = {k: np.asarray(v) for k, v in inputs.items()}

    def c(v):
        return np.ascontiguousarray(v)

    arrays = {
        "x": c(a["x"]), "ctx": c(a["ctx_1024"]), "pos": c(a["fside_BxSx2_0"].transpose(1, 0, 2).reshape(P, 2 * B)),
        "consts": shape_constants(),
        "wq1": c(a["L0_attn_Wq"].T), "wk1": c(a["L0_attn_Wk"].T), "wv1": c(a["L0_attn_Wv"].T), "wo1": c(a["L0_attn_Wo"].T),
        "wq2": c(a["L0_xattn_Wq"]), "wkv2": c(a["L0_xattn_Wkv"]), "wo2": c(a["L0_xattn_Wout"]), "bout": c(a["L0_xattn_bout"]),
        "wg": c(a["L0_ffn_wq_gate"].T), "sg": c(a["L0_ffn_s_gate"].reshape(HT, P).T),
        "wu": c(a["L0_ffn_wq_up"].T), "su": c(a["L0_ffn_s_up"].reshape(HT, P).T),
        "wd": c(a["L0_ffn_wq_down"].T), "sd": c(a["L0_ffn_s_down"]),
    }
    nc = bacc.Bacc("TRN2", target_bir_lowering=False, num_devices=1)
    t = {n: nc.dram_tensor(f"in_{n}", v.shape, mybir.dt.from_np(v.dtype), kind="ExternalInput").ap() for n, v in arrays.items()}
    out = nc.dram_tensor("out", (B, P, D), mybir.dt.float32, kind="ExternalOutput").ap()
    x2_dram = nc.dram_tensor("x2_scratch", (B, P, D), mybir.dt.float32, kind="Internal").ap()
    build_decoder(nc, t["x"], t["ctx"], t["pos"], t["consts"], t["wq1"], t["wk1"], t["wv1"], t["wo1"],
                  t["wq2"], t["wkv2"], t["wo2"], t["bout"], t["wg"], t["sg"], t["wu"], t["su"], t["wd"], t["sd"],
                  out, x2_dram)
    r = run_bass_kernel_spmd(nc, [{f"in_{n}": v for n, v in arrays.items()}], core_ids=[0])
    return r.results[0]["out"]
```

```python
import math
from contextlib import ExitStack, contextmanager

import numpy as np

import concourse.bass as bass
from concourse import mybir

P = 128
B = 32
D = 512
KT = D // P
CD = 256
CKT = CD // P
H1, DK1 = 16, 32
H2, DK2 = 32, 16
HID = 1408
HT = HID // P
G = 4
NS = H1 // G
NC = H2 // G
TPB = 4
NBLK = B // TPB
EPS = 1e-5
ZERO_POINT = 128.0
NEG = -1.0e30
THETA = 10000.0
HALF = 4
MAGIC = 12582912.0
TWO_PI = 2.0 * math.pi
PI_A = 6.28125
PI_B = float(np.float32(np.round((TWO_PI - PI_A) * 2.0 ** 20) / 2.0 ** 20))
PI_C = float(np.float32(TWO_PI - PI_A - PI_B))
NCONST = 2 * DK1 + 2


def shape_constants():
    inv = np.exp(np.float32(-math.log(THETA)) * np.arange(0, DK1, 2, dtype=np.float32) / np.float32(DK1))
    ang = np.arange(P, dtype=np.float32)[:, None] * inv.astype(np.float32)[None, :]
    cos, sin = np.cos(ang), np.sin(ang)
    c = np.zeros((P, NCONST), np.float32)
    c[:, 0:DK1:2] = cos
    c[:, 1:DK1:2] = cos
    c[:, DK1:2 * DK1:2] = -sin
    c[:, DK1 + 1:2 * DK1:2] = sin
    odd = (np.arange(P) // DK2) % 2
    c[:, 2 * DK1] = 1 - odd
    c[:, 2 * DK1 + 1] = odd
    return c


def build_decoder(nc, x, ctx_in, pos, consts, wq1, wk1, wv1, wo1, wq2, wkv2, wo2, bout,
                  wg, sg, wu, su, wd, sd, out, x2_dram):
    fp32, fp32r, i32 = mybir.dt.float32, mybir.dt.float32r, mybir.dt.int32
    ALU = mybir.AluOpType
    ACT = mybir.ActivationFunctionType
    AX = mybir.AxisListType.X

    es = ExitStack()
    with es:
        shared_f, shared = two_types(nc, es, "shared", [P, 6, KT * D], fp32, fp32r)
        ident = es.enter_context(nc.sbuf_tensor("ident", [P, P], fp32))
        mhalf = es.enter_context(nc.sbuf_tensor("mhalf", [P, TPB], fp32))
        low_flag = es.enter_context(nc.sbuf_tensor("low_flag", [1, 1], i32))
        ffn = ffn_head_layout(shared_f, shared, i32, wg, wu, wd)
        ffn["low_flag"] = low_flag
        ffn["x2_out"] = es.enter_context(nc.semaphore("x2_stored"))
        ffn["rows"] = [w.rearrange("(p a) n -> p (a n)", p=P) for w in (wg, wu, wd)]

        attention_phase(nc, fp32, fp32r, ALU, ACT, AX, x, ctx_in, pos, consts,
                        wq1, wk1, wv1, wo1, wq2, wkv2, wo2, bout, x2_dram, shared_f, shared, ident, mhalf, ffn)
        ffn_phase(nc, fp32, fp32r, i32, ALU, ACT, x2_dram, wg, sg, wu, su, wd, sd, out, ident, mhalf, ffn)


PIECES = [(kind, j, min(2, HT - j)) for j in range(0, HT, 2) for kind in "gud"]
HEAD = 3
TURNS = B - 5
STEP = HID * D // P // TURNS
WINDOW = HID * D // P - (TURNS - 1) * STEP
EXACT = 1024.0


def piece_source(n, wg, wu, wd):
    kind, j, m = PIECES[n]
    if kind == "d":
        return wd[j * P:(j + m) * P, :].rearrange("(k p) n -> p k n", p=P)
    return {"g": wg, "u": wu}[kind][:, j * P:(j + m) * P].rearrange("(k p) n -> p k n", p=P)


def piece_view(n, flat):
    kind, j, m = PIECES[n]
    return flat.rearrange("p (k n) -> p k n", k=m if kind == "d" else KT)


def two_types(nc, es, name, shape, fp32, fp32r):
    with ExitStack() as first:
        loaded = first.enter_context(nc.sbuf_tensor(f"{name}_loaded", shape, fp32))
    return loaded, es.enter_context(nc.sbuf_tensor(name, shape, fp32r))


def ffn_head_layout(shared_f, shared, i32, wg, wu, wd):
    half = KT * D // 2
    return {
        "xn": shared_f[:, 0, :].rearrange("p (s d) -> p s d", s=TPB),
        "zT_h": shared[:, 1, :].rearrange("p (k t) -> p k t", k=KT),
        "zT_l": shared[:, 2, :].rearrange("p (k t) -> p k t", k=KT),
        "hi": [piece_view(n, shared[:, 3 + n, 0:half]) for n in range(HEAD)],
        "lo": [piece_view(n, shared[:, 3 + n, half:2 * half]) for n in range(HEAD)],
        "raw": [piece_view(n, shared_f[:, 3 + n, half:2 * half].bitcast(i32)) for n in range(HEAD)],
        "source": [piece_source(n, wg, wu, wd) for n in range(HEAD)],
    }


def block_rows(ap, nb):
    first = nb * TPB
    return ap[bass.ds(first, TPB), :, :].rearrange("s p d -> p s d")


def attention_phase(nc, fp32, fp32r, ALU, ACT, AX, x, ctx_in, pos, consts,
                    wq1, wk1, wv1, wo1, wq2, wkv2, wo2, bout, x2_dram, shared_f, shared, ident, mhalf_c, ffn):
    es = ExitStack()
    with es:
        def sb(name, shape, dt=fp32):
            return es.enter_context(nc.sbuf_tensor(name, shape, dt))

        def sem(name):
            return es.enter_context(nc.semaphore(name))

        WSRC = [("q1", wq1, KT, D), ("k1", wk1, KT, D), ("v1", wv1, KT, D), ("o1", wo1, KT, D),
                ("kv2", wkv2, CKT, 2 * D), ("q2", wq2, KT, D), ("o2", wo2, KT, D)]
        WHI = {n: shared[:, 2 * i, :].rearrange("p (k m) -> p k m", k=KT) for i, (n, _, _, _) in enumerate(WSRC[:3])}
        WLO = {n: shared[:, 2 * i + 1, :].rearrange("p (k m) -> p k m", k=KT) for i, (n, _, _, _) in enumerate(WSRC[:3])}
        LOADED = {n: shared_f[:, 2 * i + 1, :].rearrange("p (k m) -> p k m", k=KT) for i, (n, _, _, _) in enumerate(WSRC[:3])}
        for n, _, k, m in WSRC[3:]:
            WHI[n] = sb(f"w_{n}_hi", [P, k, m], fp32r)
            LOADED[n], WLO[n] = two_types(nc, es, f"w_{n}_lo", [P, k, m], fp32, fp32r)

        cst = sb("cst", [P, NCONST])
        causal = sb("causal", [P, P])
        bout_b = sb("bout_b", [P, D])
        cos2 = sb("cos2", [P, B, DK2])
        sin2 = sb("sin2", [P, B, DK2])
        one_c = sb("one_c", [P, 1])

        xA, xB = sb("xA", [P, D]), sb("xB", [P, D])
        x1A, x1B, x2 = sb("x1A", [P, D]), sb("x1B", [P, D]), sb("x2", [P, D])
        z1, z2 = sb("z1", [P, D]), sb("z2", [P, D])
        z1T_h, z1T_l = sb("z1T_h", [P, KT, P], fp32r), sb("z1T_l", [P, KT, P], fp32r)
        z2T_h, z2T_l = sb("z2T_h", [P, KT, P], fp32r), sb("z2T_l", [P, KT, P], fp32r)
        cx = sb("cx", [P, CD])
        cxT_h, cxT_l = sb("cxT_h", [P, CKT, P], fp32r), sb("cxT_l", [P, CKT, P], fp32r)
        rope_buf = sb("rope_buf", [P, 8, D])
        RA = {n: rope_buf[:, j, :] for j, n in enumerate(("q1", "k1", "q2", "k2"))}
        RB = {n: rope_buf[:, 4 + j, :] for j, n in enumerate(("q1", "k1", "q2", "k2"))}
        qT1, kT1 = sb("qT1", [P, KT, P]), sb("kT1", [P, KT, P])
        qT2, kT2e, kT2o = sb("qT2", [P, KT, P]), sb("kT2e", [P, KT, P]), sb("kT2o", [P, KT, P])
        v1 = sb("v1", [P, D])
        v2e, v2o = sb("v2e", [P, H2 // 2, 2, DK2]), sb("v2o", [P, H2 // 2, 2, DK2])
        NP = 3
        prob = sb("prob", [P, NP, G, P])
        probT = sb("probT", [P, NP, G, P])
        nmax = sb("nmax", [P, NP, G])
        rsum1, rsum2 = sb("rsum1", [P, H1]), sb("rsum2", [P, H2])
        rinv1, rinv2 = sb("rinv1", [P, H1]), sb("rinv2", [P, H2])
        rbc1, rbc2 = sb("rbc1", [P, H1, DK1]), sb("rbc2", [P, H2, DK2])
        rT1, rT2 = sb("rT1", [P, D]), sb("rT2", [P, D])
        cn, cn_h, cn_l = sb("cn", [P, KT, P]), sb("cn_h", [P, KT, P], fp32r), sb("cn_l", [P, KT, P], fp32r)
        st = {n: sb(f"st{n}", [P, 6]) for n in (1, 2)}
        mv = {n: sb(f"mv{n}", [P, 2]) for n in (1, 2)}
        ve = {n: sb(f"ve{n}", [P, 1]) for n in (1, 2)}
        r0 = {n: sb(f"r0{n}", [P, 1]) for n in (1, 2)}
        nt = {n: sb(f"nt{n}", [P, 4]) for n in (1, 2)}
        fst, fmv = sb("fst", [P, TPB, 6]), sb("fmv", [P, TPB, 2])
        window = sb("range_window", [P, 3, WINDOW], mybir.dt.int32)
        rng, rng_col = sb("range_per_window", [P, TURNS]), sb("range_per_partition", [P, 1])
        rng_line, rng_max = sb("range_line", [1, P]), sb("range_max", [1, 1])
        fve, fr0, fnt = sb("fve", [P, TPB]), sb("fr0", [P, TPB]), sb("fnt", [P, 4, TPB])

        ang_s, ang_c = z2[:, 0:B * 2 * HALF], z2[:, B * 2 * HALF:2 * B * 2 * HALF]
        turns_sb, pos_sb = rT2[:, 0:B * 2 * HALF], rT2[:, B * 2 * HALF:B * 2 * HALF + 2 * B]

        def whole(name):
            return LOADED[name][:, :, :]

        bank = [es.enter_context(nc.psum_tensor(f"bank{n}", [P, 512], fp32)) for n in range(8)]
        PA, PB, PC = bank[0], bank[1], bank[6]
        SC = [bank[2], bank[3]]
        TA, TB, TC = bank[4], bank[5], bank[7]
        TP = [TA, TB]
        FZ = [SC[0], SC[1], PA, PC]

        w_in = {n: sem(f"w_{n}_loaded") for n, _, _, _ in WSRC}
        w_hi = sem("w_hi_ready")
        w_lo = {"dve": sem("w_lo_early_ready"), "pool": sem("w_lo_late_ready")}
        c_in, c_zero, c_ready = sem("const_loaded"), sem("const_zeroed"), sem("const_ready")
        pos_in, tab, tab_act = sem("pos_loaded"), sem("rotary_table"), sem("rotary_sin")
        x_in, xb_in, cx_in = sem("x_loaded"), sem("x_residual_loaded"), sem("ctx_loaded")
        mv_r = {n: sem(f"mean_var{n}_ready") for n in (1, 2)}
        ve_r = {n: sem(f"var_eps{n}_ready") for n in (1, 2)}
        rs_r = {n: sem(f"rough_rstd{n}_ready") for n in (1, 2)}
        z_r = {n: sem(f"z{n}_ready") for n in (1, 2)}
        zT_d = {n: sem(f"z{n}T_done") for n in (1, 2)}
        zT_hi = {n: sem(f"z{n}T_hi_ready") for n in (1, 2)}
        zT_lo = {n: sem(f"z{n}T_lo_ready") for n in (1, 2)}
        cxT_d, cxT_hi, cxT_lo = sem("ctxT_done"), sem("ctxT_hi_ready"), sem("ctxT_lo_ready")
        NAMES = ("q1", "k1", "q2", "k2")
        pj = {n: sem(f"proj_{n}_done") for n in NAMES + ("v1", "v2", "o1", "o2")}
        ab = {n: sem(f"rope_{n}_products") for n in NAMES}
        rot = {n: sem(f"rope_{n}_ready") for n in NAMES}
        rT_d = {n: sem(f"{n}_transposed") for n in NAMES}
        rT_r = {n: sem(f"{n}T_ready") for n in NAMES}
        v1_r, v2_r = sem("v1_ready"), sem("v2_ready")
        s_done, nmax_r, p_r = sem("scores_done"), sem("nmax_ready"), sem("prob_ready")
        pT_d, pTe_r, pTo_r = sem("probT_done"), sem("probT_even_ready"), sem("probT_odd_ready")
        av_d = sem("attn_out_done")
        ri_r = {n: sem(f"rinv{n}_ready") for n in (1, 2)}
        rb_r = {n: sem(f"rinv{n}_spread") for n in (1, 2)}
        ri_d = {n: sem(f"rinv{n}T_done") for n in (1, 2)}
        riT_r = {n: sem(f"rinv{n}T_ready") for n in (1, 2)}
        cn_r = {n: sem(f"ctxn{n}_ready") for n in (1, 2)}
        cn_hi = {n: sem(f"ctxn{n}_hi_ready") for n in (1, 2)}
        cn_lo = {n: sem(f"ctxn{n}_lo_ready") for n in (1, 2)}
        x1_r, x1b_r, x2_r, x2_out = sem("x1_ready"), sem("x1_bout_ready"), sem("x2_ready"), ffn["x2_out"]
        dstep = sem("vector_small_step")
        aggr, masked = sem("vector_aggregates"), sem("scores_masked")
        f_xn, f_w = sem("ffn_x2_loaded"), [sem(f"ffn_piece{n}_loaded") for n in range(HEAD)]
        f_hi, f_lo = sem("ffn_piece_hi_ready"), sem("ffn_piece_lo_ready")
        f_mv, f_ve, f_rs, f_z = sem("ffn_mean_var_ready"), sem("ffn_var_eps_ready"), sem("ffn_rough_rstd_ready"), sem("ffn_z_ready")
        rng_in, rng_r = sem("range_window_loaded"), sem("range_window_reduced")
        rng_p, rng_row, rng_m, rng_flag = sem("range_partitions_ready"), sem("range_row_loaded"), sem("range_max_ready"), sem("low_flag_ready")
        f_zT, f_zTh, f_zTl = sem("ffn_zT_done"), sem("ffn_zT_hi_ready"), sem("ffn_zT_lo_ready")

        block = es.enter_context(nc.Block())

        def wait(eng, s, value):
            if not isinstance(value, int) or value > 0:
                eng.wait_ge(s, value)

        def chunks(sq, cq):
            return ([(1, c) for c in range(NS)] if sq is not None else []) + \
                   ([(2, c) for c in range(NC)] if cq is not None else [])

        def is_first(q):
            return isinstance(q, int) and q == 0

        def head(kind, c, j):
            return (P // DK1) * j + c if kind == 1 else (P // DK2) * j + c

        def first_chunk(cq, oq):
            if cq is None:
                return 0 if oq is None else (NS + NC) * B
            return NS + (NS + NC) * cq

        def first_pair(cq, oq):
            if cq is None:
                return 0 if oq is None else (NS + NC) // 2 * B
            return NS // 2 + (NS + NC) // 2 * cq

        def slots(cq):
            return 0 if cq is None else NS

        LT, LA = 2, 3
        STEPS = NS + NC + LA
        PE_O2 = 1
        PE_CTX, READ_CTX = 4, 4
        DVE_NORM2 = 9
        PE_K2 = 10
        PE_V2 = 12
        DVE_ROPE_K2 = 13
        PE_Z2 = 14
        READ_Q2, READ_V1 = 3, 7
        DVE_RANGE = 11
        DVE_FFN_NORM = 9

        EARLY, LATE = [w[0] for w in WSRC[:3]], [w[0] for w in WSRC[3:]]

        def schedule(turn, fori, before_last=None, after_last=None):
            turn(None, None, 0, 1, None)
            turn(0, None, 1, 2, None)
            turn(1, 0, 2, 3, None)
            turn(2, 1, 3, 4, 0)
            with fori(2, B - 3) as c:
                turn(c + 1, c, c + 2, c + 3, c - 1)
            turn(B - 2, B - 3, B - 1, None, B - 4)
            if before_last is not None:
                before_last()
            turn(B - 1, B - 2, None, None, B - 3)
            turn(None, B - 1, None, None, B - 2)
            if after_last is not None:
                after_last()
            turn(None, None, None, None, B - 1)

        @block.sync
        def _(sp):
            sp.dma_start(xA[:, :], x[0, :, :]).then_inc(x_in, 16)
            sp.dma_start(pos_sb[:, :], pos).then_inc(pos_in, 16)
            for n, (name, src, k, m) in enumerate(WSRC):
                if n == 2:
                    sp.dma_start(cst[:, :], consts).then_inc(c_in, 16)
                    sp.dma_start(bout_b[:, :], bout.partition_broadcast(P)).then_inc(c_in, 16)
                sp.dma_start(whole(name), src.rearrange("(k p) n -> p k n", p=P)).then_inc(w_in[name], 16)

            def turn(sq, cq, nx, nz, oq):
                if sq is not None and cq is not None and not isinstance(sq, int):
                    sp.wait_ge(rng_r, cq - 1)
                    for n in range(3):
                        sp.dma_start(window[:, n, :], ffn["rows"][n][:, bass.ds((cq - 2) * STEP, WINDOW)]).then_inc(rng_in, 16)
                if sq is not None:
                    wait(sp, cxT_d, sq)
                    sp.dma_start(cx[:, :], ctx_in[sq, :, :]).then_inc(cx_in, 16)
                    wait(sp, x1_r, sq)
                    sp.dma_start(xB[:, :], x[sq, :, :]).then_inc(xb_in, 16)
                if nz is not None:
                    sp.wait_ge(z_r[1], nz)
                    sp.dma_start(xA[:, :], x[nz, :, :]).then_inc(x_in, 16)
                if oq is not None:
                    sp.wait_ge(x2_r, oq + 1)
                    sp.dma_start(x2_dram[oq, :, :], x2[:, :]).then_inc(x2_out, 16)

            def load_ffn_head():
                sp.wait_ge(rng_p, 1)
                sp.dma_start(rng_line[:, :], rng_col[:, :]).then_inc(rng_row, 16)
                sp.wait_ge(pj["v1"], B)
                sp.wait_ge(x2_out, 16 * (B - 3))
                sp.dma_start(ffn["xn"], block_rows(x2_dram, 0)).then_inc(f_xn, 16)
                for n in range(HEAD):
                    sp.dma_start(ffn["raw"][n], ffn["source"][n]).then_inc(f_w[n], 16)

            schedule(turn, sp.Fori, before_last=load_ffn_head)

        @block.gpsimd
        def _(pool):
            pool.memset(ident[:, :], 0.0).then_inc(c_zero, 1)
            pool.memset(causal[:, :], 0.0).then_inc(c_zero, 1)
            pool.memset(v2e[:, :, :, :], 0.0).then_inc(c_zero, 1)
            pool.memset(v2o[:, :, :, :], 0.0).then_inc(c_zero, 1)
            pool.memset(mhalf_c[:, :], -0.5).then_inc(c_zero, 1)
            pool.memset(one_c[:, :], 1.0).then_inc(c_zero, 1)
            pool.wait_ge(c_zero, 6)
            pool.affine_select(out=ident[:, :], in_=ident[:, :], compare_op=ALU.not_equal, fill=1.0,
                               base=0, pattern=[[-1, P]], channel_multiplier=1).then_inc(c_ready, 1)
            pool.affine_select(out=causal[:, :], in_=causal[:, :], compare_op=ALU.is_ge, fill=NEG,
                               base=0, pattern=[[-1, P]], channel_multiplier=1).then_inc(c_ready, 1)

            def rough_rstd(n, q):
                pool.wait_ge(ve_r[n], q + 1)
                pool.tensor_tensor(r0[n][:, :], ve[n][:, :], mhalf_c[:, 0:1], ALU.pow).then_inc(rs_r[n], 1)

            def rope_sum(n, q):
                wait(pool, ab[n], q + 1)
                pool.tensor_tensor(RA[n][:, :], RA[n][:, :], RB[n][:, :], ALU.add).then_inc(rot[n], 1)

            def spread(n, q, r, tile, h, w):
                wait(pool, ri_d[n], q)
                pool.wait_ge(ri_r[n], q + 1)
                pool.tensor_tensor(tile[:, :, :], r[:, :].unsqueeze(2).to_broadcast([P, h, w]),
                                   one_c[:, :].unsqueeze(2).to_broadcast([P, h, w]), ALU.mult).then_inc(rb_r[n], 1)

            def ctx_low(n, q):
                pool.wait_ge(cn_r[n], q + 1)
                pool.tensor_tensor(cn_l[:, :, :], cn[:, :, :], cn_h[:, :, :], ALU.subtract).then_inc(cn_lo[n], 1)

            def turn(sq, cq, nx, nz, oq):
                if oq is not None:
                    ctx_low(2, oq)
                if cq is not None:
                    rope_sum("q2", cq)
                    if sq is None:
                        pool.wait_ge(f_ve, 1)
                        pool.tensor_tensor(fr0[:, :], fve[:, :], mhalf_c[:, :], ALU.pow).then_inc(f_rs, 1)
                    pool.wait_ge(x1_r, cq + 1)
                    wait(pool, x2_r, cq)
                    pool.tensor_tensor(x1B[:, :], x1A[:, :], bout_b[:, :], ALU.add).then_inc(x1b_r, 1)
                if nx is not None:
                    rope_sum("q1", nx)
                if sq is not None:
                    spread(1, sq, rinv1, rbc1, H1, DK1)
                if nx is not None:
                    rope_sum("k1", nx)
                if nz is not None:
                    rough_rstd(1, nz)
                if sq is not None:
                    ctx_low(1, sq)
                    rough_rstd(2, sq)
                if cq is not None:
                    spread(2, cq, rinv2, rbc2, H2, DK2)
                if sq is not None:
                    rope_sum("k2", sq)
                if is_first(nx):
                    split_low(LATE)

            def split_low(names):
                for name in names:
                    pool.wait_ge(w_hi, len(EARLY) + LATE.index(name) + 1)
                    pool.tensor_tensor(WLO[name][:, :, :], whole(name), WHI[name][:, :, :], ALU.subtract)\
                        .then_inc(w_lo["pool"], 1)

            rough_rstd(1, 0)
            pool.wait_ge(c_in, 32)
            schedule(turn, pool.Fori)

        @block.tensor
        def _(pe):
            def transpose4(dst, src, k=KT):
                for j in range(k):
                    last = nc.tensor.transpose(dst[:, j * P:(j + 1) * P], src(j), ident[:, :])
                return last

            def project(dst, th, tl, name, k, cols=slice(0, D), lo_ready=None, fresh=False):
                hi, lo = WHI[name], WLO[name]
                if fresh:
                    if name in EARLY:
                        pe.wait_ge(w_lo["dve"], EARLY.index(name) + 1)
                    else:
                        pe.wait_ge(w_lo["pool"], LATE.index(name) + 1)
                n = 0
                for a, w in ((th, hi), (th, lo), (tl, hi)):
                    if a is tl and lo_ready is not None:
                        pe.wait_ge(*lo_ready)
                    for j in range(k):
                        last = nc.tensor.matmul(dst[:, :], a[:, j, :], w[:, j, cols],
                                                start=(n == 0), stop=(n == 3 * k - 1))
                        n += 1
                return last

            def scores(kind, c, slot, m):
                for j in range(G):
                    if kind == 1:
                        r, q, k = DK1 * c, qT1, kT1
                    else:
                        r, q, k = 2 * DK2 * (c // 2), qT2, (kT2e, kT2o)[c % 2]
                    last = nc.tensor.matmul(SC[m][:, j * P:(j + 1) * P], q[r:r + 32, j, :], k[r:r + 32, j, :],
                                            start=True, stop=True, skip_group_check=True)
                last.then_inc(s_done, 1)

            def attend(kind, c, slot):
                for j in range(G):
                    if kind == 1:
                        r, dst, v = DK1 * c, PC, v1[:, head(1, c, j) * DK1:(head(1, c, j) + 1) * DK1]
                        start, stop = True, True
                    else:
                        pair = head(2, c, j) // 2
                        r, dst, v = 2 * DK2 * (c // 2), PB, (v2e, v2o)[c % 2][:, pair, :, :].rearrange("p a d -> p (a d)")
                        start, stop = c % 2 == 0 and j == 0, c % 2 == 1
                    last = nc.tensor.matmul(dst[r:r + 32, j * P:(j + 1) * P], v, probT[:, slot, j, :],
                                            start=start, stop=stop, skip_group_check=True)
                last.then_inc(av_d, 1)

            def columns(t):
                return lambda j: t[:, j * P:(j + 1) * P]

            def turn(sq, cq, nx, nz, oq):
                order = chunks(sq, cq)
                n0, s0, par = first_chunk(cq, oq), slots(cq), first_pair(cq, oq)
                has_s, has_c, has_n, has_o = sq is not None, cq is not None, nx is not None, oq is not None
                if has_n:
                    pe.wait_ge(z_r[1], nx + 1)
                    wait(pe, pTe_r, par)
                    transpose4(TA, columns(z1)).then_inc(zT_d[1], 1)
                if has_o and not has_s:
                    transpose_rinv2(oq, par)
                if not (has_s or has_c or has_n):
                    transpose_ffn_head()
                if has_c and not has_s:
                    project_q2(cq)
                for t in range(STEPS):
                    if t < len(order):
                        kind, c = order[t]
                        wait(pe, p_r, n0 + t - 1)
                        if kind == 1 and c == 0:
                            pe.wait_ge(rT_r["q1"], sq + 1)
                            pe.wait_ge(rT_r["k1"], sq + 1)
                        if kind == 2 and c == 0:
                            if not has_s:
                                transpose_q2_k2(cq, par, has_o)
                            pe.wait_ge(rT_r["q2"], cq + 1)
                            pe.wait_ge(rT_r["k2"], cq + 1)
                        scores(kind, c, (s0 + t) % NP, t % 2)
                    if t == 0 and has_o and has_s:
                        transpose_rinv2(oq, par)
                    if t == 0 and has_c and has_s:
                        project_q2(cq)
                    if t == PE_O2 and has_o:
                        pe.wait_ge(cn_r[2], oq + 1)
                        project(PB, cn_h, cn_l, "o2", KT, lo_ready=(cn_lo[2], oq + 1), fresh=is_first(oq)).then_inc(pj["o2"], 1)
                    if t == 2 and has_c and has_s:
                        transpose_q2_k2(cq, par, has_o)
                    if t == 3 and has_n:
                        pe.wait_ge(zT_hi[1], nx + 1)
                        if has_c:
                            pe.wait_ge(ab["q2"], cq + 1)
                        else:
                            wait(pe, v1_r, nx)
                        project(PA, z1T_h, z1T_l, "q1", KT, lo_ready=(zT_lo[1], nx + 1), fresh=is_first(nx)).then_inc(pj["q1"], 1)
                    if t == 4 and has_n:
                        if has_o:
                            pe.wait_ge(x2_r, oq + 1)
                        else:
                            wait(pe, ab["k1"], nx)
                        project(PB, z1T_h, z1T_l, "k1", KT, fresh=is_first(nx)).then_inc(pj["k1"], 1)
                    if t == PE_CTX and has_s:
                        pe.wait_ge(cx_in, 16 * (sq + 1))
                        if has_c:
                            pe.wait_ge(rT_r["k2"], cq + 1)
                        transpose4(TC, columns(cx), CKT).then_inc(cxT_d, 1)
                    if t == 6 and has_n:
                        pe.wait_ge(ab["q1"], nx + 1)
                        project(PA, z1T_h, z1T_l, "v1", KT, fresh=is_first(nx)).then_inc(pj["v1"], 1)
                    if t == 6 and has_s:
                        pe.wait_ge(rb_r[1], sq + 1)
                        pe.wait_ge(cxT_lo, sq + 1)
                        transpose4(TC, columns(rbc1[:, :, :].rearrange("p h d -> p (h d)"))).then_inc(ri_d[1], 1)
                    if t == 8 and has_s:
                        pe.wait_ge(cn_r[1], sq + 1)
                        project(PC, cn_h, cn_l, "o1", KT, lo_ready=(cn_lo[1], sq + 1), fresh=is_first(sq)).then_inc(pj["o1"], 1)
                    if t == 9 and has_n:
                        pe.wait_ge(rot["q1"], nx + 1)
                        if has_s:
                            pe.wait_ge(riT_r[1], sq + 1)
                        transpose4(TC, columns(RA["q1"])).then_inc(rT_d["q1"], 1)
                    if t == 11 and has_n:
                        pe.wait_ge(rot["k1"], nx + 1)
                        pe.wait_ge(rT_r["q1"], nx + 1)
                        transpose4(TC, columns(RA["k1"])).then_inc(rT_d["k1"], 1)
                    if t == PE_K2 and has_s:
                        if has_n:
                            pe.wait_ge(v1_r, nx + 1)
                        elif has_c:
                            pe.wait_ge(ab["q2"], cq + 1)
                        project(PA, cxT_h, cxT_l, "kv2", CKT, slice(0, D), fresh=is_first(sq)).then_inc(pj["k2"], 1)
                    if t == PE_V2 and has_s:
                        pe.wait_ge(x1_r, sq + 1)
                        project(PC, cxT_h, cxT_l, "kv2", CKT, slice(D, 2 * D)).then_inc(pj["v2"], 1)
                    if t == PE_Z2 and has_s:
                        pe.wait_ge(z_r[2], sq + 1)
                        if has_n:
                            pe.wait_ge(rT_r["k1"], nx + 1)
                        transpose4(TC, columns(z2)).then_inc(zT_d[2], 1)
                    if 0 <= t - LT < len(order):
                        u = t - LT
                        pe.wait_ge(p_r, n0 + u + 1)
                        if u >= 2:
                            pe.wait_ge((pTe_r, pTo_r)[u % 2], par + u // 2)
                        elif u == 0 and has_n:
                            pe.wait_ge(zT_lo[1], nx + 1)
                        elif has_c:
                            pe.wait_ge(rT_r["q2"], cq + 1)
                        transpose4(TP[u % 2], lambda j, s=(s0 + u) % NP: prob[:, s, j, :]).then_inc(pT_d, 1)
                    if 0 <= t - LA < len(order):
                        u = t - LA
                        kind, c = order[u]
                        pe.wait_ge((pTe_r, pTo_r)[u % 2], par + u // 2 + 1)
                        if kind == 1 and c == 0:
                            pe.wait_ge(v1_r, sq + 1)
                            wait(pe, v2_r, sq)
                        if kind == 2 and c == 0:
                            pe.wait_ge(v2_r, cq + 1)
                            if has_n:
                                pe.wait_ge(ab["k1"], nx + 1)
                            elif has_o:
                                pe.wait_ge(x2_r, oq + 1)
                        attend(kind, c, (s0 + u) % NP)

            def transpose_ffn_head():
                pe.wait_ge(f_z, 1)
                for k in range(KT):
                    for s in range(TPB):
                        last = nc.tensor.transpose(FZ[k][:, s * P:(s + 1) * P], ffn["xn"][:, s, k * P:(k + 1) * P], ident[:, :])
                    last.then_inc(f_zT, 1)

            def transpose_rinv2(oq, par):
                pe.wait_ge(rb_r[2], oq + 1)
                pe.wait_ge(pTo_r, par)
                transpose4(TB, columns(rbc2[:, :, :].rearrange("p h d -> p (h d)"))).then_inc(ri_d[2], 1)

            def project_q2(cq):
                pe.wait_ge(zT_hi[2], cq + 1)
                pe.wait_ge(ab["k2"], cq + 1)
                project(PA, z2T_h, z2T_l, "q2", KT, lo_ready=(zT_lo[2], cq + 1), fresh=is_first(cq)).then_inc(pj["q2"], 1)

            def transpose_q2_k2(cq, par, has_o):
                pe.wait_ge(rot["q2"], cq + 1)
                if has_o:
                    pe.wait_ge(riT_r[2], cq)
                else:
                    wait(pe, pTo_r, par)
                transpose4(TB, columns(RA["q2"])).then_inc(rT_d["q2"], 1)
                pe.wait_ge(rot["k2"], cq + 1)
                pe.wait_ge(zT_lo[2], cq + 1)
                transpose4(TC, columns(RA["k2"])).then_inc(rT_d["k2"], 1)

            pe.wait_ge(c_ready, 2)
            schedule(turn, pe.Fori)

        @block.scalar
        def _(act):
            act.wait_ge(tab, 1)
            nc.scalar.activation(ang_s[:, :], ang_s[:, :], ACT.Sin).then_inc(tab_act, 1)
            nc.scalar.activation(ang_c[:, :], ang_c[:, :], ACT.Sin).then_inc(tab_act, 1)

            def split_high(names):
                for name in names:
                    act.wait_ge(w_in[name], 16)
                    nc.scalar.activation(WHI[name][:, :, :], whole(name), ACT.Copy).then_inc(w_hi, 1)

            split_high(EARLY)
            act.wait_ge(c_ready, 2)

            def flat(t):
                return t[:, :, :].rearrange("p k t -> p (k t)")

            def copy_rinv2(oq):
                act.wait_ge(ri_d[2], oq + 1)
                nc.scalar.activation(rT2[:, :], TB[:, :], ACT.Copy).then_inc(riT_r[2], 1)

            def turn(sq, cq, nx, nz, oq):
                order = chunks(sq, cq)
                n0, s0 = first_chunk(cq, oq), slots(cq)
                has_s, has_c, has_n, has_o = sq is not None, cq is not None, nx is not None, oq is not None
                if has_o and not has_s:
                    copy_rinv2(oq)
                if not (has_s or has_c or has_n):
                    for k in range(KT):
                        act.wait_ge(f_zT, k + 1)
                        nc.scalar.activation(ffn["zT_h"][:, k, :], FZ[k][:, :], ACT.Copy).then_inc(f_zTh, 1)
                if has_n:
                    act.wait_ge(zT_d[1], nx + 1)
                    wait(act, pj["v1"], nx)
                    nc.scalar.activation(flat(z1T_h), TA[:, :], ACT.Copy).then_inc(zT_hi[1], 1)
                if is_first(nx):
                    split_high(LATE)
                if has_o and has_s:
                    copy_rinv2(oq)
                for t in range(STEPS):
                    if t == (READ_Q2 if has_s else 0) and has_c:
                        act.wait_ge(rT_d["q2"], cq + 1)
                        nc.scalar.activation(flat(qT2), TB[:, :], ACT.Copy).then_inc(rT_r["q2"], 1)
                    if t < len(order):
                        s = (s0 + t) % NP
                        kind, c = order[t]
                        rs = (rsum1, rsum2)[kind - 1]
                        act.wait_ge(nmax_r, n0 + t + 1)
                        if c == 0:
                            wait(act, ri_r[kind], (sq, cq)[kind - 1])
                        if kind == 2:
                            wait(act, pT_d, n0 + t - NP + 1)
                        for j in range(G):
                            src = prob[:, s, j, :] if kind == 1 else SC[t % 2][:, j * P:(j + 1) * P]
                            last = nc.scalar.activation(prob[:, s, j, :], src, ACT.Exp,
                                                        bias=nmax[:, s, j:j + 1],
                                                        accum_out=rs[:, head(kind, c, j):head(kind, c, j) + 1])
                        last.then_inc(p_r, 1)
                    u = t - LT
                    if 0 <= u < len(order) and u % 2 == 1:
                        act.wait_ge(pT_d, n0 + u + 1)
                        wait(act, av_d, n0 + u - NP + 1)
                        nc.scalar.activation(probT[:, (s0 + u) % NP, :, :].rearrange("p g t -> p (g t)"),
                                             TP[1][:, :], ACT.Copy).then_inc(pTo_r, 1)
                    if t == READ_CTX and has_s:
                        act.wait_ge(cxT_d, sq + 1)
                        nc.scalar.activation(flat(cxT_h), TC[:, 0:CD], ACT.Copy).then_inc(cxT_hi, 1)
                    if t == 6 and has_s:
                        act.wait_ge(ri_d[1], sq + 1)
                        nc.scalar.activation(rT1[:, :], TC[:, :], ACT.Copy).then_inc(riT_r[1], 1)
                    if t == 9 and has_n:
                        act.wait_ge(rT_d["q1"], nx + 1)
                        nc.scalar.activation(flat(qT1), TC[:, :], ACT.Copy).then_inc(rT_r["q1"], 1)
                    if t == READ_V1 and has_n:
                        act.wait_ge(pj["v1"], nx + 1)
                        if has_s:
                            act.wait_ge(av_d, n0 + NS)
                        nc.scalar.activation(v1[:, :], PA[:, :], ACT.Copy).then_inc(v1_r, 1)
                    if t == PE_Z2 and has_s:
                        act.wait_ge(zT_d[2], sq + 1)
                        nc.scalar.activation(flat(z2T_h), TC[:, :], ACT.Copy).then_inc(zT_hi[2], 1)
                if has_s:
                    act.wait_ge(pj["v2"], sq + 1)
                    act.wait_ge(av_d, n0 + len(order))
                    v2p = PC[:, :].rearrange("p (g a d) -> p g a d", a=2, d=DK2)
                    nc.scalar.activation(v2e[:, :, 0, :], v2p[:, :, 0, :], ACT.Copy)
                    nc.scalar.activation(v2o[:, :, 1, :], v2p[:, :, 1, :], ACT.Copy).then_inc(v2_r, 1)

            def split_ffn_head():
                for n in range(HEAD):
                    act.wait_ge(f_w[n], 16)
                    nc.scalar.activation(ffn["hi"][n], ffn["raw"][n], ACT.Copy, bias=-ZERO_POINT).then_inc(f_hi, 1)

            schedule(turn, act.Fori, after_last=split_ffn_head)

        @block.vector
        def _(dve):
            small = {"n": 0, "base": 0}

            def link(ins):
                small["n"] += 1
                ins.then_inc(dstep, 1)
                dve.wait_ge(dstep, small["base"] + small["n"])

            pos_t = pos_sb[:, :].rearrange("p (b c) -> p b c", c=2)
            full_s = ang_s[:, :].rearrange("p (b c i) -> p b c i", b=B, c=2)
            turns = turns_sb[:, :]
            dve.wait_ge(pos_in, 16)
            for i in range(HALF):
                last = nc.vector.tensor_scalar(full_s[:, :, :, i], pos_t, float(np.float32(10000.0 ** (-i / HALF))), None, ALU.mult)
            link(last)
            link(nc.vector.tensor_scalar(turns, ang_s[:, :], 1.0 / TWO_PI, MAGIC, ALU.mult, ALU.add))
            link(nc.vector.tensor_scalar(turns, turns, MAGIC, None, ALU.subtract))
            for part in (PI_A, PI_B, PI_C):
                link(nc.vector.scalar_tensor_tensor(out=ang_s[:, :], in0=turns, scalar=-part, in1=ang_s[:, :],
                                                    op0=ALU.mult, op1=ALU.add))
            link(nc.vector.tensor_scalar(ang_s[:, :], ang_s[:, :], math.pi - 1e-6, -(math.pi - 1e-6), ALU.min, ALU.max))
            link(nc.vector.scalar_tensor_tensor(out=ang_c[:, :], in0=ang_s[:, :], scalar=-1.0, in1=ang_s[:, :],
                                                op0=ALU.mult, op1=ALU.max))
            nc.vector.tensor_scalar(ang_c[:, :], ang_c[:, :], -1.0, math.pi / 2, ALU.mult, ALU.add).then_inc(tab, 1)
            dve.wait_ge(tab_act, 2)
            flat_s = ang_s[:, :].rearrange("p (b j) -> p b j", b=B)
            flat_c = ang_c[:, :].rearrange("p (b j) -> p b j", b=B)
            c2 = cos2[:, :, :].rearrange("p b (j e) -> p b j e", e=2)
            s2 = sin2[:, :, :].rearrange("p b (j e) -> p b j e", e=2)
            nc.vector.tensor_copy(c2[:, :, :, 0], flat_c)
            nc.vector.tensor_copy(c2[:, :, :, 1], flat_c)
            nc.vector.tensor_scalar(s2[:, :, :, 0], flat_s, -1.0, None, ALU.mult)
            link(nc.vector.tensor_copy(s2[:, :, :, 1], flat_s))

            def flat(t):
                return t[:, :, :].rearrange("p k t -> p (k t)")

            def statistics(n, tile, q):
                link(nc.vector.bn_stats(st[n][:, :], tile[:, :]))
                dve.sem_inc(aggr, 1)
                nc.vector.bn_aggr(mv[n][:, :], st[n][:, :]).then_inc(mv_r[n], 1)
                dve.wait_ge(mv_r[n], q + 1)
                nc.vector.tensor_scalar(ve[n][:, :], mv[n][:, 1:2], EPS, None, ALU.add).then_inc(ve_r[n], 1)

            def normalise(n, tile, z, q):
                t = nt[n]
                dve.wait_ge(rs_r[n], q + 1)
                link(nc.vector.scalar_tensor_tensor(out=t[:, 1:2], in0=r0[n][:, :], scalar=ve[n][:, :], in1=r0[n][:, :],
                                                    op0=ALU.mult, op1=ALU.mult))
                link(nc.vector.tensor_scalar(t[:, 2:3], t[:, 1:2], -0.5, 1.5, ALU.mult, ALU.add))
                link(nc.vector.tensor_tensor(t[:, 3:4], t[:, 2:3], r0[n][:, :], ALU.mult))
                wait(dve, zT_d[n], q)
                nc.vector.tensor_scalar(z[:, :], tile[:, :], mv[n][:, 0:1], t[:, 3:4], ALU.subtract, ALU.mult)\
                    .then_inc(z_r[n], 1)

            def rope(n, q, src, w, cos, sin, scale):
                h = D // w
                dve.wait_ge(pj[n], q + 1)
                wait(dve, rT_d[n], q)
                nc.vector.scalar_tensor_tensor(
                    out=RA[n][:, :].rearrange("p (h j) -> p h j", j=w), in0=src[:, :].rearrange("p (h j) -> p h j", j=w),
                    scalar=scale, in1=cos.to_broadcast([P, h, w]), op0=ALU.mult, op1=ALU.mult)
                for e in range(2):
                    last = nc.vector.scalar_tensor_tensor(
                        out=RB[n][:, :].rearrange("p (h j e) -> p h j e", j=w // 2, e=2)[:, :, :, e],
                        in0=src[:, :].rearrange("p (h j e) -> p h j e", j=w // 2, e=2)[:, :, :, 1 - e], scalar=scale,
                        in1=sin.rearrange("p o (j e) -> p o j e", e=2)[:, :, :, e].to_broadcast([P, h, w // 2]),
                        op0=ALU.mult, op1=ALU.mult)
                last.then_inc(ab[n], 1)

            def ffn_statistics():
                dve.wait_ge(f_xn, 16)
                for s in range(TPB):
                    last = nc.vector.bn_stats(fst[:, s, :], ffn["xn"][:, s, :])
                link(last)
                for s in range(TPB):
                    last = nc.vector.bn_aggr(fmv[:, s, :], fst[:, s, :])
                last.then_inc(f_mv, 1)
                dve.wait_ge(f_mv, 1)
                nc.vector.tensor_scalar(fve[:, :], fmv[:, :, 1], EPS, None, ALU.add).then_inc(f_ve, 1)

            def ffn_normalise():
                dve.wait_ge(f_rs, 1)
                link(nc.vector.tensor_tensor(fnt[:, 0, :], fve[:, :], fr0[:, :], ALU.mult))
                link(nc.vector.tensor_tensor(fnt[:, 1, :], fnt[:, 0, :], fr0[:, :], ALU.mult))
                link(nc.vector.tensor_scalar(fnt[:, 2, :], fnt[:, 1, :], -0.5, 1.5, ALU.mult, ALU.add))
                link(nc.vector.tensor_tensor(fnt[:, 3, :], fnt[:, 2, :], fr0[:, :], ALU.mult))
                for s in range(TPB):
                    last = nc.vector.tensor_scalar(ffn["xn"][:, s, :], ffn["xn"][:, s, :], fmv[:, s, 0:1], fnt[:, 3, s:s + 1],
                                                   ALU.subtract, ALU.mult)
                last.then_inc(f_z, 1)

            cos1, sin1 = cst[:, 0:DK1].unsqueeze(1), cst[:, DK1:2 * DK1].unsqueeze(1)
            even, odd = cst[:, 2 * DK1:2 * DK1 + 1], cst[:, 2 * DK1 + 1:2 * DK1 + 2]

            def normalise_ctx(n, src, r):
                nc.vector.tensor_tensor(flat(cn_h), src[:, :], r[:, :], ALU.mult).then_inc(cn_hi[n], 1)
                nc.vector.tensor_tensor(flat(cn), src[:, :], r[:, :], ALU.mult).then_inc(cn_r[n], 1)

            def cross_out(oq, n0):
                dve.wait_ge(riT_r[2], oq + 1)
                dve.wait_ge(av_d, n0)
                normalise_ctx(2, PB, rT2)

            def low(dst, src, hi, s):
                nc.vector.tensor_tensor(flat(dst), src, flat(hi), ALU.subtract).then_inc(s, 1)

            def turn(sq, cq, nx, nz, oq):
                order = chunks(sq, cq)
                n0, s0 = first_chunk(cq, oq), slots(cq)
                has_s, has_c, has_n, has_o = sq is not None, cq is not None, nx is not None, oq is not None
                m0 = NS * sq if has_s else None
                in_loop = has_c and not isinstance(cq, int)
                if in_loop:
                    small["base"], small["n"] = small["n"] - 2 * LOOP_STEPS + LOOP_STEPS * cq, 0
                if has_n:
                    dve.wait_ge(zT_hi[1], nx + 1)
                    low(z1T_l, TA[:, :], z1T_h, zT_lo[1])
                if has_o and not has_s:
                    cross_out(oq, n0)
                if not (has_s or has_c or has_n):
                    for k in range(KT):
                        dve.wait_ge(f_zTh, k + 1)
                        nc.vector.tensor_tensor(ffn["zT_l"][:, k, :], FZ[k][:, :], ffn["zT_h"][:, k, :], ALU.subtract).then_inc(f_zTl, 1)
                if has_c and not has_s:
                    rope("q2", cq, PA, DK2, cos2[:, bass.ds(cq, 1), :], sin2[:, bass.ds(cq, 1), :], DK2 ** -0.5)
                    ffn_statistics()
                for t in range(STEPS):
                    if t == (3 if has_s else 0) and has_c:
                        dve.wait_ge(rT_d["k2"], cq + 1)
                        nc.vector.tensor_scalar(flat(kT2e), TC[:, :], even, None, ALU.mult)
                        nc.vector.tensor_scalar(flat(kT2o), TC[:, :], odd, None, ALU.mult).then_inc(rT_r["k2"], 1)
                    if t < len(order):
                        s = (s0 + t) % NP
                        dve.wait_ge(s_done, n0 + t + 1)
                        wait(dve, p_r, n0 + t - NP + 1)
                        scored = SC[t % 2][:, :].rearrange("p (g k) -> p g k", g=G)
                        if order[t][0] == 1:
                            wait(dve, pT_d, n0 + t - NP + 1)
                            nc.vector.tensor_tensor(prob[:, s, :, :], scored, causal[:, :].unsqueeze(1).to_broadcast([P, G, P]),
                                                    ALU.add).then_inc(masked, 1)
                            dve.wait_ge(masked, m0 + t + 1)
                            scored = prob[:, s, :, :]
                        nc.vector.tensor_reduce(out=nmax[:, s, :], in_=scored, op=ALU.max, axis=AX, negate=True)\
                            .then_inc(nmax_r, 1)
                    u = t - LT
                    if 0 <= u < len(order) and u % 2 == 0:
                        dve.wait_ge(pT_d, n0 + u + 1)
                        wait(dve, av_d, n0 + u - NP + 1)
                        nc.vector.tensor_copy(probT[:, (s0 + u) % NP, :, :].rearrange("p g t -> p (g t)"),
                                              TP[0][:, :]).then_inc(pTe_r, 1)
                    if t == 0 and has_o and has_s:
                        cross_out(oq, n0)
                    if t == 0 and has_c and has_s:
                        rope("q2", cq, PA, DK2, cos2[:, bass.ds(cq, 1), :], sin2[:, bass.ds(cq, 1), :], DK2 ** -0.5)
                    if t == PE_O2 and has_o:
                        dve.wait_ge(pj["o2"], oq + 1)
                        dve.wait_ge(x1b_r, oq + 1)
                        wait(dve, x2_out, 16 * oq)
                        nc.vector.tensor_tensor(x2[:, :], PB[:, :], x1B[:, :], ALU.add).then_inc(x2_r, 1)
                    if t == DVE_RANGE and in_loop:
                        dve.wait_ge(rng_in, 48 * (cq - 1))
                        nc.vector.tensor_reduce(out=rng[:, bass.ds(cq - 2, 1)], in_=window[:, :, :].rearrange("p a n -> p (a n)"),
                                                op=ALU.max, axis=AX, apply_absolute_value=True).then_inc(rng_r, 1)
                    if t == DVE_FFN_NORM and has_c and not has_s:
                        ffn_normalise()
                    if t == 3 and has_n:
                        rope("q1", nx, PA, DK1, cos1, sin1, DK1 ** -0.5)
                    if t == 4 and has_s:
                        dve.wait_ge(p_r, n0 + NS)
                        wait(dve, rb_r[1], sq)
                        nc.vector.reciprocal(rinv1[:, :], rsum1[:, :]).then_inc(ri_r[1], 1)
                    if t == 4 and has_n:
                        rope("k1", nx, PB, DK1, cos1, sin1, 1.0)
                    if t == READ_CTX and has_s:
                        dve.wait_ge(cxT_hi, sq + 1)
                        low(cxT_l, TC[:, 0:CD], cxT_h, cxT_lo)
                    if t == 5 and nz is not None:
                        dve.wait_ge(x_in, 16 * (nz + 1))
                        statistics(1, xA, nz)
                    if t == 6 and has_s:
                        dve.wait_ge(riT_r[1], sq + 1)
                        dve.wait_ge(av_d, n0 + NS)
                        normalise_ctx(1, PC, rT1)
                    if t == 7 and nz is not None:
                        normalise(1, xA, z1, nz)
                    if t == 8 and has_s:
                        dve.wait_ge(pj["o1"], sq + 1)
                        dve.wait_ge(xb_in, 16 * (sq + 1))
                        wait(dve, x1b_r, sq)
                        nc.vector.tensor_tensor(x1A[:, :], PC[:, :], xB[:, :], ALU.add).then_inc(x1_r, 1)
                        dve.wait_ge(x1_r, sq + 1)
                        statistics(2, x1A, sq)
                    if t == DVE_NORM2 and has_s:
                        normalise(2, x1A, z2, sq)
                    if t == DVE_ROPE_K2 and has_s:
                        rope("k2", sq, PA, DK2, cos2[:, bass.ds(sq, 1), :], sin2[:, bass.ds(sq, 1), :], 1.0)
                    if t == 11 and has_n:
                        dve.wait_ge(rT_d["k1"], nx + 1)
                        nc.vector.tensor_copy(flat(kT1), TC[:, :]).then_inc(rT_r["k1"], 1)
                    if t == PE_Z2 and has_s:
                        dve.wait_ge(zT_hi[2], sq + 1)
                        low(z2T_l, TC[:, :], z2T_h, zT_lo[2])
                    if t == STEPS - LA and has_c:
                        dve.wait_ge(p_r, n0 + len(order))
                        wait(dve, rb_r[2], cq)
                        nc.vector.reciprocal(rinv2[:, :], rsum2[:, :]).then_inc(ri_r[2], 1)
                if in_loop:
                    assert small["n"] == LOOP_STEPS
                    small["base"], small["n"] = 0, before["n"] + LOOP_STEPS * (B - 5)

            LOOP_STEPS = 8
            dve.wait_ge(x_in, 16)
            statistics(1, xA, 0)
            normalise(1, xA, z1, 0)
            for n, name in enumerate(EARLY):
                dve.wait_ge(w_hi, n + 1)
                nc.vector.tensor_tensor(WLO[name][:, :, :], whole(name), WHI[name][:, :, :], ALU.subtract)\
                    .then_inc(w_lo["dve"], 1)
            dve.wait_ge(c_in, 32)
            before = {"n": 0}

            @contextmanager
            def turns_of(a, b):
                before["n"] = small["n"]
                with dve.Fori(a, b) as c:
                    yield c

            def reduce_windows():
                dve.wait_ge(rng_r, TURNS + 1)
                nc.vector.tensor_reduce(out=rng_col[:, :], in_=rng[:, :], op=ALU.max, axis=AX).then_inc(rng_p, 1)

            def split_ffn_head():
                dve.wait_ge(rng_row, 16)
                nc.vector.tensor_reduce(out=rng_max[:, :], in_=rng_line[:, :], op=ALU.max, axis=AX).then_inc(rng_m, 1)
                dve.wait_ge(rng_m, 1)
                nc.vector.tensor_scalar(ffn["low_flag"][:, :], rng_max[:, :], EXACT, None, ALU.is_gt).then_inc(rng_flag, 1)
                for n in range(HEAD):
                    dve.wait_ge(f_hi, n + 1)
                    nc.vector.scalar_tensor_tensor(out=ffn["lo"][n], in0=ffn["raw"][n], scalar=ZERO_POINT, in1=ffn["hi"][n],
                                                   op0=ALU.subtract, op1=ALU.subtract).then_inc(f_lo, 1)

            dve.sem_inc(rng_r, 1)
            schedule(turn, turns_of, before_last=reduce_windows, after_last=split_ffn_head)
            dve.wait_ge(rng_flag, 1)


def ffn_phase(nc, fp32, fp32r, i32, ALU, ACT, x2_dram, wg, sg, wu, su, wd, sd, out, ident, mhalf, ffn):
    es = ExitStack()
    with es:
        def sb(name, shape, dt=fp32):
            return es.enter_context(nc.sbuf_tensor(name, shape, dt))

        def sem(name):
            return es.enter_context(nc.semaphore(name))

        T = TPB * P
        hi, lo, raw = list(ffn["hi"]), list(ffn["lo"]), [None] * HEAD
        for n in range(HEAD, len(PIECES)):
            m = PIECES[n][2]
            h_ = sb(f"piece{n}_hi", [P, m * D], fp32r)
            loaded, l_ = two_types(nc, es, f"piece{n}_lo", [P, m * D], fp32, fp32r)
            hi.append(piece_view(n, h_[:, :]))
            lo.append(piece_view(n, l_[:, :]))
            raw.append(piece_view(n, loaded[:, :].bitcast(i32)))
        sg_c, su_c, sd_b = sb("sg_c", [P, HT]), sb("su_c", [P, HT]), sb("sd_b", [P, D])
        xn = ffn["xn"]
        xr = sb("xr", [P, TPB, D])
        zT_h, zT_l = ffn["zT_h"], ffn["zT_l"]
        sil = [sb(f"sil{n}", [P, T]) for n in range(2)]
        h = [sb(f"h{n}", [P, T]) for n in range(2)]
        h_h = [sb(f"h_h{n}", [P, T], fp32r) for n in range(2)]
        h_l = [sb(f"h_l{n}", [P, T], fp32r) for n in range(2)]
        ys = [sb(f"ys{n}", [P, D]) for n in range(2)]
        st, mv = sb("st", [P, TPB, 6]), sb("mv", [P, TPB, 2])
        ve, r0, nt = sb("ve", [P, TPB]), sb("r0", [P, TPB]), sb("nt", [P, 4, TPB])

        bank = [es.enter_context(nc.psum_tensor(f"fbank{n}", [P, 512], fp32)) for n in range(8)]
        DN = bank[0:TPB]
        GT = [bank[4], bank[6]]
        UP = [bank[5], bank[7]]
        TZ = [bank[6], bank[7], bank[4], bank[5]]

        w_in = {n: sem(f"fw_piece{n}_loaded") for n in range(HEAD, len(PIECES))}
        w_hi, w_lo = sem("fw_hi_ready"), sem("fw_lo_ready")
        cin = sem("f_scales_loaded")
        xn_in, xr_in, stored = sem("xn_loaded"), sem("xr_loaded"), sem("out_stored")
        mv_r, ve_r, rs_r, z_r = sem("f_mean_var_ready"), sem("f_var_eps_ready"), sem("f_rough_rstd_ready"), sem("f_z_ready")
        zT_d, zT_hr, zT_lr = sem("f_zT_done"), sem("f_zT_hi_ready"), sem("f_zT_lo_ready")
        g_d, u_d, dn_d = sem("gate_done"), sem("up_done"), sem("down_done")
        sil_r, h_r, hh_r, hl_r = sem("silu_ready"), sem("h_ready"), sem("h_hi_ready"), sem("h_lo_ready")
        ys_r, y_r = sem("scaled_down_ready"), sem("out_ready")
        rstd_r = sem("f_rstd_ready")
        dstep, aggr = sem("f_vector_small_step"), sem("f_vector_aggregates")

        block = es.enter_context(nc.Block())

        def wait(eng, s, value):
            if not isinstance(value, int) or value > 0:
                eng.wait_ge(s, value)

        def pieces_at(j):
            return range(3 * (j // 2 + 1), min(3 * (j // 2 + 2), len(PIECES))) if j % 2 == 0 else ()

        def schedule(program, fori):
            program(0, 1, True)
            with fori(1, NBLK - 1) as nb:
                program(nb, nb + 1, False)
            program(NBLK - 1, None, False)

        @block.sync
        def _(sp):
            sp.dma_start(sg_c[:, :], sg).then_inc(cin, 16)
            sp.dma_start(su_c[:, :], su).then_inc(cin, 16)
            sp.dma_start(sd_b[:, :], sd.partition_broadcast(P)).then_inc(cin, 16)

            def load_pieces(a, b):
                for n in range(a, b):
                    sp.dma_start(raw[n], piece_source(n, wg, wu, wd)).then_inc(w_in[n], 16)

            load_pieces(HEAD, 3 * HEAD)
            sp.wait_ge(ffn["x2_out"], 16 * B)

            def program(nb, nx, first):
                wait(sp, stored, 16 * nb)
                sp.dma_start(xr[:, :, :], block_rows(x2_dram, nb)).then_inc(xr_in, 16)
                if nx is not None:
                    wait(sp, zT_d, KT * nb)
                    sp.dma_start(xn[:, :, :], block_rows(x2_dram, nx)).then_inc(xn_in, 16)
                if first:
                    load_pieces(3 * HEAD, len(PIECES))
                sp.wait_ge(y_r, TPB * (nb + 1))
                sp.dma_start(block_rows(out, nb), xr[:, :, :]).then_inc(stored, 16)

            schedule(program, sp.Fori)
            sp.wait_ge(stored, 16 * NBLK)

        @block.gpsimd
        def _(pool):
            def rough_rstd(q):
                pool.wait_ge(ve_r, q + 1)
                pool.tensor_tensor(r0[:, :], ve[:, :], mhalf[:, :], ALU.pow).then_inc(rs_r, 1)

            def program(nb, nx, first):
                if nx is not None:
                    rough_rstd(nb)
                pool.wait_ge(xr_in, 16 * (nb + 1))
                for s in range(TPB):
                    pool.wait_ge(ys_r, TPB * nb + s + 1)
                    pool.tensor_tensor(xr[:, s, :], xr[:, s, :], ys[s % 2][:, :], ALU.add).then_inc(y_r, 1)

            schedule(program, pool.Fori)

        @block.tensor
        def _(pe):
            def hidden(dst, kind, j, nb, low):
                piece = 3 * (j // 2) + "gud".index(kind)
                wh, wl = hi[piece], lo[piece]
                cols = slice((j % 2) * P, (j % 2 + 1) * P)
                passes = ((wh, zT_h), (wl, zT_h), (wh, zT_l)) if low else ((wh, zT_h), (wh, zT_l))
                n = 0
                for w, z in passes:
                    if z is zT_l and j == 0:
                        wait(pe, zT_lr, KT * nb)
                    for k in range(KT):
                        last = nc.tensor.matmul(dst[:, :], w[:, k, cols], z[:, k, :], start=(n == 0),
                                                stop=(n == len(passes) * KT - 1))
                        n += 1
                return last

            def down(j, nb, low):
                piece = 3 * (j // 2) + 2
                passes = ((h_h, hi), (h_h, lo), (h_l, hi)) if low else ((h_h, hi), (h_l, hi))
                pe.wait_ge(hh_r, HT * nb + j + 1)
                pe.wait_ge(hl_r, HT * nb + j + 1)
                if j == 0:
                    wait(pe, ys_r, TPB * nb)
                for s in range(TPB):
                    tok = slice(s * P, (s + 1) * P)
                    for n, (a, w) in enumerate(passes):
                        last = nc.tensor.matmul(DN[s][:, :], a[j % 2][:, tok], w[piece][:, j % 2, :], start=(j == 0 and n == 0),
                                                stop=(j == HT - 1 and n == len(passes) - 1))
                last.then_inc(dn_d, 1)

            def transpose_tile(k, nx):
                for s in range(TPB):
                    last = nc.tensor.transpose(TZ[k][:, s * P:(s + 1) * P], xn[:, s, k * P:(k + 1) * P], ident[:, :])
                last.then_inc(zT_d, 1)

            def program(nb, nx, first, low):
                w_split = w_lo if low else w_hi
                wait(pe, zT_hr, KT * nb)
                for j in range(HT):
                    if j >= 2:
                        pe.wait_ge(sil_r, HT * nb + j - 1)
                    elif not first:
                        pe.wait_ge(zT_lr, KT * nb - 1 - j)
                    if first:
                        wait(pe, w_split, 3 * (j // 2) + 1 - HEAD)
                    hidden(GT[j % 2], "g", j, nb, low).then_inc(g_d, 1)
                    if j >= 2:
                        pe.wait_ge(h_r, HT * nb + j - 1)
                    elif j == 0:
                        wait(pe, zT_lr, KT * nb)
                    if first:
                        wait(pe, w_split, 3 * (j // 2) + 2 - HEAD)
                    hidden(UP[j % 2], "u", j, nb, low).then_inc(u_d, 1)
                    if nx is not None and j == HT - 1:
                        pe.wait_ge(z_r, nx)
                        pe.wait_ge(sil_r, HT * nb + HT - 1)
                        pe.wait_ge(h_r, HT * nb + HT - 1)
                        transpose_tile(0, nx)
                        transpose_tile(1, nx)
                    if j >= 1:
                        if first:
                            wait(pe, w_split, 3 * ((j - 1) // 2) + 3 - HEAD)
                        down(j - 1, nb, low)
                if nx is not None:
                    pe.wait_ge(sil_r, HT * (nb + 1))
                    pe.wait_ge(h_r, HT * (nb + 1))
                    transpose_tile(2, nx)
                    transpose_tile(3, nx)
                if first:
                    pe.wait_ge(w_split, len(PIECES) - HEAD)
                down(HT - 1, nb, low)

            some_low = pe.value_load(ffn["low_flag"][0:1, 0:1], min_val=0, max_val=1)
            for low in (True, False):
                with pe.If(some_low == 1 if low else some_low == 0):
                    program(0, 1, True, low)
                    with pe.Fori(1, NBLK - 1) as nb:
                        program(nb, nb + 1, False, low)
                    program(NBLK - 1, None, False, low)

        @block.scalar
        def _(act):
            def split_hi(n):
                act.wait_ge(w_in[n], 16)
                nc.scalar.activation(hi[n], raw[n], ACT.Copy, bias=-ZERO_POINT).then_inc(w_hi, 1)

            def zT_high(k, nb):
                act.wait_ge(zT_d, KT * nb + k + 1)
                nc.scalar.activation(zT_h[:, k, :], TZ[k][:, :], ACT.Copy).then_inc(zT_hr, 1)

            def program(nb, nx, first):
                for j in range(HT):
                    act.wait_ge(g_d, HT * nb + j + 1)
                    if j >= 2:
                        act.wait_ge(h_r, HT * nb + j - 1)
                    nc.scalar.activation(sil[j % 2][:, :], GT[j % 2][:, :], ACT.Silu, scale=sg_c[:, j:j + 1]).then_inc(sil_r, 1)
                    act.wait_ge(h_r, HT * nb + j + 1)
                    if j >= 2:
                        act.wait_ge(dn_d, HT * nb + j - 1)
                    else:
                        wait(act, dn_d, HT * nb)
                    nc.scalar.activation(h_h[j % 2][:, :], h[j % 2][:, :], ACT.Copy).then_inc(hh_r, 1)
                    if first:
                        for n in pieces_at(j):
                            split_hi(n)
                if nx is not None:
                    for k in range(KT):
                        zT_high(k, nb)

            act.wait_ge(cin, 48)
            schedule(program, act.Fori)

        @block.vector
        def _(dve):
            def split_lo(n):
                dve.wait_ge(w_hi, n - HEAD + 1)
                nc.vector.scalar_tensor_tensor(out=lo[n], in0=raw[n], scalar=ZERO_POINT, in1=hi[n],
                                               op0=ALU.subtract, op1=ALU.subtract).then_inc(w_lo, 1)

            NSTEP = 4

            def statistics(q):
                dve.wait_ge(xn_in, 16 * (q + 1))
                for s in range(TPB):
                    last = nc.vector.bn_stats(st[:, s, :], xn[:, s, :])
                last.then_inc(dstep, 1)
                dve.wait_ge(dstep, NSTEP * q + 1)
                dve.sem_inc(aggr, 1)
                for s in range(TPB):
                    last = nc.vector.bn_aggr(mv[:, s, :], st[:, s, :])
                last.then_inc(mv_r, 1)
                dve.wait_ge(mv_r, q + 1)
                nc.vector.tensor_scalar(ve[:, :], mv[:, :, 1], EPS, None, ALU.add).then_inc(ve_r, 1)

            def normalise(q):
                dve.wait_ge(rs_r, q + 1)
                nc.vector.tensor_tensor(nt[:, 0, :], ve[:, :], r0[:, :], ALU.mult).then_inc(dstep, 1)
                dve.wait_ge(dstep, NSTEP * q + 2)
                nc.vector.tensor_tensor(nt[:, 1, :], nt[:, 0, :], r0[:, :], ALU.mult).then_inc(dstep, 1)
                dve.wait_ge(dstep, NSTEP * q + 3)
                nc.vector.tensor_scalar(nt[:, 2, :], nt[:, 1, :], -0.5, 1.5, ALU.mult, ALU.add).then_inc(dstep, 1)
                dve.wait_ge(dstep, NSTEP * q + 4)
                nc.vector.tensor_tensor(nt[:, 3, :], nt[:, 2, :], r0[:, :], ALU.mult).then_inc(rstd_r, 1)
                dve.wait_ge(rstd_r, q + 1)
                for s in range(TPB):
                    last = nc.vector.tensor_scalar(xn[:, s, :], xn[:, s, :], mv[:, s, 0:1], nt[:, 3, s:s + 1],
                                                   ALU.subtract, ALU.mult)
                last.then_inc(z_r, 1)

            def zT_low(k, q):
                dve.wait_ge(zT_hr, KT * q + k + 1)
                nc.vector.tensor_tensor(zT_l[:, k, :], TZ[k][:, :], zT_h[:, k, :], ALU.subtract).then_inc(zT_lr, 1)

            def program(nb, nx, first):
                for j in range(HT):
                    dve.wait_ge(u_d, HT * nb + j + 1)
                    dve.wait_ge(sil_r, HT * nb + j + 1)
                    if j >= 2:
                        dve.wait_ge(hh_r, HT * nb + j - 1)
                    nc.vector.scalar_tensor_tensor(out=h[j % 2][:, :], in0=UP[j % 2][:, :], scalar=su_c[:, j:j + 1],
                                                   in1=sil[j % 2][:, :], op0=ALU.mult, op1=ALU.mult).then_inc(h_r, 1)
                    dve.wait_ge(hh_r, HT * nb + j + 1)
                    nc.vector.tensor_tensor(h_l[j % 2][:, :], h[j % 2][:, :], h_h[j % 2][:, :], ALU.subtract).then_inc(hl_r, 1)
                    if first:
                        for n in pieces_at(j):
                            split_lo(n)
                    if j == 4 and nx is not None:
                        statistics(nb)
                    if j == 6 and nx is not None:
                        normalise(nb)
                if nx is not None:
                    for k in range(KT):
                        zT_low(k, nb)
                dve.wait_ge(dn_d, HT * (nb + 1))
                for s in range(TPB):
                    if s >= 2:
                        dve.wait_ge(y_r, TPB * nb + s - 1)
                    else:
                        wait(dve, y_r, TPB * nb)
                    nc.vector.tensor_tensor(ys[s % 2][:, :], DN[s][:, :], sd_b[:, :], ALU.mult).then_inc(ys_r, 1)

            dve.wait_ge(cin, 48)
            schedule(program, dve.Fori)


def kernel(**inputs):
    import concourse.bacc as bacc
    from concourse.bass_utils import run_bass_kernel_spmd

    a = {k: np.asarray(v) for k, v in inputs.items()}

    def c(v):
        return np.ascontiguousarray(v)

    arrays = {
        "x": c(a["x"]), "ctx": c(a["ctx_1024"]), "pos": c(a["fside_BxSx2_0"].transpose(1, 0, 2).reshape(P, 2 * B)),
        "consts": shape_constants(),
        "wq1": c(a["L0_attn_Wq"].T), "wk1": c(a["L0_attn_Wk"].T), "wv1": c(a["L0_attn_Wv"].T), "wo1": c(a["L0_attn_Wo"].T),
        "wq2": c(a["L0_xattn_Wq"]), "wkv2": c(a["L0_xattn_Wkv"]), "wo2": c(a["L0_xattn_Wout"]), "bout": c(a["L0_xattn_bout"]),
        "wg": c(a["L0_ffn_wq_gate"].T), "sg": c(a["L0_ffn_s_gate"].reshape(HT, P).T),
        "wu": c(a["L0_ffn_wq_up"].T), "su": c(a["L0_ffn_s_up"].reshape(HT, P).T),
        "wd": c(a["L0_ffn_wq_down"].T), "sd": c(a["L0_ffn_s_down"]),
    }
    nc = bacc.Bacc("TRN2", target_bir_lowering=False, num_devices=1)
    t = {n: nc.dram_tensor(f"in_{n}", v.shape, mybir.dt.from_np(v.dtype), kind="ExternalInput").ap() for n, v in arrays.items()}
    out = nc.dram_tensor("out", (B, P, D), mybir.dt.float32, kind="ExternalOutput").ap()
    x2_dram = nc.dram_tensor("x2_scratch", (B, P, D), mybir.dt.float32, kind="Internal").ap()
    build_decoder(nc, t["x"], t["ctx"], t["pos"], t["consts"], t["wq1"], t["wk1"], t["wv1"], t["wo1"],
                  t["wq2"], t["wkv2"], t["wo2"], t["bout"], t["wg"], t["sg"], t["wu"], t["su"], t["wd"], t["sd"],
                  out, x2_dram)
    r = run_bass_kernel_spmd(nc, [{f"in_{n}": v for n, v in arrays.items()}], core_ids=[0])
    return r.results[0]["out"]
```
